# Optimizing a Trainium2 kernel written in Bass

```python
import numpy as np
import jax
import jax.numpy as jnp

def _softmax(x, axis=-1):
    return jax.nn.softmax(x, axis=axis)

def _gelu(x):
    return jax.nn.gelu(x, approximate=True)

def _silu(x):
    return jax.nn.silu(x)

def _sigmoid(x):
    return jax.nn.sigmoid(x)

def _layernorm(x, axis=-1, eps=1e-05):
    m = jnp.mean(x, axis=axis, keepdims=True)
    v = jnp.var(x, axis=axis, keepdims=True)
    return (x - m) / jnp.sqrt(v + eps)

def _scatter_add(tgt, idx, src, axis=0):
    return tgt.at[idx].add(src)

def _segment_sum(src, seg, n):
    return jax.ops.segment_sum(src, seg, n)
kernel_name = 'mk_seq_postln_d4_jaxref_r8_2f12ef'

def setup_inputs(seed: int=0):
    np.random.seed(seed)
    _w = jnp.asarray

    def _L0_attn_setup():
        import jax, jax.numpy as jnp
        import numpy as np
        D_MODEL = 128
        NUM_HEADS = 16
        HEAD_DIM = D_MODEL // NUM_HEADS
        WINDOW = 128
        NEG_INF = -1e+30

        def _sliding_mask(seqlen: int) -> jnp.ndarray:
            rel = jnp.arange(seqlen)[:, None] - jnp.arange(seqlen)[None, :]
            allowed = (rel >= 0) & (rel < WINDOW)
            return jnp.where(allowed, 0.0, NEG_INF).astype(jnp.float32)
        key = jax.random.key(seed)
        kx, kq, kk, kv, ko = jax.random.split(key, 5)
        B, S = (2, 256)
        scale = 0.02
        x = jax.random.normal(kx, (B, S, D_MODEL), dtype=jnp.float32)
        Wq = jax.random.normal(kq, (D_MODEL, D_MODEL), dtype=jnp.float32) * scale
        Wk = jax.random.normal(kk, (D_MODEL, D_MODEL), dtype=jnp.float32) * scale
        Wv = jax.random.normal(kv, (D_MODEL, D_MODEL), dtype=jnp.float32) * scale
        Wo = jax.random.normal(ko, (D_MODEL, D_MODEL), dtype=jnp.float32) * scale
        return {'x': x, 'Wq': Wq, 'Wk': Wk, 'Wv': Wv, 'Wo': Wo}
    _L0_attn_in = _L0_attn_setup()

    def _L0_ffn_setup():
        import jax, jax.numpy as jnp
        import numpy as np
        HIDDEN = 128
        NUM_EXPERTS = 8
        CAPACITY_FACTOR = 1.25
        key = jax.random.key(seed)
        k_tok, k_g, k_w1, k_b1, k_w2, k_b2 = jax.random.split(key, 6)
        B, S, H, E = (4, 256, HIDDEN, NUM_EXPERTS)
        tokens = jax.random.normal(k_tok, (B, S, H), dtype=jnp.float32)
        gate_w = jax.random.normal(k_g, (E, H), dtype=jnp.float32) * 0.02
        W1 = jax.random.normal(k_w1, (E, H, H), dtype=jnp.float32) * 0.02
        b1 = jax.random.normal(k_b1, (E, H), dtype=jnp.float32) * 0.02
        W2 = jax.random.normal(k_w2, (E, H, H), dtype=jnp.float32) * 0.02
        b2 = jax.random.normal(k_b2, (E, H), dtype=jnp.float32) * 0.02
        return {'tokens': tokens, 'gate_w': gate_w, 'W1': W1, 'b1': b1, 'W2': W2, 'b2': b2}
    _L0_ffn_in = _L0_ffn_setup()

    def _L1_attn_setup():
        import jax, jax.numpy as jnp
        import numpy as np
        from jax import lax
        D_MODEL = 128
        BATCH = 4
        SEQ = 512
        DECAY = 0.9
        INPUT_SCALE = 0.1
        key = jax.random.key(seed)
        k1, k2, k3 = jax.random.split(key, 3)
        scale_in = 1.0 / np.sqrt(D_MODEL)
        return {'x': jax.random.normal(k1, (BATCH, SEQ, D_MODEL), dtype=jnp.float32), 'W_in': jax.random.normal(k2, (D_MODEL, 2 * D_MODEL), dtype=jnp.float32) * scale_in, 'b_in': jnp.zeros((2 * D_MODEL,), dtype=jnp.float32), 'W_out': jax.random.normal(k3, (D_MODEL, D_MODEL), dtype=jnp.float32) * scale_in, 'b_out': jnp.zeros((D_MODEL,), dtype=jnp.float32)}
    _L1_attn_in = _L1_attn_setup()

    def _L1_ffn_setup():
        import jax, jax.numpy as jnp
        import numpy as np
        D_IN, D_HID = (128, 512)

        def _ternary(key, shape):
            return jax.random.randint(key, shape, -1, 2).astype(jnp.float32)

        def _tlin(x, w, s):
            return jnp.einsum('bsi,oi->bso', x, w) * s
        key = jax.random.key(seed)
        ks = jax.random.split(key, 12)
        inv = lambda fan: 1.0 / np.sqrt(fan).astype(np.float32)
        return {'x': jax.random.normal(ks[0], (4, 256, D_IN), dtype=jnp.float32), 'w1_w': _ternary(ks[1], (D_HID, D_IN)), 'w1_s': jax.random.uniform(ks[2], (D_HID,), dtype=jnp.float32) * inv(D_IN), 'w2_w': _ternary(ks[3], (D_HID, D_IN)), 'w2_s': jax.random.uniform(ks[4], (D_HID,), dtype=jnp.float32) * inv(D_IN), 'h1_w': _ternary(ks[5], (D_HID, D_HID)), 'h1_s': jax.random.uniform(ks[6], (D_HID,), dtype=jnp.float32) * inv(D_HID), 'h2_w': _ternary(ks[7], (D_HID, D_HID)), 'h2_s': jax.random.uniform(ks[8], (D_HID,), dtype=jnp.float32) * inv(D_HID), 'w3_w': _ternary(ks[9], (D_IN, D_HID)), 'w3_s': jax.random.uniform(ks[10], (D_IN,), dtype=jnp.float32) * inv(D_HID)}
    _L1_ffn_in = _L1_ffn_setup()

    def _L2_attn_setup():
        import jax, jax.numpy as jnp
        import numpy as np
        CHUNK = 64
        HEADS = 16

        def _chunk_mask(T, cs):
            idx = jnp.arange(T)
            blk = idx // cs * cs
            qb = blk[:, None]
            kb = blk[None, :]
            masked = (qb >= kb) & (idx[None, :] - idx[:, None] - 2 * (kb - qb) >= 1)
            return masked
        key = jax.random.key(seed)
        ks = jax.random.split(key, 6)
        B, T, C = (2, 256, 128)
        w = 0.02
        return {'x': jax.random.normal(ks[0], (B, T, C), jnp.float32), 'Wq': jax.random.normal(ks[1], (C, C), jnp.float32) * w, 'bq': jnp.zeros((C,), jnp.float32), 'Wk': jax.random.normal(ks[2], (C, C), jnp.float32) * w, 'bk': jnp.zeros((C,), jnp.float32), 'Wv': jax.random.normal(ks[3], (C, C), jnp.float32) * w, 'bv': jnp.zeros((C,), jnp.float32), 'Wo': jax.random.normal(ks[4], (C, C), jnp.float32) * w, 'bo': jnp.zeros((C,), jnp.float32), 'attn_scale': jnp.full((1,), 1.0 / np.sqrt(C // HEADS), jnp.float32)}
    _L2_attn_in = _L2_attn_setup()

    def _L2_ffn_setup():
        import jax, jax.numpy as jnp
        import numpy as np
        N_EMBD = 128
        NUM_EXPERTS = 8
        TOP_K = 2
        D_FF = 4 * N_EMBD
        B, S = (4, 256)
        key = jax.random.key(seed)
        ks = jax.random.split(key, 7)
        scale = lambda fan_in: 1.0 / np.sqrt(fan_in)
        x = jax.random.normal(ks[0], (B, S, N_EMBD), dtype=jnp.float32)
        W_router = jax.random.normal(ks[1], (N_EMBD, NUM_EXPERTS), dtype=jnp.float32) * scale(N_EMBD)
        b_router = jnp.zeros((NUM_EXPERTS,), dtype=jnp.float32)
        W1 = jax.random.normal(ks[2], (NUM_EXPERTS, N_EMBD, D_FF), dtype=jnp.float32) * scale(N_EMBD)
        b1 = jnp.zeros((NUM_EXPERTS, D_FF), dtype=jnp.float32)
        W2 = jax.random.normal(ks[3], (NUM_EXPERTS, D_FF, N_EMBD), dtype=jnp.float32) * scale(D_FF)
        b2 = jnpp = jnp.zeros((NUM_EXPERTS, N_EMBD), dtype=jnp.float32)
        return {'x': x, 'W_router': W_router, 'b_router': b_router, 'W1': W1, 'b1': b1, 'W2': W2, 'b2': b2}
    _L2_ffn_in = _L2_ffn_setup()

    def _L3_attn_setup():
        import jax, jax.numpy as jnp
        import numpy as np
        EMBED_DIM = 128
        NUM_HEADS = 16
        HEAD_DIM = EMBED_DIM // NUM_HEADS
        NUM_FEATS = 32
        YAT_EPS = 0.1
        BATCH = 4
        SEQ = 512

        def _spherical_features(x, projection):
            x_norm = x / (jnp.linalg.norm(x, axis=-1, keepdims=True) + 1e-08)
            proj = jnp.einsum('bhsd,hfd->bhsf', x_norm, projection)
            return jax.nn.relu(proj) + YAT_EPS
        key = jax.random.key(seed)
        ks = jax.random.split(key, 6)
        s = 1.0 / np.sqrt(EMBED_DIM)
        return {'x': jax.random.normal(ks[0], (BATCH, SEQ, EMBED_DIM), jnp.float32), 'Wq': jax.random.normal(ks[1], (EMBED_DIM, EMBED_DIM), jnp.float32) * s, 'bq': jnp.zeros((EMBED_DIM,), jnp.float32), 'Wk': jax.random.normal(ks[2], (EMBED_DIM, EMBED_DIM), jnp.float32) * s, 'bk': jnp.zeros((EMBED_DIM,), jnp.float32), 'Wv': jax.random.normal(ks[3], (EMBED_DIM, EMBED_DIM), jnp.float32) * s, 'bv': jnp.zeros((EMBED_DIM,), jnp.float32), 'Wo': jax.random.normal(ks[4], (EMBED_DIM, EMBED_DIM), jnp.float32) * s, 'bo': jnp.zeros((EMBED_DIM,), jnp.float32), 'projection': jax.random.normal(ks[5], (NUM_HEADS, NUM_FEATS, HEAD_DIM), jnp.float32)}
    _L3_attn_in = _L3_attn_setup()

    def _L3_ffn_setup():
        import jax, jax.numpy as jnp
        import numpy as np
        B, S, DIM = (4, 256, 128)
        E, K, HID = (8, 2, 512)
        key = jax.random.key(seed)
        ks = jax.random.split(key, 8)
        init = lambda k, sh: jax.random.normal(k, sh, jnp.float32) * 0.02
        return {'x': jax.random.normal(ks[0], (B, S, DIM), jnp.float32), 'gate_w': init(ks[1], (DIM, E)), 'gate_b': jnp.zeros((E,), jnp.float32), 'w1': init(ks[2], (E, DIM, HID)), 'b1': jnp.zeros((E, HID), jnp.float32), 'w2': init(ks[3], (E, HID, DIM)), 'b2': jnp.zeros((E, DIM), jnp.float32), 'ws1': init(ks[4], (DIM, HID)), 'bs1': jnp.zeros((HID,), jnp.float32), 'ws2': init(ks[5], (HID, DIM)), 'bs2': jnp.zeros((DIM,), jnp.float32)}
    _L3_ffn_in = _L3_ffn_setup()
    _d = {'L0_attn_x': _L0_attn_in['x'], 'L0_attn_Wq': _L0_attn_in['Wq'], 'L0_attn_Wk': _L0_attn_in['Wk'], 'L0_attn_Wv': _L0_attn_in['Wv'], 'L0_attn_Wo': _L0_attn_in['Wo'], 'L0_ffn_gate_w': _L0_ffn_in['gate_w'], 'L0_ffn_W1': _L0_ffn_in['W1'], 'L0_ffn_b1': _L0_ffn_in['b1'], 'L0_ffn_W2': _L0_ffn_in['W2'], 'L0_ffn_b2': _L0_ffn_in['b2'], 'L1_attn_W_in': _L1_attn_in['W_in'], 'L1_attn_b_in': _L1_attn_in['b_in'], 'L1_attn_W_out': _L1_attn_in['W_out'], 'L1_attn_b_out': _L1_attn_in['b_out'], 'L1_ffn_w1_w': _L1_ffn_in['w1_w'], 'L1_ffn_w1_s': _L1_ffn_in['w1_s'], 'L1_ffn_w2_w': _L1_ffn_in['w2_w'], 'L1_ffn_w2_s': _L1_ffn_in['w2_s'], 'L1_ffn_h1_w': _L1_ffn_in['h1_w'], 'L1_ffn_h1_s': _L1_ffn_in['h1_s'], 'L1_ffn_h2_w': _L1_ffn_in['h2_w'], 'L1_ffn_h2_s': _L1_ffn_in['h2_s'], 'L1_ffn_w3_w': _L1_ffn_in['w3_w'], 'L1_ffn_w3_s': _L1_ffn_in['w3_s'], 'L2_attn_Wq': _L2_attn_in['Wq'], 'L2_attn_bq': _L2_attn_in['bq'], 'L2_attn_Wk': _L2_attn_in['Wk'], 'L2_attn_bk': _L2_attn_in['bk'], 'L2_attn_Wv': _L2_attn_in['Wv'], 'L2_attn_bv': _L2_attn_in['bv'], 'L2_attn_Wo': _L2_attn_in['Wo'], 'L2_attn_bo': _L2_attn_in['bo'], 'L2_attn_attn_scale': _L2_attn_in['attn_scale'], 'L2_ffn_W_router': _L2_ffn_in['W_router'], 'L2_ffn_b_router': _L2_ffn_in['b_router'], 'L2_ffn_W1': _L2_ffn_in['W1'], 'L2_ffn_b1': _L2_ffn_in['b1'], 'L2_ffn_W2': _L2_ffn_in['W2'], 'L2_ffn_b2': _L2_ffn_in['b2'], 'L3_attn_Wq': _L3_attn_in['Wq'], 'L3_attn_bq': _L3_attn_in['bq'], 'L3_attn_Wk': _L3_attn_in['Wk'], 'L3_attn_bk': _L3_attn_in['bk'], 'L3_attn_Wv': _L3_attn_in['Wv'], 'L3_attn_bv': _L3_attn_in['bv'], 'L3_attn_Wo': _L3_attn_in['Wo'], 'L3_attn_bo': _L3_attn_in['bo'], 'L3_attn_projection': _L3_attn_in['projection'], 'L3_ffn_gate_w': _L3_ffn_in['gate_w'], 'L3_ffn_gate_b': _L3_ffn_in['gate_b'], 'L3_ffn_w1': _L3_ffn_in['w1'], 'L3_ffn_b1': _L3_ffn_in['b1'], 'L3_ffn_w2': _L3_ffn_in['w2'], 'L3_ffn_b2': _L3_ffn_in['b2'], 'L3_ffn_ws1': _L3_ffn_in['ws1'], 'L3_ffn_bs1': _L3_ffn_in['bs1'], 'L3_ffn_ws2': _L3_ffn_in['ws2'], 'L3_ffn_bs2': _L3_ffn_in['bs2']}
    _x0 = _d['L0_attn_x']
    _d['L0_attn_x'] = jax.random.normal(jax.random.fold_in(jax.random.key(seed), 1), (8, 512, 128), dtype=_x0.dtype)
    del _x0
    return _d

def reference(L0_attn_x, L0_attn_Wq, L0_attn_Wk, L0_attn_Wv, L0_attn_Wo, L0_ffn_gate_w, L0_ffn_W1, L0_ffn_b1, L0_ffn_W2, L0_ffn_b2, L1_attn_W_in, L1_attn_b_in, L1_attn_W_out, L1_attn_b_out, L1_ffn_w1_w, L1_ffn_w1_s, L1_ffn_w2_w, L1_ffn_w2_s, L1_ffn_h1_w, L1_ffn_h1_s, L1_ffn_h2_w, L1_ffn_h2_s, L1_ffn_w3_w, L1_ffn_w3_s, L2_attn_Wq, L2_attn_bq, L2_attn_Wk, L2_attn_bk, L2_attn_Wv, L2_attn_bv, L2_attn_Wo, L2_attn_bo, L2_attn_attn_scale, L2_ffn_W_router, L2_ffn_b_router, L2_ffn_W1, L2_ffn_b1, L2_ffn_W2, L2_ffn_b2, L3_attn_Wq, L3_attn_bq, L3_attn_Wk, L3_attn_bk, L3_attn_Wv, L3_attn_bv, L3_attn_Wo, L3_attn_bo, L3_attn_projection, L3_ffn_gate_w, L3_ffn_gate_b, L3_ffn_w1, L3_ffn_b1, L3_ffn_w2, L3_ffn_b2, L3_ffn_ws1, L3_ffn_bs1, L3_ffn_ws2, L3_ffn_bs2):

    def _L0_attn_ref(x, Wq, Wk, Wv, Wo):
        import jax, jax.numpy as jnp
        import numpy as np
        D_MODEL = 128
        NUM_HEADS = 16
        HEAD_DIM = D_MODEL // NUM_HEADS
        WINDOW = 128
        NEG_INF = -1e+30

        def _sliding_mask(seqlen: int) -> jnp.ndarray:
            rel = jnp.arange(seqlen)[:, None] - jnp.arange(seqlen)[None, :]
            allowed = (rel >= 0) & (rel < WINDOW)
            return jnp.where(allowed, 0.0, NEG_INF).astype(jnp.float32)
        B, S, _ = x.shape

        def proj(W):
            y = jnp.einsum('bsd,ed->bse', x, W)
            return y.reshape(B, S, NUM_HEADS, HEAD_DIM).transpose(0, 2, 1, 3)
        q, k, v = (proj(Wq), proj(Wk), proj(Wv))
        scale = 1.0 / jnp.sqrt(jnp.float32(HEAD_DIM))
        scores = jnp.einsum('bhqd,bhkd->bhqk', q, k) * scale + _sliding_mask(S)
        attn = jax.nn.softmax(scores, axis=-1)
        y = jnp.einsum('bhqk,bhkd->bhqd', attn, v)
        y = y.transpose(0, 2, 1, 3).reshape(B, S, D_MODEL)
        return jnp.einsum('bsd,ed->bse', y, Wo)

    def _L0_ffn_ref(tokens, gate_w, W1, b1, W2, b2):
        import jax, jax.numpy as jnp
        import numpy as np
        HIDDEN = 128
        NUM_EXPERTS = 8
        CAPACITY_FACTOR = 1.25
        B, S, H = tokens.shape
        E = gate_w.shape[0]
        T = B * S
        x = tokens.reshape(T, H)
        logits = x @ gate_w.T
        probs = jax.nn.softmax(logits, axis=-1)
        top2_w, top2_idx = jax.lax.top_k(probs, 2)
        cap = int(CAPACITY_FACTOR * T / E)
        counts = jnp.bincount(top2_idx.reshape(-1), length=E)
        keep = (counts <= cap).astype(x.dtype)
        comb = jnp.zeros((T, E), dtype=x.dtype).at[jnp.arange(T)[:, None], top2_idx].add(top2_w)
        comb = comb * keep[None, :]
        h = jax.nn.relu(jnp.einsum('th,ehf->tef', x, W1) + b1[None, :, :])
        y = jnp.einsum('teh,ehf->tef', h, W2) + b2[None, :, :]
        out = jnp.einsum('te,tef->tf', comb, y)
        return out.reshape(B, S, H)

    def _L1_attn_ref(x, W_in, b_in, W_out, b_out):
        import jax, jax.numpy as jnp
        import numpy as np
        from jax import lax
        D_MODEL = 128
        BATCH = 4
        SEQ = 512
        DECAY = 0.9
        INPUT_SCALE = 0.1
        x_proj = jnp.einsum('bsd,de->bse', x, W_in) + b_in
        x_gate, x_hidden = jnp.split(x_proj, 2, axis=-1)
        x_gated = jax.nn.sigmoid(x_gate) * jax.nn.silu(x_hidden)

        def step(h, g_t):
            h = DECAY * h + INPUT_SCALE * g_t
            return (h, h)
        g_tm = jnp.swapaxes(x_gated, 0, 1)
        h0 = jnp.zeros((x.shape[0], x.shape[2]), dtype=x.dtype)
        _, hs = lax.scan(step, h0, g_tm)
        hidden_seq = jnp.swapaxes(hs, 0, 1)
        out = jnp.einsum('bsd,de->bse', hidden_seq, W_out) + b_out
        return out

    def _L1_ffn_ref(x, w1_w, w1_s, w2_w, w2_s, h1_w, h1_s, h2_w, h2_s, w3_w, w3_s):
        import jax, jax.numpy as jnp
        import numpy as np
        D_IN, D_HID = (128, 512)

        def _ternary(key, shape):
            return jax.random.randint(key, shape, -1, 2).astype(jnp.float32)

        def _tlin(x, w, s):
            return jnp.einsum('bsi,oi->bso', x, w) * s
        h = jax.nn.silu(_tlin(x, w1_w, w1_s)) * _tlin(x, w2_w, w2_s)
        h = jax.nn.gelu(_tlin(h, h1_w, h1_s), approximate=False)
        h = jax.nn.gelu(_tlin(h, h2_w, h2_s), approximate=False)
        return _tlin(h, w3_w, w3_s)

    def _L2_attn_ref(x, Wq, bq, Wk, bk, Wv, bv, Wo, bo, attn_scale):
        import jax, jax.numpy as jnp
        import numpy as np
        CHUNK = 64
        HEADS = 16

        def _chunk_mask(T, cs):
            idx = jnp.arange(T)
            blk = idx // cs * cs
            qb = blk[:, None]
            kb = blk[None, :]
            masked = (qb >= kb) & (idx[None, :] - idx[:, None] - 2 * (kb - qb) >= 1)
            return masked
        B, T, C = x.shape
        H = HEADS
        D = C // H
        q = (x @ Wq.T + bq).reshape(B, T, H, D)
        k = (x @ Wk.T + bk).reshape(B, T, H, D)
        v = (x @ Wv.T + bv).reshape(B, T, H, D)
        scores = jnp.einsum('bqhd,bkhd->bhqk', q, k) * attn_scale[0]
        mask = _chunk_mask(T, CHUNK)
        scores = jnp.where(mask[None, None], -jnp.inf, scores)
        attn = jax.nn.softmax(scores, axis=-1)
        out = jnp.einsum('bhqk,bkhd->bqhd', attn, v).reshape(B, T, C)
        return out @ Wo.T + bo

    def _L2_ffn_ref(x, W_router, b_router, W1, b1, W2, b2):
        import jax, jax.numpy as jnp
        import numpy as np
        N_EMBD = 128
        NUM_EXPERTS = 8
        TOP_K = 2
        D_FF = 4 * N_EMBD
        B, S = (4, 256)
        Bv, Sv, D = x.shape
        flat_x = x.reshape(-1, D)
        T = flat_x.shape[0]
        logits = flat_x @ W_router + b_router
        top_vals, top_idx = jax.lax.top_k(logits, TOP_K)
        neg_inf = jnp.full_like(logits, -jnp.inf)
        sparse_logits = neg_inf.at[jnp.arange(T)[:, None], top_idx].set(top_vals)
        router_weights = jax.nn.softmax(sparse_logits, axis=-1)
        final_output = jnp.zeros_like(flat_x)
        for e in range(NUM_EXPERTS):
            expert_mask = jnp.any(top_idx == e, axis=-1)
            h = jax.nn.relu(flat_x @ W1[e] + b1[e])
            y = h @ W2[e] + b2[e]
            w = router_weights[:, e] * expert_mask.astype(x.dtype)
            final_output = final_output + y * w[:, None]
        return final_output.reshape(Bv, Sv, D)

    def _L3_attn_ref(x, Wq, bq, Wk, bk, Wv, bv, Wo, bo, projection):
        import jax, jax.numpy as jnp
        import numpy as np
        EMBED_DIM = 128
        NUM_HEADS = 16
        HEAD_DIM = EMBED_DIM // NUM_HEADS
        NUM_FEATS = 32
        YAT_EPS = 0.1
        BATCH = 4
        SEQ = 512

        def _spherical_features(x, projection):
            x_norm = x / (jnp.linalg.norm(x, axis=-1, keepdims=True) + 1e-08)
            proj = jnp.einsum('bhsd,hfd->bhsf', x_norm, projection)
            return jax.nn.relu(proj) + YAT_EPS
        b, s, _ = x.shape

        def heads(t):
            return jnp.transpose(t.reshape(b, s, NUM_HEADS, HEAD_DIM), (0, 2, 1, 3))
        Q = heads(x @ Wq + bq)
        K = heads(x @ Wk + bk)
        V = heads(x @ Wv + bv)
        Qp = _spherical_features(Q, projection)
        Kp = _spherical_features(K, projection)
        KV = jnp.einsum('bhsf,bhsd->bhfd', Kp, V)
        QKV = jnp.einsum('bhsf,bhfd->bhsd', Qp, KV)
        K_sum = jnp.sum(Kp, axis=2)
        normalizer = jnp.einsum('bhsf,bhf->bhs', Qp, K_sum)[..., None]
        normalizer = jnp.maximum(normalizer, 1e-06)
        out = QKV / normalizer
        out = jnp.transpose(out, (0, 2, 1, 3)).reshape(b, s, EMBED_DIM)
        return out @ Wo + bo

    def _L3_ffn_ref(x, gate_w, gate_b, w1, b1, w2, b2, ws1, bs1, ws2, bs2):
        import jax, jax.numpy as jnp
        import numpy as np
        B, S, DIM = (4, 256, 128)
        E, K, HID = (8, 2, 512)
        orig_shape = x.shape
        xf = x.reshape(-1, DIM)
        logits = xf @ gate_w + gate_b
        top_w, top_i = jax.lax.top_k(logits, K)
        gw = jax.nn.softmax(top_w, axis=-1).astype(xf.dtype)
        combine = (gw[:, :, None] * jax.nn.one_hot(top_i, E, dtype=xf.dtype)).sum(axis=1)
        out = jnp.zeros_like(xf)
        for e in range(E):
            h = jax.nn.gelu(xf @ w1[e] + b1[e], approximate=False)
            out = out + combine[:, e:e + 1] * (h @ w2[e] + b2[e])
        shared = jax.nn.gelu(xf @ ws1 + bs1, approximate=False) @ ws2 + bs2
        return (out + shared).reshape(orig_shape)
    x = L0_attn_x
    x = _layernorm(x + _L0_attn_ref(x, L0_attn_Wq, L0_attn_Wk, L0_attn_Wv, L0_attn_Wo), axis=-1)
    x = _layernorm(x + _L0_ffn_ref(x, L0_ffn_gate_w, L0_ffn_W1, L0_ffn_b1, L0_ffn_W2, L0_ffn_b2), axis=-1)
    x = _layernorm(x + _L1_attn_ref(x, L1_attn_W_in, L1_attn_b_in, L1_attn_W_out, L1_attn_b_out), axis=-1)
    x = _layernorm(x + _L1_ffn_ref(x, L1_ffn_w1_w, L1_ffn_w1_s, L1_ffn_w2_w, L1_ffn_w2_s, L1_ffn_h1_w, L1_ffn_h1_s, L1_ffn_h2_w, L1_ffn_h2_s, L1_ffn_w3_w, L1_ffn_w3_s), axis=-1)
    x = _layernorm(x + _L2_attn_ref(x, L2_attn_Wq, L2_attn_bq, L2_attn_Wk, L2_attn_bk, L2_attn_Wv, L2_attn_bv, L2_attn_Wo, L2_attn_bo, L2_attn_attn_scale), axis=-1)
    x = _layernorm(x + _L2_ffn_ref(x, L2_ffn_W_router, L2_ffn_b_router, L2_ffn_W1, L2_ffn_b1, L2_ffn_W2, L2_ffn_b2), axis=-1)
    x = _layernorm(x + _L3_attn_ref(x, L3_attn_Wq, L3_attn_bq, L3_attn_Wk, L3_attn_bk, L3_attn_Wv, L3_attn_bv, L3_attn_Wo, L3_attn_bo, L3_attn_projection), axis=-1)
    x = _layernorm(x + _L3_ffn_ref(x, L3_ffn_gate_w, L3_ffn_gate_b, L3_ffn_w1, L3_ffn_b1, L3_ffn_w2, L3_ffn_b2, L3_ffn_ws1, L3_ffn_bs1, L3_ffn_ws2, L3_ffn_bs2), axis=-1)
    return x

_drawn_inputs = setup_inputs


def setup_inputs(seed=0):
    import zlib

    import numpy as np

    out = dict(_drawn_inputs(seed))
    spreads = {'L1_attn_b_in': (0.0, 0.1),
     'L1_attn_b_out': (0.0, 0.1),
     'L2_attn_bq': (0.0, 2.0),
     'L2_attn_bk': (0.0, 2.0),
     'L2_attn_bv': (0.0, 0.1),
     'L2_attn_bo': (0.0, 0.1),
     'L2_ffn_b_router': (0.0, 0.1),
     'L2_ffn_b1': (0.0, 0.1),
     'L2_ffn_b2': (0.0, 0.1),
     'L3_attn_bq': (0.0, 2.0),
     'L3_attn_bk': (0.0, 2.0),
     'L3_attn_bv': (0.0, 0.1),
     'L3_attn_bo': (0.0, 0.1),
     'L3_ffn_gate_b': (0.0, 0.1),
     'L3_ffn_b1': (0.0, 0.459),
     'L3_ffn_b2': (0.0, 0.1),
     'L3_ffn_bs1': (0.0, 0.344),
     'L3_ffn_bs2': (0.0, 0.1)}
    factors = {'L0_attn_Wq': 7.744,
     'L0_attn_Wk': 8.0,
     'L0_attn_Wv': 2.728,
     'L1_ffn_w1_w': 3.616,
     'L1_ffn_w1_s': 6.232,
     'L1_ffn_w2_w': 3.223,
     'L1_ffn_w2_s': 4.954,
     'L1_ffn_h1_w': 3.18,
     'L1_ffn_h1_s': 5.064,
     'L1_ffn_h2_w': 3.009,
     'L1_ffn_h2_s': 4.575,
     'L1_ffn_w3_w': 3.993,
     'L1_ffn_w3_s': 4.673,
     'L2_attn_Wq': 8.0,
     'L2_attn_Wk': 8.0,
     'L3_attn_Wq': 5.23,
     'L3_attn_projection': 3.103}
    for name, (base, spread) in spreads.items():
        noise = np.random.default_rng([zlib.crc32(name.encode()), seed]).standard_normal(out[name].shape)
        drawn = base * np.exp(spread * noise) if base else spread * noise
        out[name] = jnp.asarray(drawn.astype(out[name].dtype))
    for name, factor in factors.items():
        out[name] = (out[name] * factor).astype(out[name].dtype)
    return out
```

```python
from contextlib import ExitStack

import concourse.bass as bass
from concourse import mybir
from concourse.alu_op_type import AluOpType as ALU

F32 = mybir.dt.float32
F32R = mybir.dt.float32r
BF16 = mybir.dt.bfloat16
U32 = mybir.dt.uint32
ACT = mybir.ActivationFunctionType
AX = mybir.AxisListType

P = 128
D = 128
BATCH = 8
SEQ = 512
NC = BATCH
CH = SEQ
NB = CH // P
HEADS = 16
DH = D // HEADS
GROUPS = 4
GH = HEADS // GROUPS
QUAD = 32
E = 8
HID = 512
NEG = -1.0e30
EPS = 1e-5
R_MAX = 3 * DH
K_RAW = 3 * DH
K_MAX = 3 * DH + 2


def wait(eng, sem, count):
    if isinstance(count, int) and count <= 0:
        return
    eng.wait_ge(sem, count)


def settle(eng, net):
    eng.sem_inc(net.settled, 1)


def at(c):
    return bass.ds(c * CH, CH)


def tile3(ap, n=NB):
    return ap.rearrange("p (j d) -> p j d", j=n)


class Layer(ExitStack):

    def __init__(self, nc):
        super().__init__()
        self.nc, self.sems = nc, []

    def sem(self, name):
        self.sems.append(self.nc.alloc_semaphore(name=name))
        return self.sems[-1]

    def __exit__(self, *failure):
        super().__exit__(*failure)
        self.nc.clear_and_free_semaphores(self.sems)
        self.nc.all_engine_barrier()


class Net:

    def __init__(self, nc, ctx, dram):
        self.nc, self.dram = nc, dram

        def sb(name, shape, dt=F32):
            return ctx.enter_context(nc.sbuf_tensor(name, shape, dt))

        self.settled = ctx.sem("settled")
        self.x_tok = sb("x_tok", [P, NC, CH])
        self.x_hi = sb("x_hi", [P, NC * CH], F32R)
        self.x_lo = sb("x_lo", [P, NC * CH], F32R)
        self.y_stage = sb("y_stage", [P, CH])
        self.res = sb("res", [P, CH])
        self.x_new = sb("x_new", [P, CH])
        self.stats = sb("stats", [P, NB, 6])
        self.mv = sb("mv", [P, NB, 2])
        self.ve = sb("ve", [P, NB])
        self.rstd = sb("rstd", [P, NB])
        self.m_half = sb("m_half", [P, NB])
        self.spare = sb("spare", [P, NB])
        self.ident = sb("ident", [P, P])
        self.ident16 = sb("ident16", [P, P], BF16)
        self.const = sb("const", [P, 4])


class Norm:

    STEPS = 3

    def __init__(self, nc, ctx, net, name, last=False, shared=None):
        self.nc, self.net, self.last, self.shared = nc, net, last, shared

        def sem(n):
            return ctx.sem(f"{name}_{n}")

        self.y_staged = sem("y_staged")
        self.y_turned = sem("y_turned")
        self.y_added = sem("y_added")
        self.stepped = sem("stepped")
        self.rstd_ready = sem("rstd_ready")
        self.xn_ready = sem("xn_ready")
        self.xn_turned = sem("xn_turned")
        self.hi_ready = sem("hi_ready")
        self.lo_ready = sem("lo_ready")
        self.x_saved = sem("x_saved")

    def turn(self, pe, src, bank):
        for j in range(NB):
            mm = pe.transpose(bank[:, j * P:(j + 1) * P], src[:, j * P:(j + 1) * P], self.net.ident[:])
        return mm

    def pe_turn_y(self, pe, c, bank, n=None):
        if n is None:
            pe.wait_ge(self.y_staged, c + 1)
            wait(pe, self.y_added, c)
            self.turn(pe, self.net.y_stage, bank).then_inc(self.y_turned, 1)
        else:
            full, free = self.shared
            pe.wait_ge(free, n)
            self.turn(pe, self.net.y_stage, bank).then_inc(full, 1)

    def dve_norm(self, dve, c, bank, n=None):
        net = self.net
        wait(dve, self.xn_ready, c)
        if n is None:
            dve.wait_ge(self.y_turned, c + 1)
            dve.tensor_tensor(net.res[:], bank[:], net.x_tok[:, c, :], ALU.add).then_inc(self.y_added, 1)
            dve.wait_ge(self.y_added, c + 1)
        else:
            full, free = self.shared
            dve.wait_ge(full, n + 1)
            dve.tensor_tensor(net.res[:], bank[:], net.x_tok[:, c, :], ALU.add).then_inc(free, 1)
            dve.wait_ge(free, n + 1)
        for j in range(NB):
            last = dve.bn_stats(net.stats[:, j, :], net.res[:, j * P:(j + 1) * P])
        last.then_inc(self.stepped, 1)
        dve.wait_ge(self.stepped, self.STEPS * c + 1)
        settle(dve, net)
        for j in range(NB):
            last = dve.bn_aggr(net.mv[:, j, :], net.stats[:, j, :])
        last.then_inc(self.stepped, 1)
        dve.wait_ge(self.stepped, self.STEPS * c + 2)
        wait(dve, self.rstd_ready, c)
        dve.tensor_scalar(net.ve[:], net.mv[:, :, 1], EPS, None, ALU.add).then_inc(self.stepped, 1)

    def pool_root(self, pool, c):
        net = self.net
        pool.wait_ge(self.stepped, self.STEPS * (c + 1))
        wait(pool, self.xn_ready, c)
        pool.tensor_tensor(net.rstd[:], net.ve[:], net.m_half[:, 0:NB], ALU.pow).then_inc(self.rstd_ready, 1)

    def dve_scale(self, dve, c):
        net = self.net
        dve.wait_ge(self.rstd_ready, c + 1)
        wait(dve, self.x_saved, 16 * c)
        if not self.last and self.shared is None:
            wait(dve, self.xn_turned, c)
        for j in range(NB):
            sl = slice(j * P, (j + 1) * P)
            last = dve.tensor_scalar(net.x_new[:, sl], net.res[:, sl], net.mv[:, j, 0:1], net.rstd[:, j:j + 1],
                                     ALU.subtract, ALU.mult)
        last.then_inc(self.xn_ready, 1)

    def pe_turn_x(self, pe, c, bank, n=None):
        pe.wait_ge(self.xn_ready, c + 1)
        if n is None:
            wait(pe, self.lo_ready, c)
            self.turn(pe, self.net.x_new, bank).then_inc(self.xn_turned, 1)
        else:
            full, free = self.shared
            pe.wait_ge(free, n)
            self.turn(pe, self.net.x_new, bank).then_inc(full, 1)

    def act_hi(self, act, c, bank, n=None):
        if n is None:
            act.wait_ge(self.xn_turned, c + 1)
        else:
            act.wait_ge(self.shared[0], n + 1)
        act.activation(self.net.x_hi[:, at(c)], bank[:], ACT.Copy).then_inc(self.hi_ready, 1)

    def dve_lo(self, dve, c, bank, n=None):
        net = self.net
        dve.wait_ge(self.hi_ready, c + 1)
        dve.tensor_tensor(net.x_lo[:, at(c)], bank[:], net.x_hi[:, at(c)].bitcast(F32),
                          ALU.subtract).then_inc(self.lo_ready if n is None else self.shared[1], 1)

    def sp_save(self, sp, c):
        net = self.net
        sp.wait_ge(self.xn_ready, c + 1)
        if self.last:
            dst = net.dram["out"][bass.ds(c, 1)].rearrange("a (j p) d -> p (a j) d", p=P)
            sp.dma_start(dst, tile3(net.x_new[:])).then_inc(self.x_saved, 16)
        else:
            sp.dma_start(net.x_tok[:, bass.ds(c, 1), :], net.x_new[:].rearrange("p (a n) -> p a n", a=1)
                         ).then_inc(self.x_saved, 16)

    def sp_end(self, sp):
        sp.wait_ge(self.x_saved, 16 * NC)


class Weights:

    def __init__(self, nc, ctx, name, dram, width):
        self.dram, self.width = dram, width
        self.raw = ctx.enter_context(nc.sbuf_tensor(f"{name}_w_raw", [P, dram.shape[1]], F32))
        self.hi = ctx.enter_context(nc.sbuf_tensor(f"{name}_w_hi", [P, width], F32R))
        self.lo = ctx.enter_context(nc.sbuf_tensor(f"{name}_w_lo", [P, width], F32R))
        self.loaded = ctx.sem(f"{name}_w_loaded")
        self.hi_ready = ctx.sem(f"{name}_w_hi_ready")
        self.lo_ready = ctx.sem(f"{name}_w_lo_ready")

    def sp_load(self, sp):
        sp.dma_start(self.raw[:], self.dram).then_inc(self.loaded, 16)

    def act_split(self, act):
        act.wait_ge(self.loaded, 16)
        act.activation(self.hi[:], self.raw[:, 0:self.width], ACT.Copy).then_inc(self.hi_ready, 1)

    def dve_split(self, dve):
        dve.wait_ge(self.hi_ready, 1)
        dve.tensor_tensor(self.lo[:], self.raw[:, 0:self.width], self.hi[:].bitcast(F32),
                          ALU.subtract).then_inc(self.lo_ready, 1)


def product3(pe, out, w_hi, w_lo, x_hi, x_lo, start=True, stop=True):
    pe.matmul(out, w_hi, x_hi, start=start, stop=False)
    pe.matmul(out, w_hi, x_lo, start=False, stop=False)
    return pe.matmul(out, w_lo, x_hi, start=False, stop=stop)


def lagged(eng, body, tail):
    body(0, None)
    with eng.Fori(1, NC) as c:
        body(c, c - 1)
    tail(NC - 1)


def each(eng, body):
    body(0)
    with eng.Fori(1, NC) as c:
        body(c)


def enter(nc, net):
    with Layer(nc) as ctx:
        sem = lambda n: ctx.sem(f"in_{n}")
        bank = ctx.enter_context(nc.psum_tensor("in_bank", [P, CH], F32))
        x_loaded = [sem(f"x_loaded{c}") for c in range(NC)]
        const_loaded, made = sem("const_loaded"), sem("made")
        staged, turned, hi_ready, lo_ready = sem("staged"), sem("turned"), sem("hi_ready"), sem("lo_ready")
        with nc.Block() as block:
            @block.sync
            def _(sp):
                sp.dma_start(net.ident[:], net.dram["ident"]).then_inc(const_loaded, 16)
                sp.dma_start(net.ident16[:], net.dram["ident16"]).then_inc(const_loaded, 16)
                sp.dma_start(net.const[:], net.dram["const"]).then_inc(const_loaded, 16)
                for c in range(NC):
                    sp.dma_start(tile3(net.x_tok[:, c, :]),
                                 net.dram["x"][c].rearrange("(j p) d -> p j d", p=P)).then_inc(x_loaded[c], 16)

            @block.gpsimd
            def _(pool):
                pool.memset(net.m_half[:], -0.5).then_inc(made, 1)

            @block.tensor
            def _(pe):
                pe.wait_ge(const_loaded, 48)
                for c in range(NC):
                    pe.wait_ge(x_loaded[c], 16)
                    wait(pe, lo_ready, c)
                    for j in range(NB):
                        mm = pe.transpose(bank[:, j * P:(j + 1) * P], net.x_tok[:, c, j * P:(j + 1) * P], net.ident[:])
                    mm.then_inc(turned, 1)

            @block.scalar
            def _(act):
                with act.Fori(0, NC) as c:
                    act.wait_ge(turned, c + 1)
                    act.activation(net.x_hi[:, at(c)], bank[:], ACT.Copy).then_inc(hi_ready, 1)

            @block.vector
            def _(dve):
                with dve.Fori(0, NC) as c:
                    dve.wait_ge(hi_ready, c + 1)
                    dve.tensor_tensor(net.x_lo[:, at(c)], bank[:], net.x_hi[:, at(c)].bitcast(F32),
                                      ALU.subtract).then_inc(lo_ready, 1)


def softmax_attention(nc, net, name, windowed):
    dram = net.dram[name]
    WQ, WK, WV, WO = 0, GROUPS * P, 2 * GROUPS * P, 2 * GROUPS * P + P
    WIDTH = WO + P
    BIAS = WIDTH
    if windowed:
        max_slots = [[(0, 0, 1, 0, [(0, 0)]), (1, 0, 2, 128, [(1, 128), (0, 256)])],
                     [(2, 1, 2, 0, [(1, 0), (0, 128)]), (3, 2, 2, 256, [(1, 256), (0, 384)])]]
        exp_slots = [[(0, 0, 2, 0, [(0, 0), (1, 128)]), (1, 1, 2, 256, [(0, 256), (1, 384)])],
                     [(2, 2, 2, 0, [(0, 0), (1, 128)]), (3, 3, 1, 256, [(0, 256)])]]
    else:
        max_slots = [[(0, 0, 4, 0, [(0, 0)])],
                     [(1, 1, 3, 0, [(0, 0)]), (3, 3, 1, 384, [(0, 384)])],
                     [(2, 2, 2, 0, [(0, 0)])]]
        exp_slots = [[(3, 0, 4, 0, [(0, 384)])],
                     [(2, 0, 3, 0, [(0, 256)]), (0, 0, 1, 384, [(0, 384)])],
                     [(1, 0, 2, 0, [(0, 128)])]]
    NMS, NES = len(max_slots) * GH, len(exp_slots) * GH // 2
    PAIRS = GH // 2
    NP = 4

    EV = ["V", "AT", "VT", "Q0", "K0", "WO", "Q1", "K1", "Y", "T0", "Q2", "K2", "X", "T1", "O0",
          "Q3", "K3", "T2", "O1", "T3", "O2", "O3"]
    LAG = ["AT", "WO", "Y", "X"]
    FIRST = [e for e in EV if e not in LAG]

    def nth(c, e):
        if isinstance(c, int) and c == 0:
            return FIRST.index(e)
        return c * len(EV) - len(LAG) + EV.index(e)

    def nth_last(e):
        return NC * len(EV) - len(LAG) + LAG.index(e)

    with Layer(nc) as ctx:
        sb = lambda n, s, dt=F32: ctx.enter_context(nc.sbuf_tensor(f"{name}_{n}", s, dt))
        ps = lambda n, s: ctx.enter_context(nc.psum_tensor(f"{name}_{n}", s, F32))
        sem = lambda n: ctx.sem(f"{name}_{n}")
        w = Weights(nc, ctx, name, dram["w"], WIDTH)
        masks = sb("masks", [P, 4, P], BF16)
        q_bias = sb("q_bias", [P, GROUPS])
        v_t = sb("v_t", [P, CH])
        vals = sb("vals", [P, NB, HEADS, QUAD])
        raw = [sb(f"raw{i}", [P, CH]) for i in range(2)]
        raw_hi = [sb(f"raw_hi{i}", [P, CH], F32R) for i in range(2)]
        q_st = [sb(f"q_st{i}", [P, CH], F32R) for i in range(2)]
        k_st = [sb(f"k_st{i}", [P, CH], F32R) for i in range(2)]
        qm_st = [sb(f"qm_st{i}", [P, CH], F32R) for i in range(2)]
        mx = sb("mx", [P, HEADS, NB])
        nm_hi = sb("nm_hi", [P, NB, GH], F32R)
        m_stage = sb("m_stage", [P, NB, P])
        probs = [sb(f"probs{i}", [P, 2, CH]) for i in range(NP)]
        o_t = sb("o_t", [P, CH])
        rden = sb("rden", [P, NB * GH])
        attn = sb("attn", [P, CH])
        a_hi = sb("a_hi", [P, CH], F32R)
        a_lo = sb("a_lo", [P, CH], F32R)
        SM = [ps(f"SM{i}", [P, CH]) for i in range(2)]
        SE = [ps(f"SE{i}", [P, 2, CH]) for i in range(2)]
        OT = ps("OT", [P, CH])
        MISC = ps("MISC", [P, CH])

        masks_loaded, zeroed = sem("masks_loaded"), sem("zeroed")
        bank_full, bank_free = sem("bank_full"), sem("bank_free")
        norm = Norm(nc, ctx, net, name, shared=(bank_full, bank_free))
        split_ready = sem("split_ready")
        smax_full, smax_read = sem("smax_full"), sem("smax_read")
        m_stepped, m_staged = sem("m_stepped"), sem("m_staged")
        sexp_full, exp_done, pv_done = sem("sexp_full"), sem("exp_done"), sem("pv_done")
        ot_read, rden_ready, attn_hi = sem("ot_read"), sem("rden_ready"), sem("attn_hi")
        bias_ready = sem("bias_ready")

        def mst3(i):
            return m_stage[:, :, R_MAX + i:R_MAX + i + QUAD * (GH - 1) + 1:QUAD]

        def n_static(g, s):
            return g * NES + s

        with nc.Block() as block:
            @block.sync
            def _(sp):
                w.sp_load(sp)
                sp.dma_start(masks[:], dram["masks"]).then_inc(masks_loaded, 16)

                def body(c, lag):
                    if lag is not None:
                        norm.sp_save(sp, lag)
                lagged(sp, body, lambda c: norm.sp_save(sp, c))
                norm.sp_end(sp)

            @block.gpsimd
            def _(pool):
                pool.memset(m_stage[:], 0.0).then_inc(zeroed, 1)
                pool.memset(vals[:], 0.0).then_inc(zeroed, 1)
                pool.wait_ge(zeroed, 2)
                pool.memset(vals[:, :, :, DH:DH + 1], 1.0).then_inc(zeroed, 1)

                def body(c, lag):
                    if lag is not None:
                        norm.pool_root(pool, lag)
                lagged(pool, body, lambda c: norm.pool_root(pool, c))

            @block.tensor
            def _(pe):
                def claim(n):
                    wait(pe, bank_free, n)

                def project(c, e, col):
                    claim(nth(c, e))
                    product3(pe, MISC[:], w.hi[:, col:col + P], w.lo[:, col:col + P],
                             net.x_hi[:, at(c)], net.x_lo[:, at(c)]).then_inc(bank_full, 1)

                def turn(n, src):
                    claim(n)
                    for j in range(NB):
                        mm = pe.transpose(MISC[:, j * P:(j + 1) * P], src(j), net.ident[:])
                    mm.then_inc(bank_full, 1)

                def max_slot(c, g, s):
                    r, slot = s // len(max_slots), max_slots[s % len(max_slots)]
                    n = (c * GROUPS + g) * NMS + s
                    bank, q0 = SM[s % 2], QUAD * r
                    if s == 0:
                        pe.wait_ge(split_ready, c * 2 * GROUPS + 2 * g + 2)
                    if not (isinstance(c, int) and c == 0 and g == 0 and s < 2):
                        pe.wait_ge(smax_read, n - 1)
                    for qi, k0, nk, col, mk in slot:
                        pe.matmul(bank[:, col:col + nk * P], q_st[g % 2][q0:q0 + K_RAW, qi * P:(qi + 1) * P],
                                  k_st[g % 2][q0:q0 + K_RAW, k0 * P:(k0 + nk) * P], start=True, stop=False,
                                  tile_position=(q0, 0))
                        for i, (table, mcol) in enumerate(mk):
                            mm = pe.matmul(bank[:, mcol:mcol + P], net.ident16[:], masks[:, table, :],
                                           start=False, stop=i == len(mk) - 1)
                    mm.then_inc(smax_full, 1)

                def exp_slot(c, g, s):
                    pair, slot = s // len(exp_slots), exp_slots[s % len(exp_slots)]
                    n = (c * GROUPS + g) * NES + s
                    if s == 0:
                        pe.wait_ge(bank_free, nth(c, f"T{g}") + 1)
                    if not (isinstance(c, int) and c == 0 and g == 0 and s < 2):
                        pe.wait_ge(exp_done, n - 1)
                    for b in range(2):
                        bank, q0 = SE[s % 2][:, b, :], QUAD * (2 * pair + b)
                        for kj, qa, nq, col, mk in slot:
                            pe.matmul(bank[:, col:col + nq * P], k_st[g % 2][q0:q0 + K_MAX, kj * P:(kj + 1) * P],
                                      qm_st[g % 2][q0:q0 + K_MAX, qa * P:(qa + nq) * P], start=True, stop=False,
                                      tile_position=(q0, 0))
                            for i, (table, mcol) in enumerate(mk):
                                mm = pe.matmul(bank[:, mcol:mcol + P], net.ident16[:], masks[:, 2 + table, :],
                                               start=False, stop=i == len(mk) - 1)
                    mm.then_inc(sexp_full, 1)

                def pv_slot(c, g, s):
                    pair, slot = s // len(exp_slots), exp_slots[s % len(exp_slots)]
                    n = (c * GROUPS + g) * NES + s
                    if s == 0:
                        wait(pe, ot_read, c * GROUPS + g)
                    pe.wait_ge(exp_done, n + 1)
                    for b in range(2):
                        r = 2 * pair + b
                        for i, (kj, qa, nq, col, mk) in enumerate(slot):
                            first = s % len(exp_slots) == 0 and i == 0
                            final = s % len(exp_slots) == len(exp_slots) - 1 and i == len(slot) - 1
                            mm = pe.matmul(OT[QUAD * r:QUAD * r + QUAD, qa * P:(qa + nq) * P],
                                           vals[:, kj, GH * g + r, :], probs[n_static(g, s) % NP][:, b, col:col + nq * P],
                                           start=first, stop=final, skip_group_check=True,
                                           tile_position=(0, QUAD * r))
                    mm.then_inc(pv_done, 1)

                def group(c, g):
                    m = 0
                    for s in range(NES):
                        exp_slot(c, g, s)
                        if g + 1 < GROUPS:
                            for _ in range(NMS // NES):
                                max_slot(c, g + 1, m)
                                m += 1
                        if s:
                            pv_slot(c, g, s - 1)
                    pv_slot(c, g, NES - 1)

                def turn_max(c, g):
                    pe.wait_ge(m_staged, c * GROUPS + g + 1)
                    turn(nth(c, f"T{g}"), lambda j: m_stage[:, j, :])

                def turn_out(c, g):
                    pe.wait_ge(ot_read, c * GROUPS + g + 1)
                    turn(nth(c, f"O{g}"), lambda j: o_t[:, j * P:(j + 1) * P])

                def attn_t(n):
                    turn(n, lambda j: attn[:, j * P:(j + 1) * P])

                def out_proj(lag, n):
                    claim(n)
                    product3(pe, MISC[:], w.hi[:, WO:WO + P], w.lo[:, WO:WO + P], a_hi[:], a_lo[:]).then_inc(bank_full, 1)

                def body(c, lag):
                    project(c, "V", WV)
                    if lag is not None:
                        attn_t(nth(c, "AT"))
                    pe.wait_ge(bank_free, nth(c, "V") + 1)
                    turn(nth(c, "VT"), lambda j: v_t[:, j * P:(j + 1) * P])
                    project(c, "Q0", WQ)
                    project(c, "K0", WK)
                    if lag is not None:
                        out_proj(lag, nth(c, "WO"))
                    for s in range(NMS):
                        max_slot(c, 0, s)
                    project(c, "Q1", WQ + P)
                    project(c, "K1", WK + P)
                    if lag is not None:
                        norm.pe_turn_y(pe, lag, MISC, nth(c, "Y"))
                    turn_max(c, 0)
                    group(c, 0)
                    project(c, "Q2", WQ + 2 * P)
                    project(c, "K2", WK + 2 * P)
                    if lag is not None:
                        norm.pe_turn_x(pe, lag, MISC, nth(c, "X"))
                    turn_max(c, 1)
                    turn_out(c, 0)
                    group(c, 1)
                    project(c, "Q3", WQ + 3 * P)
                    project(c, "K3", WK + 3 * P)
                    turn_max(c, 2)
                    turn_out(c, 1)
                    group(c, 2)
                    turn_max(c, 3)
                    turn_out(c, 2)
                    group(c, 3)
                    turn_out(c, 3)

                def tail(c):
                    attn_t(nth_last("AT"))
                    out_proj(c, nth_last("WO"))
                    norm.pe_turn_y(pe, c, MISC, nth_last("Y"))
                    norm.pe_turn_x(pe, c, MISC, nth_last("X"))

                pe.wait_ge(w.lo_ready, 1)
                pe.wait_ge(masks_loaded, 16)
                pe.wait_ge(zeroed, 3)
                lagged(pe, body, tail)

            @block.scalar
            def _(act):
                def take(n):
                    act.wait_ge(bank_full, n + 1)

                def v(c):
                    take(nth(c, "V"))
                    act.activation(v_t[:], MISC[:], ACT.Identity, bias=w.raw[:, BIAS + 8:BIAS + 9]).then_inc(bank_free, 1)

                def qk(c, e):
                    g, k = int(e[1]), e[0] == "K"
                    n = 2 * g + k
                    take(nth(c, e))
                    i = n % 2
                    if not (isinstance(c, int) and c == 0 and n < 2):
                        act.wait_ge(split_ready, c * 2 * GROUPS + n - 1)
                    bias = w.raw[:, BIAS + 4 + g:BIAS + 5 + g] if k else q_bias[:, g:g + 1]
                    scale = 1.0 if k else w.raw[:, BIAS + 10:BIAS + 11]
                    act.activation(raw[i][:], MISC[:], ACT.Identity, bias=bias, scale=scale)
                    act.activation(raw_hi[i][:], MISC[:], ACT.Identity, bias=bias, scale=scale).then_inc(bank_free, 1)

                def attn_upper(n):
                    take(n)
                    act.activation(a_hi[:], MISC[:], ACT.Copy).then_inc(attn_hi, 1)

                def y(lag, n):
                    take(n)
                    act.activation(net.y_stage[:], MISC[:], ACT.Identity,
                                   bias=w.raw[:, BIAS + 9:BIAS + 10]).then_inc(bank_free, 1)

                def exps(c, g, s):
                    slot = exp_slots[s % len(exp_slots)]
                    n = (c * GROUPS + g) * NES + s
                    width = max(col + nq * P for _, _, nq, col, _ in slot)
                    act.wait_ge(sexp_full, n + 1)
                    if not (isinstance(c, int) and c == 0 and n_static(g, s) < NP):
                        act.wait_ge(pv_done, n - NP + 1)
                    act.activation(probs[n_static(g, s) % NP][:, :, 0:width], SE[s % 2][:, :, 0:width],
                                   ACT.Exp).then_inc(exp_done, 1)

                def outputs(c, g):
                    act.wait_ge(pv_done, (c * GROUPS + g + 1) * NES)
                    if g:
                        act.wait_ge(bank_full, nth(c, f"O{g - 1}") + 1)
                    elif not isinstance(c, int):
                        act.wait_ge(bank_full, nth(c, "V"))
                    act.activation(o_t[:], OT[:], ACT.Copy).then_inc(ot_read, 1)

                def group(c, g):
                    for s in range(NES):
                        exps(c, g, s)
                    outputs(c, g)

                def body(c, lag):
                    v(c)
                    if lag is not None:
                        attn_upper(nth(c, "AT"))
                    qk(c, "Q0")
                    qk(c, "K0")
                    if lag is not None:
                        y(lag, nth(c, "WO"))
                    qk(c, "Q1")
                    qk(c, "K1")
                    group(c, 0)
                    qk(c, "Q2")
                    qk(c, "K2")
                    if lag is not None:
                        norm.act_hi(act, lag, MISC, nth(c, "X"))
                    group(c, 1)
                    qk(c, "Q3")
                    qk(c, "K3")
                    group(c, 2)
                    group(c, 3)

                def tail(c):
                    attn_upper(nth_last("AT"))
                    y(c, nth_last("WO"))
                    norm.act_hi(act, c, MISC, nth_last("X"))

                w.act_split(act)
                act.wait_ge(bias_ready, 1)
                act.activation(net.spare[:, 0:1], w.raw[:, 0:1], ACT.Exp)
                lagged(act, body, tail)

            @block.vector
            def _(dve):
                def take(n):
                    dve.wait_ge(bank_full, n + 1)

                def v(c):
                    take(nth(c, "VT"))
                    for j in range(NB):
                        last = dve.tensor_copy(vals[:, j, :, 0:DH],
                                               MISC[:, j * P:(j + 1) * P].rearrange("p (h d) -> p h d", d=DH))
                    last.then_inc(bank_free, 1)

                def split(c, e):
                    g, k = int(e[1]), e[0] == "K"
                    n, i = 2 * g + k, (2 * g + k) % 2
                    dve.wait_ge(bank_free, nth(c, e) + 1)
                    if not (isinstance(c, int) and c == 0 and g < 2):
                        dve.wait_ge(sexp_full, (c * GROUPS + g - 1) * NES)
                    dst = (k_st if k else q_st)[g % 2]
                    dve.scalar_tensor_tensor(out=dst[:], in0=raw_hi[i][:].bitcast(F32), scalar=net.const[:, k:k + 1],
                                             in1=raw[i][:], op0=ALU.mult, op1=ALU.add).then_inc(split_ready, 1)

                def maxima(c, g):
                    for s in range(NMS):
                        r, slot = s // len(max_slots), max_slots[s % len(max_slots)]
                        n = (c * GROUPS + g) * NMS + s
                        dve.wait_ge(smax_full, n + 1)
                        if s == 0:
                            wait(dve, m_staged, c * GROUPS + g)
                        for qi, k0, nk, col, mk in slot:
                            last = dve.tensor_reduce(mx[:, GH * g + r, qi:qi + 1], SM[s % 2][:, col:col + nk * P],
                                                     AX.X, ALU.max)
                        last.then_inc(smax_read, 1)

                def stage_max(c, g):
                    n = c * GROUPS + g
                    mg = mx[:, GH * g:GH * g + GH, :].rearrange("p h j -> p j h")
                    dve.wait_ge(smax_read, (n + 1) * NMS)
                    dve.tensor_scalar(nm_hi[:], mg, -1.0, None, ALU.mult).then_inc(m_stepped, 1)
                    dve.wait_ge(m_stepped, n + 1)
                    dve.tensor_copy(mst3(0), nm_hi[:].bitcast(F32))
                    dve.scalar_tensor_tensor(out=mst3(1), in0=mg, scalar=-1.0, in1=nm_hi[:].bitcast(F32),
                                             op0=ALU.mult, op1=ALU.subtract).then_inc(m_staged, 1)

                def add_max(c, g):
                    take(nth(c, f"T{g}"))
                    dve.tensor_tensor(qm_st[g % 2][:], q_st[g % 2][:].bitcast(F32), MISC[:],
                                      ALU.add).then_inc(bank_free, 1)

                def outputs(c, g):
                    take(nth(c, f"O{g}"))
                    o4 = MISC[:].rearrange("p (j r w) -> p j r w", j=NB, w=QUAD)
                    r3 = rden[:].rearrange("p (j r) -> p j r", r=GH)
                    n = c * GROUPS + g
                    dve.reciprocal(r3, o4[:, :, :, DH]).then_inc(rden_ready, 1)
                    dve.wait_ge(rden_ready, n + 1)
                    a4 = attn[:].rearrange("p (j g r d) -> p j g r d", j=NB, g=GROUPS, d=DH)[:, :, g]
                    dve.tensor_tensor(a4, o4[:, :, :, 0:DH], r3.unsqueeze(3).broadcast_to([P, NB, GH, DH]),
                                      ALU.mult).then_inc(bank_free, 1)

                def attn_lower(lag, n):
                    dve.wait_ge(attn_hi, lag + 1)
                    dve.tensor_tensor(a_lo[:], MISC[:], a_hi[:].bitcast(F32), ALU.subtract).then_inc(bank_free, 1)

                def body(c, lag):
                    if lag is not None:
                        attn_lower(lag, nth(c, "AT"))
                    v(c)
                    split(c, "Q0")
                    split(c, "K0")
                    maxima(c, 0)
                    split(c, "Q1")
                    split(c, "K1")
                    stage_max(c, 0)
                    if lag is not None:
                        norm.dve_norm(dve, lag, MISC, nth(c, "Y"))
                        norm.dve_scale(dve, lag)
                    add_max(c, 0)
                    maxima(c, 1)
                    split(c, "Q2")
                    split(c, "K2")
                    stage_max(c, 1)
                    if lag is not None:
                        norm.dve_lo(dve, lag, MISC, nth(c, "X"))
                    add_max(c, 1)
                    outputs(c, 0)
                    maxima(c, 2)
                    split(c, "Q3")
                    split(c, "K3")
                    stage_max(c, 2)
                    add_max(c, 2)
                    outputs(c, 1)
                    maxima(c, 3)
                    stage_max(c, 3)
                    add_max(c, 3)
                    outputs(c, 2)
                    outputs(c, 3)

                def tail(c):
                    attn_lower(c, nth_last("AT"))
                    norm.dve_norm(dve, c, MISC, nth_last("Y"))
                    norm.dve_scale(dve, c)
                    norm.dve_lo(dve, c, MISC, nth_last("X"))

                w.dve_split(dve)
                dve.tensor_scalar(q_bias[:], w.raw[:, BIAS:BIAS + 4], w.raw[:, BIAS + 10:BIAS + 11], None,
                                  ALU.mult).then_inc(bias_ready, 1)
                dve.wait_ge(zeroed, 3)
                lagged(dve, body, tail)


def gated_recurrence(nc, net):
    dram = net.dram["L1_attn"]
    WG, WH, WO = 0, P, 2 * P
    WIDTH = 3 * P
    BIAS = WIDTH
    with Layer(nc) as ctx:
        sb = lambda n, s, dt=F32: ctx.enter_context(nc.sbuf_tensor(f"rec_{n}", s, dt))
        ps = lambda n: ctx.enter_context(nc.psum_tensor(f"rec_{n}", [P, CH], F32))
        sem = lambda n: ctx.sem(f"rec_{n}")
        w = Weights(nc, ctx, "rec", dram["w"], WIDTH)
        norm = Norm(nc, ctx, net, "rec")
        bias = sb("bias", [P, 3])
        t_gate, t_hid, hid = sb("t_gate", [P, CH]), sb("t_hid", [P, CH]), sb("hid", [P, CH])
        u, v, h = sb("u", [P, CH]), sb("v", [P, CH]), sb("h", [P, CH])
        h_hi, h_lo = sb("h_hi", [P, CH], F32R), sb("h_lo", [P, CH], F32R)
        decay = sb("decay", [P, CH])
        GATE, HIDB, OUT, TY, TX = ps("GATE"), ps("HIDB"), ps("OUT"), ps("TY"), ps("TX")
        made, bias_ready = sem("made"), sem("bias_ready")
        gate_full, hid_full, gate_read, hid_read = sem("gate_full"), sem("hid_full"), sem("gate_read"), sem("hid_read")
        u_ready, v_ready, h_ready = sem("u_ready"), sem("v_ready"), sem("h_ready")
        h_hi_ready, h_lo_ready, out_full = sem("h_hi_ready"), sem("h_lo_ready"), sem("out_full")
        with nc.Block() as block:
            @block.sync
            def _(sp):
                w.sp_load(sp)
                with sp.Fori(0, NC) as c:
                    norm.sp_save(sp, c)
                norm.sp_end(sp)

            @block.gpsimd
            def _(pool):
                pool.memset(decay[:], 0.9).then_inc(made, 1)
                each(pool, lambda c: norm.pool_root(pool, c))

            @block.tensor
            def _(pe):
                def body(c, lag):
                    xh, xl = net.x_hi[:, at(c)], net.x_lo[:, at(c)]
                    wait(pe, gate_read, c)
                    product3(pe, GATE[:], w.hi[:, WG:WG + P], w.lo[:, WG:WG + P], xh, xl).then_inc(gate_full, 1)
                    wait(pe, hid_read, c)
                    product3(pe, HIDB[:], w.hi[:, WH:WH + P], w.lo[:, WH:WH + P], xh, xl).then_inc(hid_full, 1)
                    if lag is not None:
                        norm.pe_turn_y(pe, lag, TY)
                    pe.wait_ge(h_lo_ready, c + 1)
                    wait(pe, norm.y_staged, c)
                    product3(pe, OUT[:], w.hi[:, WO:WO + P], w.lo[:, WO:WO + P], h_hi[:], h_lo[:]).then_inc(out_full, 1)
                    if lag is not None:
                        norm.pe_turn_x(pe, lag, TX)

                def tail(c):
                    norm.pe_turn_y(pe, c, TY)
                    norm.pe_turn_x(pe, c, TX)

                pe.wait_ge(w.lo_ready, 1)
                lagged(pe, body, tail)

            @block.scalar
            def _(act):
                def body(c, lag):
                    act.wait_ge(gate_full, c + 1)
                    wait(act, v_ready, c)
                    act.activation(t_gate[:], GATE[:], ACT.Tanh, bias=bias[:, 0:1], scale=0.5).then_inc(gate_read, 1)
                    act.wait_ge(hid_full, c + 1)
                    act.activation(t_hid[:], HIDB[:], ACT.Tanh, bias=bias[:, 1:2], scale=0.5)
                    act.activation(hid[:], HIDB[:], ACT.Identity, bias=bias[:, 2:3], scale=0.025).then_inc(hid_read, 1)
                    act.wait_ge(h_ready, c + 1)
                    wait(act, out_full, c)
                    act.activation(h_hi[:], h[:], ACT.Copy).then_inc(h_hi_ready, 1)
                    if lag is not None:
                        norm.act_hi(act, lag, TX)
                    act.wait_ge(out_full, c + 1)
                    wait(act, norm.y_turned, c)
                    act.activation(net.y_stage[:], OUT[:], ACT.Identity,
                                   bias=w.raw[:, BIAS + 2:BIAS + 3]).then_inc(norm.y_staged, 1)

                w.act_split(act)
                act.wait_ge(bias_ready, 1)
                act.activation(net.spare[:, 0:1], bias[:, 0:1], ACT.Tanh)
                lagged(act, body, lambda c: norm.act_hi(act, c, TX))

            @block.vector
            def _(dve):
                def body(c, lag):
                    if lag is not None:
                        norm.dve_norm(dve, lag, TY)
                    dve.wait_ge(gate_read, c + 1)
                    dve.wait_ge(hid_read, c + 1)
                    dve.scalar_tensor_tensor(out=u[:], in0=t_hid[:], scalar=1.0, in1=hid[:],
                                             op0=ALU.add, op1=ALU.mult).then_inc(u_ready, 1)
                    dve.wait_ge(u_ready, c + 1)
                    dve.scalar_tensor_tensor(out=v[:], in0=t_gate[:], scalar=1.0, in1=u[:],
                                             op0=ALU.add, op1=ALU.mult).then_inc(v_ready, 1)
                    dve.wait_ge(v_ready, c + 1)
                    wait(dve, h_hi_ready, c)
                    dve.tensor_tensor_scan(h[:], decay[:], v[:], 0.0, ALU.mult, ALU.add).then_inc(h_ready, 1)
                    if lag is not None:
                        norm.dve_scale(dve, lag)
                    dve.wait_ge(h_hi_ready, c + 1)
                    wait(dve, out_full, c)
                    dve.tensor_tensor(h_lo[:], h[:], h_hi[:].bitcast(F32), ALU.subtract).then_inc(h_lo_ready, 1)
                    if lag is not None:
                        norm.dve_lo(dve, lag, TX)

                def tail(c):
                    norm.dve_norm(dve, c, TY)
                    norm.dve_scale(dve, c)
                    norm.dve_lo(dve, c, TX)

                w.dve_split(dve)
                dve.tensor_scalar(bias[:, 0:2], w.raw[:, BIAS:BIAS + 2], 0.5, None, ALU.mult)
                dve.tensor_scalar(bias[:, 2:3], w.raw[:, BIAS + 1:BIAS + 2], 0.025, None, ALU.mult).then_inc(bias_ready, 1)
                dve.wait_ge(made, 1)
                lagged(dve, body, tail)


def ternary_ffn(nc, net):
    dram = net.dram["L1_ffn"]
    KT = HID // P
    W1, W2 = 0, HID
    H1, H2 = 2 * HID, 2 * HID + KT * HID
    W3 = 2 * HID + 2 * KT * HID
    WIDTH = W3 + KT * P
    S1, S2, SH1, SH2, S3 = 0, KT, 2 * KT, 3 * KT, 4 * KT
    UNITS = 3 * KT
    with Layer(nc) as ctx:
        sb = lambda n, s, dt=F32: ctx.enter_context(nc.sbuf_tensor(f"ter_{n}", s, dt))
        ps = lambda n: ctx.enter_context(nc.psum_tensor(f"ter_{n}", [P, CH], F32))
        sem = lambda n: ctx.sem(f"ter_{n}")
        norm = Norm(nc, ctx, net, "ter")
        w_hi, w_lo = sb("w_hi", [P, WIDTH], F32R), sb("w_lo", [P, WIDTH], F32R)
        PIECES = [(0, H1), (H1, H2), (H2, W3), (W3, WIDTH)]
        w_raw = [sb(f"w_raw{i}", [P, KT * HID]) for i in range(2)]
        scales = sb("scales", [P, 4 * KT + 1])
        half = sb("half", [P, KT])
        t_silu = [sb(f"t_silu{i}", [P, CH]) for i in range(2)]
        z_half = [sb(f"z_half{i}", [P, CH]) for i in range(2)]
        silu = [sb(f"silu{i}", [P, CH]) for i in range(2)]
        hid = [sb(f"hid{i}", [P, CH]) for i in range(2)]
        h_hi = [sb(f"h_hi{i}", [P, KT, CH], F32R) for i in range(2)]
        h_lo = [sb(f"h_lo{i}", [P, KT, CH], F32R) for i in range(2)]
        B = [ps(f"B{i}") for i in range(4)]
        OUT, TY, TX = ps("OUT"), ps("TY"), ps("TX")
        w_loaded = [sem(f"w_loaded{i}") for i in range(len(PIECES))]
        scales_loaded, w_hi_ready, w_lo_ready, half_ready = (sem("scales_loaded"), sem("w_hi_ready"),
                                                             sem("w_lo_ready"), sem("half_ready"))
        a_full, b_full, a_read = sem("a_full"), sem("b_full"), sem("a_read")
        silu_ready, hid_made = sem("silu_ready"), sem("hid_made")
        g_full, g_made = sem("g_full"), sem("g_made")
        hi_made, lo_made, out_full = sem("hi_made"), sem("lo_made"), sem("out_full")
        with nc.Block() as block:
            @block.sync
            def _(sp):
                for i, (a, b) in enumerate(PIECES):
                    if i >= 2:
                        sp.wait_ge(w_lo_ready, i - 1)
                    sp.dma_start(w_raw[i % 2][:, 0:b - a], dram["w"][:, a:b]).then_inc(w_loaded[i], 16)
                    if i == 0:
                        sp.dma_start(scales[:], dram["scales"]).then_inc(scales_loaded, 16)
                with sp.Fori(0, NC) as c:
                    norm.sp_save(sp, c)
                norm.sp_end(sp)

            @block.gpsimd
            def _(pool):
                each(pool, lambda c: norm.pool_root(pool, c))

            @block.tensor
            def _(pe):
                def first(c):
                    xh, xl = net.x_hi[:, at(c)], net.x_lo[:, at(c)]
                    for t in range(KT):
                        a, b = B[t % 2], B[2 + t % 2]
                        if t < 2:
                            wait(pe, g_made, 2 * KT * c)
                        else:
                            pe.wait_ge(a_read, KT * c + t - 1)
                        col = W1 + t * P
                        product3(pe, a[:], w_hi[:, col:col + P], w_lo[:, col:col + P], xh, xl).then_inc(a_full, 1)
                        if t >= 2:
                            pe.wait_ge(hid_made, KT * c + t - 1)
                        col = W2 + t * P
                        product3(pe, b[:], w_hi[:, col:col + P], w_lo[:, col:col + P], xh, xl).then_inc(b_full, 1)

                def hidden(c, layer):
                    src, base = (layer - 1) % 2, (H1, H2)[layer - 1]
                    for k in range(KT):
                        pe.wait_ge(lo_made, UNITS * c + KT * (layer - 1) + k + 1)
                        for t in range(KT):
                            if k == 0:
                                if layer == 1:
                                    pe.wait_ge(a_read, KT * (c + 1))
                                    pe.wait_ge(hid_made, KT * (c + 1))
                                else:
                                    pe.wait_ge(g_made, 2 * KT * c + t + 1)
                            col = base + k * HID + t * P
                            mm = product3(pe, B[t][:], w_hi[:, col:col + P], w_lo[:, col:col + P],
                                          h_hi[src][:, k, :], h_lo[src][:, k, :], start=k == 0, stop=k == KT - 1)
                            if k == KT - 1:
                                mm.then_inc(g_full, 1)

                def out(c):
                    wait(pe, norm.y_staged, c)
                    for k in range(KT):
                        pe.wait_ge(lo_made, UNITS * c + 2 * KT + k + 1)
                        col = W3 + k * P
                        mm = product3(pe, OUT[:], w_hi[:, col:col + P], w_lo[:, col:col + P],
                                      h_hi[0][:, k, :], h_lo[0][:, k, :], start=k == 0, stop=k == KT - 1)
                    mm.then_inc(out_full, 1)

                def body(c, lag):
                    if isinstance(c, int):
                        pe.wait_ge(w_lo_ready, 1)
                    first(c)
                    if lag is not None:
                        norm.pe_turn_y(pe, lag, TY)
                    if isinstance(c, int):
                        pe.wait_ge(w_lo_ready, 2)
                    hidden(c, 1)
                    if lag is not None:
                        norm.pe_turn_x(pe, lag, TX)
                    if isinstance(c, int):
                        pe.wait_ge(w_lo_ready, 3)
                    hidden(c, 2)
                    if isinstance(c, int):
                        pe.wait_ge(w_lo_ready, 4)
                    out(c)

                def tail(c):
                    norm.pe_turn_y(pe, c, TY)
                    norm.pe_turn_x(pe, c, TX)

                lagged(pe, body, tail)

            @block.scalar
            def _(act):
                def upper(c, n):
                    layer, k = n // KT, n % KT
                    if layer == 0:
                        act.wait_ge(hid_made, KT * c + k + 1)
                    else:
                        act.wait_ge(g_made, 2 * KT * c + n - KT + 1)
                    if layer == 0:
                        wait(act, out_full, c)
                    elif layer == 1:
                        wait(act, g_full, 2 * KT * c)
                    else:
                        act.wait_ge(g_full, 2 * KT * c + KT)
                    act.activation(h_hi[layer % 2][:, k, :], hid[n % 2][:], ACT.Copy).then_inc(hi_made, 1)

                def first(c):
                    for t in range(KT):
                        act.wait_ge(a_full, KT * c + t + 1)
                        if not (isinstance(c, int) and c == 0 and t < 2):
                            act.wait_ge(silu_ready, KT * c + t - 1)
                        act.activation(t_silu[t % 2][:], B[t % 2][:], ACT.Tanh, scale=half[:, t:t + 1])
                        act.activation(z_half[t % 2][:], B[t % 2][:], ACT.Copy,
                                       scale=half[:, t:t + 1]).then_inc(a_read, 1)
                        if t:
                            upper(c, t - 1)
                    upper(c, KT - 1)

                def hidden(c, layer):
                    for t in range(KT):
                        n = KT * layer + t
                        act.wait_ge(g_full, 2 * KT * c + n - KT + 1)
                        act.wait_ge(lo_made, UNITS * c + n - 1)
                        act.activation(hid[n % 2][:], B[t][:], ACT.Gelu,
                                       scale=scales[:, KT * (layer + 1) + t:KT * (layer + 1) + t + 1]).then_inc(g_made, 1)
                        upper(c, n)

                def body(c, lag):
                    first(c)
                    hidden(c, 1)
                    if lag is not None:
                        norm.act_hi(act, lag, TX)
                    hidden(c, 2)
                    act.wait_ge(out_full, c + 1)
                    wait(act, norm.y_turned, c)
                    act.activation(net.y_stage[:], OUT[:], ACT.Copy, scale=scales[:, S3:S3 + 1]).then_inc(norm.y_staged, 1)

                for i, (a, b) in enumerate(PIECES):
                    act.wait_ge(w_loaded[i], 16)
                    act.activation(w_hi[:, a:b], w_raw[i % 2][:, 0:b - a], ACT.Copy).then_inc(w_hi_ready, 1)
                act.wait_ge(half_ready, 1)
                act.activation(net.spare[:, 0:1], half[:, 0:1], ACT.Gelu)
                lagged(act, body, lambda c: norm.act_hi(act, c, TX))

            @block.vector
            def _(dve):
                def lower(c, n):
                    layer, k = n // KT, n % KT
                    dve.wait_ge(hi_made, UNITS * c + n + 1)
                    dve.tensor_tensor(h_lo[layer % 2][:, k, :], hid[n % 2][:], h_hi[layer % 2][:, k, :].bitcast(F32),
                                      ALU.subtract).then_inc(lo_made, 1)

                def first(c):
                    for t in range(KT):
                        dve.wait_ge(a_read, KT * c + t + 1)
                        if not (isinstance(c, int) and c == 0 and t < 2):
                            dve.wait_ge(hid_made, KT * c + t - 1)
                        dve.scalar_tensor_tensor(out=silu[t % 2][:], in0=t_silu[t % 2][:], scalar=1.0,
                                                 in1=z_half[t % 2][:], op0=ALU.add, op1=ALU.mult).then_inc(silu_ready, 1)
                        dve.wait_ge(b_full, KT * c + t + 1)
                        dve.wait_ge(silu_ready, KT * c + t + 1)
                        if not (isinstance(c, int) and c == 0 and t < 2):
                            dve.wait_ge(lo_made, UNITS * c + t - 1)
                        dve.scalar_tensor_tensor(out=hid[t % 2][:], in0=B[2 + t % 2][:], scalar=scales[:, S2 + t:S2 + t + 1],
                                                 in1=silu[t % 2][:], op0=ALU.mult, op1=ALU.mult).then_inc(hid_made, 1)
                        if t:
                            lower(c, t - 1)
                    lower(c, KT - 1)

                def body(c, lag):
                    first(c)
                    if lag is not None:
                        norm.dve_norm(dve, lag, TY)
                        norm.dve_scale(dve, lag)
                    for n in range(KT, 2 * KT):
                        lower(c, n)
                    if lag is not None:
                        norm.dve_lo(dve, lag, TX)
                    for n in range(2 * KT, UNITS):
                        lower(c, n)

                def tail(c):
                    norm.dve_norm(dve, c, TY)
                    norm.dve_scale(dve, c)
                    norm.dve_lo(dve, c, TX)

                dve.wait_ge(scales_loaded, 16)
                dve.tensor_scalar(half[:], scales[:, S1:S1 + KT], 0.5, None, ALU.mult).then_inc(half_ready, 1)
                for i, (a, b) in enumerate(PIECES):
                    dve.wait_ge(w_hi_ready, i + 1)
                    dve.tensor_tensor(w_lo[:, a:b], w_raw[i % 2][:, 0:b - a], w_hi[:, a:b].bitcast(F32),
                                      ALU.subtract).then_inc(w_lo_ready, 1)
                lagged(dve, body, tail)


def linear_attention(nc, net):
    dram = net.dram["L3_attn"]
    FEATS = 32
    FW = GH * FEATS
    VW = D + HEADS
    YAT = 0.1
    WQ, WK, WV, WO, WP = 0, P, 2 * P, 3 * P, 4 * P
    WIDTH = WP + GROUPS * FW
    BIAS = WIDTH
    AT_, WO_, Y_, X_ = range(4)
    with Layer(nc) as ctx:
        sb = lambda n, s, dt=F32: ctx.enter_context(nc.sbuf_tensor(f"lin_{n}", s, dt))
        ps = lambda n: ctx.enter_context(nc.psum_tensor(f"lin_{n}", [P, CH], F32))
        sem = lambda n: ctx.sem(f"lin_{n}")
        w = Weights(nc, ctx, "lin", dram["w"], WIDTH)
        own = sb("own", [P, GROUPS, VW])
        qkv_t = [sb(f"qkv_t{i}", [P, CH]) for i in range(3)]
        sq = [sb(f"sq{i}", [P, CH]) for i in range(2)]
        ss, nrm, nrm_e, rinv = (sb("ss", [P, 2 * NB * HEADS]), sb("nrm", [P, 2 * NB * HEADS]),
                                sb("nrm_e", [P, 2 * NB * HEADS]), sb("rinv", [P, 2 * NB * HEADS]))
        root, root_g = sb("root", [P, 2 * NB * HEADS]), sb("root_g", [P, 2 * NB * HEADS])
        N_STEPS = 6
        normed = [sb(f"normed{i}", [P, CH]) for i in range(2)]
        n_hi = [sb(f"n_hi{i}", [P, CH], F32R) for i in range(2)]
        n_lo = [sb(f"n_lo{i}", [P, CH], F32R) for i in range(2)]
        vals = sb("vals", [P, NB, VW])
        k_feat = sb("k_feat", [P, NB, GROUPS * FW])
        q_relu = [sb(f"q_relu{i}", [P, CH]) for i in range(2)]
        q_feat = sb("q_feat", [P, GROUPS, CH])
        kv = sb("kv", [P, GROUPS, VW])
        den, rden = sb("den", [P, NB, HEADS]), sb("rden", [P, NB, HEADS])
        attn = sb("attn", [P, CH])
        a_hi, a_lo = sb("a_hi", [P, CH], F32R), sb("a_lo", [P, CH], F32R)
        A = [ps(f"A{i}") for i in range(3)]
        F = [ps(f"F{i}") for i in range(2)]
        KV = [ps(f"KV{i}") for i in range(2)]
        TB = ps("TB")
        norm_sems = sem("tb_full"), sem("tb_free")
        tb_full, tb_free = norm_sems
        norm = Norm(nc, ctx, net, "lin", shared=norm_sems)
        own_loaded, ones_made = sem("own_loaded"), sem("ones_made")
        proj_full, staged, turned = sem("proj_full"), sem("staged"), sem("turned")
        sq_ready, ss_ready, root_ready, n_stepped = sem("sq_ready"), sem("ss_ready"), sem("root_ready"), sem("n_stepped")
        normed_ready, vals_ready, back, n_hi_ready, n_lo_ready = (sem("normed_ready"), sem("vals_ready"), sem("back"),
                                                                  sem("n_hi_ready"), sem("n_lo_ready"))
        kf_full, kf_ready, qf_full, qr_ready, qf_ready = (sem("kf_full"), sem("kf_ready"), sem("qf_full"),
                                                          sem("qr_ready"), sem("qf_ready"))
        kv_full, kv_ready, o_full, o_stepped, attn_ready, attn_hi = (sem("kv_full"), sem("kv_ready"), sem("o_full"),
                                                                     sem("o_stepped"), sem("attn_ready"), sem("attn_hi"))
        with nc.Block() as block:
            @block.sync
            def _(sp):
                w.sp_load(sp)
                sp.dma_start(own[:], dram["own"]).then_inc(own_loaded, 16)
                with sp.Fori(0, NC) as c:
                    norm.sp_save(sp, c)
                norm.sp_end(sp)

            @block.gpsimd
            def _(pool):
                pool.memset(vals[:, :, D:VW], 1.0).then_inc(ones_made, 1)

                each(pool, lambda c: norm.pool_root(pool, c))

            @block.tensor
            def _(pe):
                def turn(src, bank):
                    for j in range(NB):
                        mm = pe.transpose(bank[:, j * P:(j + 1) * P], src[:, j * P:(j + 1) * P], net.ident[:])
                    return mm

                def attn_t(lag):
                    pe.wait_ge(attn_ready, 2 * (lag + 1))
                    wait(pe, tb_free, 4 * lag)
                    turn(attn, TB).then_inc(tb_full, 1)

                def out_proj(lag):
                    pe.wait_ge(tb_free, 4 * lag + WO_)
                    product3(pe, TB[:], w.hi[:, WO:WO + P], w.lo[:, WO:WO + P], a_hi[:], a_lo[:]).then_inc(tb_full, 1)

                def body(c, lag):
                    for i, col in enumerate((WQ, WK, WV)):
                        if i < 2:
                            wait(pe, n_lo_ready, 2 * c)
                        else:
                            wait(pe, vals_ready, c)
                        product3(pe, A[i][:], w.hi[:, col:col + P], w.lo[:, col:col + P],
                                 net.x_hi[:, at(c)], net.x_lo[:, at(c)]).then_inc(proj_full, 1)
                    if lag is not None:
                        attn_t(lag)
                    for i in range(3):
                        pe.wait_ge(staged, 3 * c + i + 1)
                        turn(qkv_t[i], A[i]).then_inc(turned, 1)
                    if lag is not None:
                        out_proj(lag)
                    for i in range(2):
                        pe.wait_ge(normed_ready, 2 * c + i + 1)
                        turn(normed[i], A[i]).then_inc(back, 1)
                    if lag is not None:
                        norm.pe_turn_y(pe, lag, TB, 4 * lag + Y_)
                    pe.wait_ge(n_lo_ready, 2 * c + 2)
                    for j in range(NB):
                        if j < 2:
                            wait(pe, qr_ready, GROUPS * c)
                        else:
                            pe.wait_ge(kf_ready, NB * c + j - 1)
                        sl = slice(j * P, (j + 1) * P)
                        ph, pl = w.hi[:, WP:WIDTH], w.lo[:, WP:WIDTH]
                        pe.matmul(F[j % 2][:], n_hi[1][:, sl], ph, start=True, stop=False)
                        pe.matmul(F[j % 2][:], n_lo[1][:, sl], ph, start=False, stop=False)
                        pe.matmul(F[j % 2][:], n_hi[1][:, sl], pl, start=False, stop=True).then_inc(kf_full, 1)
                    for g in range(GROUPS):
                        if g < 2:
                            pe.wait_ge(kf_ready, NB * c + NB - 1 + g)
                        else:
                            pe.wait_ge(qr_ready, GROUPS * c + g - 1)
                        col = WP + g * FW
                        product3(pe, F[g % 2][:], w.hi[:, col:col + FW], w.lo[:, col:col + FW],
                                 n_hi[0][:], n_lo[0][:]).then_inc(qf_full, 1)
                    if lag is not None:
                        norm.pe_turn_x(pe, lag, TB, 4 * lag + X_)
                    pe.wait_ge(vals_ready, c + 1)
                    pe.wait_ge(kf_ready, NB * (c + 1))
                    wait(pe, attn_ready, 2 * c)
                    for g in range(GROUPS):
                        for j in range(NB):
                            mm = pe.matmul(KV[g // 2][:, (g % 2) * VW:(g % 2 + 1) * VW], k_feat[:, j, g * FW:(g + 1) * FW],
                                           vals[:, j, :], start=j == 0, stop=j == NB - 1)
                        if g % 2:
                            mm.then_inc(kv_full, 1)
                    pe.wait_ge(kv_ready, 2 * c + 2)
                    pe.wait_ge(qf_ready, GROUPS * (c + 1))
                    for j in range(NB):
                        for g in range(GROUPS):
                            mm = pe.matmul(KV[j // 2][:, (j % 2) * VW:(j % 2 + 1) * VW], q_feat[:, g, j * P:(j + 1) * P],
                                           kv[:, g, :], start=g == 0, stop=g == GROUPS - 1)
                        if j % 2:
                            mm.then_inc(o_full, 1)

                def tail(c):
                    attn_t(c)
                    out_proj(c)
                    norm.pe_turn_y(pe, c, TB, 4 * c + Y_)
                    norm.pe_turn_x(pe, c, TB, 4 * c + X_)

                pe.wait_ge(w.lo_ready, 1)
                pe.wait_ge(ones_made, 1)
                lagged(pe, body, tail)

            @block.scalar
            def _(act):
                def attn_upper(lag):
                    act.wait_ge(tb_full, 4 * lag + AT_ + 1)
                    act.activation(a_hi[:], TB[:], ACT.Copy).then_inc(attn_hi, 1)

                def y(lag):
                    act.wait_ge(tb_full, 4 * lag + WO_ + 1)
                    act.activation(net.y_stage[:], TB[:], ACT.Identity, bias=w.raw[:, BIAS + 3:BIAS + 4]).then_inc(tb_free, 1)

                def body(c, lag):
                    for i in range(3):
                        act.wait_ge(proj_full, 3 * c + i + 1)
                        act.activation(qkv_t[i][:], A[i][:], ACT.Identity,
                                       bias=w.raw[:, BIAS + i:BIAS + i + 1]).then_inc(staged, 1)
                    if lag is not None:
                        attn_upper(lag)
                    for i in range(2):
                        act.wait_ge(turned, 3 * c + i + 1)
                        wait(act, ss_ready, c)
                        act.activation(sq[i][:], A[i][:], ACT.Square).then_inc(sq_ready, 1)
                    act.wait_ge(ss_ready, c + 1)
                    act.activation(root[:], ss[:], ACT.Sqrt).then_inc(root_ready, 1)
                    act.wait_ge(turned, 3 * c + 3)
                    act.activation(vals[:, :, 0:D], tile3(A[2][:]), ACT.Copy).then_inc(vals_ready, 1)
                    if lag is not None:
                        y(lag)
                    for i in range(2):
                        act.wait_ge(back, 2 * c + i + 1)
                        act.activation(n_hi[i][:], A[i][:], ACT.Copy).then_inc(n_hi_ready, 1)
                    for g in range(GROUPS):
                        act.wait_ge(qf_full, GROUPS * c + g + 1)
                        if not (isinstance(c, int) and c == 0 and g < 2):
                            act.wait_ge(qf_ready, GROUPS * c + g - 1)
                        act.activation(q_relu[g % 2][:], F[g % 2][:], ACT.Relu).then_inc(qr_ready, 1)
                        act.wait_ge(qr_ready, GROUPS * c + g + 1)
                        act.activation(q_feat[:, g, :], q_relu[g % 2][:], ACT.Copy, bias=YAT).then_inc(qf_ready, 1)
                    if lag is not None:
                        norm.act_hi(act, lag, TB, 4 * lag + X_)

                def tail(c):
                    attn_upper(c)
                    y(c)
                    norm.act_hi(act, c, TB, 4 * c + X_)

                w.act_split(act)
                act.activation(net.spare[:, 0:1], net.ident[:, 0:1], ACT.Sqrt)
                lagged(act, body, tail)

            @block.vector
            def _(dve):
                def attn_lower(lag):
                    dve.wait_ge(attn_hi, lag + 1)
                    dve.tensor_tensor(a_lo[:], TB[:], a_hi[:].bitcast(F32), ALU.subtract).then_inc(tb_free, 1)

                def body(c, lag):
                    if lag is not None:
                        attn_lower(lag)
                    for i in range(2):
                        dve.wait_ge(sq_ready, 2 * c + i + 1)
                        last = dve.tensor_reduce(ss[:, i * 64:(i + 1) * 64], sq[i][:].rearrange("p (n d) -> p n d", d=DH),
                                                 AX.X, ALU.add)
                    last.then_inc(ss_ready, 1)
                    dve.wait_ge(root_ready, c + 1)
                    dve.tensor_scalar(root_g[:], root[:], 1e-30, None, ALU.max).then_inc(n_stepped, 1)
                    dve.wait_ge(n_stepped, N_STEPS * c + 1)
                    dve.reciprocal(rinv[:], root_g[:]).then_inc(n_stepped, 1)
                    dve.wait_ge(n_stepped, N_STEPS * c + 2)
                    dve.tensor_tensor(nrm[:], ss[:], rinv[:], ALU.mult).then_inc(n_stepped, 1)
                    dve.wait_ge(n_stepped, N_STEPS * c + 3)
                    dve.tensor_tensor(nrm_e[:], nrm[:], root_g[:], ALU.add).then_inc(n_stepped, 1)
                    dve.wait_ge(n_stepped, N_STEPS * c + 4)
                    dve.tensor_scalar(nrm[:], nrm_e[:], 0.5, 1e-8, ALU.mult, ALU.add).then_inc(n_stepped, 1)
                    dve.wait_ge(n_stepped, N_STEPS * c + 5)
                    dve.reciprocal(rinv[:], nrm[:]).then_inc(n_stepped, 1)
                    dve.wait_ge(n_stepped, N_STEPS * c + 6)
                    for i in range(2):
                        r3 = rinv[:, i * 64:(i + 1) * 64].unsqueeze(2).broadcast_to([P, 64, DH])
                        dve.tensor_tensor(normed[i][:].rearrange("p (n d) -> p n d", d=DH),
                                          A[i][:].rearrange("p (n d) -> p n d", d=DH), r3, ALU.mult).then_inc(normed_ready, 1)
                    if lag is not None:
                        norm.dve_norm(dve, lag, TB, 4 * lag + Y_)
                    for i in range(2):
                        dve.wait_ge(n_hi_ready, 2 * c + i + 1)
                        dve.tensor_tensor(n_lo[i][:], A[i][:], n_hi[i][:].bitcast(F32), ALU.subtract).then_inc(n_lo_ready, 1)
                    for j in range(NB):
                        dve.wait_ge(kf_full, NB * c + j + 1)
                        dve.tensor_scalar(k_feat[:, j, :], F[j % 2][:], YAT, YAT, ALU.add, ALU.max).then_inc(kf_ready, 1)
                    if lag is not None:
                        norm.dve_scale(dve, lag)
                        norm.dve_lo(dve, lag, TB, 4 * lag + X_)
                    for i in range(2):
                        dve.wait_ge(kv_full, 2 * c + i + 1)
                        dve.tensor_tensor(kv[:, 2 * i:2 * i + 2, :], tile3(KV[i][:, 0:2 * VW], 2), own[:, 2 * i:2 * i + 2, :],
                                          ALU.mult).then_inc(kv_ready, 1)
                    for i in range(2):
                        o3 = tile3(KV[i][:, 0:2 * VW], 2)
                        dsl, rsl = den[:, 2 * i:2 * i + 2, :], rden[:, 2 * i:2 * i + 2, :]
                        dve.wait_ge(o_full, 2 * c + i + 1)
                        dve.tensor_scalar(dsl, o3[:, :, D:VW], 1e-6, None, ALU.max).then_inc(o_stepped, 1)
                        dve.wait_ge(o_stepped, 4 * c + 2 * i + 1)
                        dve.reciprocal(rsl, dsl).then_inc(o_stepped, 1)
                        dve.wait_ge(o_stepped, 4 * c + 2 * i + 2)
                        a4 = attn[:, i * 2 * P:(i + 1) * 2 * P].rearrange("p (j h d) -> p j h d", j=2, d=DH)
                        dve.tensor_tensor(a4, o3[:, :, 0:D].rearrange("p j (h d) -> p j h d", d=DH),
                                          rsl.unsqueeze(3).broadcast_to([P, 2, HEADS, DH]), ALU.mult).then_inc(attn_ready, 1)

                def tail(c):
                    attn_lower(c)
                    norm.dve_norm(dve, c, TB, 4 * c + Y_)
                    norm.dve_scale(dve, c)
                    norm.dve_lo(dve, c, TB, 4 * c + X_)

                w.dve_split(dve)
                dve.wait_ge(own_loaded, 16)
                lagged(dve, body, tail)


def experts_ffn(nc, net, name, hid, gelu, by_probs, shared, last=False):
    dram = net.dram[name]
    KT = hid // P
    NE = E + shared
    ROUND = 4
    CB = max(2, ROUND // KT)
    UNITS = CB * KT
    TURNS = NC // CB
    EW = 2 * KT * P
    B1, B2 = EW, EW + KT
    G_BIAS = P
    CAP = int(1.25 * NC * CH / E)
    S = NB * E
    with Layer(nc) as ctx:
        sb = lambda n, s, dt=F32: ctx.enter_context(nc.sbuf_tensor(f"{name}_{n}", s, dt))
        ps = lambda n: ctx.enter_context(nc.psum_tensor(f"{name}_{n}", [P, CH], F32))
        sem = lambda n: ctx.sem(f"{name}_{n}")
        norm = Norm(nc, ctx, net, name, last=last)
        gate = Weights(nc, ctx, f"{name}_gate", dram["gate"], P)
        weight_rows = nc.dram_tensor(f"{name}_weight_rows", [NE, NC, NB, P], F32, kind="Internal").ap()
        acc = sb("acc", [P, NC * CH])
        e_raw = [sb(f"e_raw{i}", [P, B2 + 1]) for i in range(2)]
        e_bias = [sb(f"e_bias{i}", [P, KT + 1]) for i in range(2)]
        e_hi = [sb(f"e_hi{i}", [P, EW], F32R) for i in range(2)]
        e_lo = [sb(f"e_lo{i}", [P, EW], F32R) for i in range(2)]
        wt = [sb(f"wt{i}", [P, NC * CH]) for i in range(2)]
        h = [sb(f"h{i}", [P, CH]) for i in range(ROUND)]
        h_hi = [sb(f"h_hi{i}", [P, CH], F32R) for i in range(ROUND)]
        h_lo = [sb(f"h_lo{i}", [P, CH], F32R) for i in range(ROUND)]
        yw = [sb(f"yw{i}", [P, CH]) for i in range(CB)]
        lg_t = sb("lg_t", [P, CH])
        iota8 = sb("iota8", [P, NB, E])
        lg = sb("lg", [P, NB, E])
        top, idx = sb("top", [P, NB, 8]), sb("idx", [P, NB, 8], U32)
        idxf, d2, e2 = sb("idxf", [P, NB, 2]), sb("d2", [P, NB, 2]), sb("e2", [P, NB, 2])
        pr, d8, d8b = sb("pr", [P, NB, E]), sb("d8", [P, NB, E]), sb("d8b", [P, NB, E])
        s1, r1 = sb("s1", [P, NB]), sb("r1", [P, NB])
        w2 = sb("w2", [P, NB, 2])
        oh = [sb(f"oh{i}", [P, NB, E]) for i in range(2)]
        pick = [sb(f"pick{i}", [P, NB, E]) for i in range(2)]
        comb_all = sb("comb_all", [P, NC, S])
        count = sb("count", [P, S])
        count8, keep = sb("count8", [P, E]), sb("keep", [P, E])
        ones = sb("ones", [P, P])
        comb = sb("comb", [P, P])
        comb_t = sb("comb_t", [P, NC, P])
        one_row = sb("one_row", [NC * NB, P])

        H = [ps(f"H{i}") for i in range(ROUND)]
        TY, TX = ps("TY"), ps("TX")
        Y = [ps("Y0"), ps("Y1"), TY, TX]

        made, iota_loaded = sem("made"), sem("iota_loaded")
        lg_full, lg_staged, lg_turned = sem("lg_full"), sem("lg_staged"), sem("lg_turned")
        g_stepped, g_exp, comb_ready, comb_turned, comb_saved = (sem("g_stepped"), sem("g_exp"), sem("comb_ready"),
                                                                 sem("comb_turned"), sem("comb_saved"))
        k_stepped, k_full, rows_out = sem("k_stepped"), sem("k_full"), sem("rows_out")
        e_loaded, wt_loaded = [sem(f"e_loaded{i}") for i in range(2)], [sem(f"wt_loaded{i}") for i in range(2)]
        e_hi_ready, e_ready = sem("e_hi_ready"), sem("e_ready")
        h_full, h_ready, h_hi_ready, h_lo_ready = sem("h_full"), sem("h_ready"), sem("h_hi_ready"), sem("h_lo_ready")
        y_full, yw_ready, acc_ready = sem("y_full"), sem("yw_ready"), sem("acc_ready")

        STEPS = 15 if by_probs else 10

        def experts(eng, body):
            with eng.Fori(0, E // 2) as q:
                for i in range(2):
                    body(2 * q + i, i)
            if shared:
                body(E, 0)

        with nc.Block() as block:
            @block.sync
            def _(sp):
                gate.sp_load(sp)
                sp.dma_start(iota8[:], dram["iota8"]).then_inc(iota_loaded, 16)
                sp.wait_ge(comb_saved, NC)
                sp.wait_ge(made, 6)
                for j in range(NB):
                    sp.dma_start(weight_rows[0:E, :, j, :], comb_t[j * E:(j + 1) * E, :, :]).then_inc(rows_out, 16)
                if shared:
                    sp.dma_start(weight_rows[E].rearrange("c j p -> (c j) p"), one_row[:]).then_inc(rows_out, 16)
                sp.wait_ge(rows_out, 16 * (NB + shared))

                def load(e, i):
                    src = dram["w"][bass.ds(e, 1)].rearrange("a p n -> p (a n)")
                    row = weight_rows[bass.ds(e, 1)].rearrange("a c j p -> a (c j p)")
                    wait(sp, e_ready, e - 1)
                    sp.dma_start(e_raw[i][:], src).then_inc(e_loaded[i], 16)
                    wait(sp, yw_ready, 1 + (e - 1) * NC)
                    sp.dma_start(wt[i][:], row.broadcast_to([P, NC * CH])).then_inc(wt_loaded[i], 16)

                load(0, 0)
                load(1, 1)
                with sp.Fori(1, E // 2) as q:
                    for i in range(2):
                        load(2 * q + i, i)
                if shared:
                    load(E, 0)
                with sp.Fori(0, NC) as c:
                    norm.sp_save(sp, c)
                norm.sp_end(sp)

            @block.gpsimd
            def _(pool):
                pool.memset(comb[:], 0.0).then_inc(made, 1)
                pool.memset(count[:], 0.0).then_inc(made, 1)
                pool.memset(ones[:], 1.0).then_inc(made, 1)
                pool.memset(one_row[:], 1.0).then_inc(made, 1)
                pool.memset(acc[:, 0:NC * CH // 2], 0.0).then_inc(made, 1)
                pool.memset(acc[:, NC * CH // 2:], 0.0).then_inc(made, 1)
                pool.sem_inc(acc_ready, 1)
                pool.wait_ge(made, 6)

                def split(e, i, turn):
                    pool.wait_ge(e_loaded[i], 16 * turn + 16)
                    wait(pool, yw_ready, 1 + (e - 1) * NC)
                    settle(pool, net)
                    pool.tensor_copy(e_hi[i][:], e_raw[i][:, 0:EW])
                    pool.tensor_copy(e_bias[i][:], e_raw[i][:, EW:B2 + 1]).then_inc(e_hi_ready, 1)
                    pool.wait_ge(e_hi_ready, e + 1)
                    pool.tensor_tensor(e_lo[i][:], e_raw[i][:, 0:EW], e_hi[i][:].bitcast(F32),
                                       ALU.subtract).then_inc(e_ready, 1)

                def gather(e):
                    with pool.Fori(0, TURNS) as b:
                        for k in range(CB):
                            c = b * CB + k
                            pool.wait_ge(yw_ready, 1 + e * NC + c + 1)
                            pool.tensor_tensor(acc[:, at(c)], acc[:, at(c)], yw[k][:], ALU.add).then_inc(acc_ready, 1)

                split(0, 0, 0)
                split(1, 1, 0)
                gather(0)
                with pool.Fori(1, E // 2) as q:
                    split(2 * q, 0, q)
                    gather(2 * q - 1)
                    split(2 * q + 1, 1, q)
                    gather(2 * q)
                if shared:
                    split(E, 0, E // 2)
                gather(E - 1)
                if shared:
                    gather(E)
                each(pool, lambda c: norm.pool_root(pool, c))

            @block.tensor
            def _(pe):
                def turn_weights(c):
                    pe.wait_ge(comb_ready, c + 1)
                    wait(pe, comb_saved, c)
                    pe.transpose(Y[0][:, 0:P], comb[:], net.ident[:]).then_inc(comb_turned, 1)

                def gates(c, lag):
                    wait(pe, lg_staged, c)
                    product3(pe, TY[:], gate.hi[:], gate.lo[:], net.x_hi[:, at(c)], net.x_lo[:, at(c)]
                             ).then_inc(lg_full, 1)
                    if lag is not None and not by_probs:
                        turn_weights(lag)
                    pe.wait_ge(lg_staged, c + 1)
                    if lag is not None:
                        pe.wait_ge(g_stepped, STEPS * lag + 1)
                    for j in range(NB):
                        mm = pe.transpose(TX[:, j * P:(j + 1) * P], lg_t[:, j * P:(j + 1) * P], net.ident[:])
                    mm.then_inc(lg_turned, 1)

                def expert(e, i):
                    pe.wait_ge(e_ready, e + 1)
                    settle(pe, net)
                    w_up, w_down = (e_hi[i], e_lo[i]), KT * P
                    with pe.Fori(0, TURNS) as b:
                        for rnd in range(UNITS // ROUND):
                            for r in range(ROUND):
                                u = rnd * ROUND + r
                                c, t = b * CB + u // KT, u % KT
                                sl = slice(t * P, (t + 1) * P)
                                product3(pe, H[r][:], e_hi[i][:, sl], e_lo[i][:, sl],
                                         net.x_hi[:, at(c)], net.x_lo[:, at(c)]).then_inc(h_full, 1)
                            for r in range(ROUND):
                                u = rnd * ROUND + r
                                k, t = u // KT, u % KT
                                if u == 0:
                                    pe.wait_ge(yw_ready, 1 + e * NC + b * CB)
                                pe.wait_ge(h_lo_ready, (e * NC + b * CB) * KT + u + 1)
                                sl = slice(w_down + t * P, w_down + (t + 1) * P)
                                mm = product3(pe, Y[k][:], e_hi[i][:, sl], e_lo[i][:, sl], h_hi[r][:], h_lo[r][:],
                                              start=t == 0, stop=t == KT - 1)
                                if t == KT - 1:
                                    mm.then_inc(y_full, 1)

                pe.wait_ge(gate.lo_ready, 1)
                pe.wait_ge(made, 6)
                lagged(pe, gates, turn_weights if not by_probs else lambda c: None)
                if by_probs:
                    pe.wait_ge(k_stepped, 1)
                    pe.matmul(Y[1][:, 0:E], ones[:], count8[:], start=True, stop=True).then_inc(k_full, 1)
                    each(pe, turn_weights)
                pe.wait_ge(comb_saved, NC)
                pe.wait_ge(g_stepped, STEPS * NC)
                experts(pe, expert)
                pe.wait_ge(yw_ready, 1 + NE * NC)

                def step(c, lag):
                    norm.pe_turn_y(pe, c, TY)
                    if lag is not None and not last:
                        norm.pe_turn_x(pe, lag, TX)
                lagged(pe, step, lambda c: None if last else norm.pe_turn_x(pe, c, TX))

            @block.scalar
            def _(act):
                def save_weights(c):
                    act.wait_ge(comb_turned, c + 1)
                    act.activation(comb_t[:, c, :], Y[0][:, 0:P], ACT.Copy).then_inc(comb_saved, 1)

                def gates(c, lag):
                    act.wait_ge(lg_full, c + 1)
                    wait(act, lg_turned, c)
                    act.activation(lg_t[:], TY[:], ACT.Identity, bias=gate.raw[:, G_BIAS:G_BIAS + 1]).then_inc(lg_staged, 1)
                    if lag is not None and not by_probs:
                        save_weights(lag)
                    if by_probs:
                        act.wait_ge(g_stepped, STEPS * c + 3)
                        act.activation(pr[:], d8[:], ACT.Exp).then_inc(g_exp, 1)
                    else:
                        act.wait_ge(g_stepped, STEPS * c + 4)
                        act.activation(e2[:, :, 0], d2[:, :, 0], ACT.Exp).then_inc(g_exp, 1)

                def expert(e, i):
                    func = ACT.Gelu if gelu else ACT.Relu
                    act.wait_ge(e_ready, e + 1)
                    with act.Fori(0, TURNS) as b:
                        for u in range(UNITS):
                            r, t = u % ROUND, u % KT
                            act.wait_ge(h_full, (e * NC + b * CB) * KT + u + 1)
                            act.activation(h[r][:], H[r][:], func, bias=e_bias[i][:, t:t + 1])
                            act.activation(h_hi[r][:], H[r][:], func, bias=e_bias[i][:, t:t + 1]).then_inc(h_hi_ready, 1)

                gate.act_split(act)
                act.activation(net.spare[:], gate.raw[:, 0:NB], ACT.Exp)
                lagged(act, gates, save_weights if not by_probs else lambda c: None)
                if by_probs:
                    with act.Fori(0, NC) as c:
                        save_weights(c)
                if gelu:
                    act.activation(net.spare[:, 0:1], gate.raw[:, 0:1], ACT.Gelu)
                experts(act, expert)
                act.wait_ge(acc_ready, 1 + NE * NC)

                def step(c, lag):
                    wait(act, norm.y_turned, c)
                    act.activation(net.y_stage[:], acc[:, at(c)], ACT.Copy).then_inc(norm.y_staged, 1)
                    if lag is not None and not last:
                        norm.act_hi(act, lag, TX)
                lagged(act, step, lambda c: None if last else norm.act_hi(act, c, TX))

            @block.vector
            def _(dve):
                def bc(ap):
                    return ap.unsqueeze(2).broadcast_to([P, NB, E])

                def gates(c, lag):
                    k = [0]

                    def link(ins):
                        k[0] += 1
                        ins.then_inc(g_stepped, 1)
                        dve.wait_ge(g_stepped, STEPS * c + k[0])
                        settle(dve, net)

                    dve.wait_ge(lg_turned, c + 1)
                    link(dve.tensor_copy(lg[:], tile3(TX[:])[:, :, 0:E]))
                    for j in range(NB):
                        ins = dve.max(top[:, j, :], lg[:, j, :])
                    link(ins)
                    if by_probs:
                        wait(dve, g_exp, c)
                        link(dve.tensor_tensor(d8[:], lg[:], bc(top[:, :, 0]), ALU.subtract))
                        dve.wait_ge(g_exp, c + 1)
                        link(dve.tensor_reduce(s1[:], pr[:], AX.X, ALU.add))
                        link(dve.reciprocal(r1[:], s1[:]))
                        link(dve.tensor_tensor(lg[:], pr[:], bc(r1[:]), ALU.mult))
                        for j in range(NB):
                            ins = dve.max(top[:, j, :], lg[:, j, :])
                        link(ins)
                    for j in range(NB):
                        ins = dve.max_index(idx[:, j, :], top[:, j, :], lg[:, j, :])
                    link(ins)
                    dve.tensor_copy(idxf[:], idx[:, :, 0:2])
                    if not by_probs:
                        wait(dve, g_exp, c)
                    link(dve.tensor_tensor(d2[:, :, 0], top[:, :, 1], top[:, :, 0], ALU.subtract))
                    for i in range(2):
                        ins = dve.tensor_tensor(oh[i][:], iota8[:], bc(idxf[:, :, i]), ALU.is_equal)
                    link(ins)
                    if by_probs:
                        w_first, w_second = top[:, :, 0], top[:, :, 1]
                    else:
                        dve.wait_ge(g_exp, c + 1)
                        link(dve.tensor_scalar(s1[:], e2[:, :, 0], 1.0, None, ALU.add))
                        link(dve.reciprocal(w2[:, :, 0], s1[:]))
                        link(dve.tensor_tensor(w2[:, :, 1], e2[:, :, 0], w2[:, :, 0], ALU.mult))
                        w_first, w_second = w2[:, :, 0], w2[:, :, 1]
                    dve.tensor_tensor(pick[0][:], oh[0][:], bc(w_first), ALU.mult)
                    link(dve.tensor_tensor(pick[1][:], oh[1][:], bc(w_second), ALU.mult))
                    if by_probs:
                        link(dve.tensor_tensor(comb_all[:, c, :].rearrange("p (j e) -> p j e", e=E), pick[0][:], pick[1][:], ALU.add))
                        link(dve.tensor_tensor(d8b[:], oh[0][:], oh[1][:], ALU.add))
                        link(dve.tensor_tensor(count[:], count[:], d8b[:].rearrange("p j e -> p (j e)"), ALU.add))
                        link(dve.nop())
                    else:
                        wait(dve, comb_turned, c)
                        dve.tensor_tensor(comb[:, 0:S].rearrange("p (j e) -> p j e", e=E), pick[0][:], pick[1][:],
                                          ALU.add).then_inc(comb_ready, 1)
                        dve.wait_ge(comb_ready, c + 1)
                        link(dve.nop())
                    assert k[0] == STEPS

                def expert(e, i):
                    with dve.Fori(0, TURNS) as b:
                        for rnd in range(UNITS // ROUND):
                            for r in range(ROUND):
                                dve.wait_ge(h_hi_ready, (e * NC + b * CB) * KT + rnd * ROUND + r + 1)
                                dve.tensor_tensor(h_lo[r][:], h[r][:], h_hi[r][:].bitcast(F32),
                                                  ALU.subtract).then_inc(h_lo_ready, 1)
                            for k in range(rnd * ROUND // KT, (rnd + 1) * ROUND // KT):
                                if k == 0:
                                    dve.wait_ge(acc_ready, 1 + e * NC + b * CB)
                                c = b * CB + k
                                dve.wait_ge(y_full, e * NC + c + 1)
                                dve.scalar_tensor_tensor(out=yw[k][:], in0=Y[k][:], scalar=e_bias[i][:, KT:KT + 1],
                                                         in1=wt[i][:, at(c)], op0=ALU.add, op1=ALU.mult).then_inc(yw_ready, 1)

                def expert_of_pair(q):
                    for i in range(2):
                        dve.wait_ge(wt_loaded[i], 16 * q + 16)
                        settle(dve, net)
                        expert(2 * q + i, i)

                dve.sem_inc(yw_ready, 1)
                gate.dve_split(dve)
                dve.wait_ge(made, 6)
                dve.wait_ge(iota_loaded, 16)
                lagged(dve, gates, lambda c: None)
                if by_probs:
                    dve.tensor_reduce(count8[:], count[:].rearrange("p (j e) -> p e j", e=E), AX.X, ALU.add).then_inc(k_stepped, 1)
                    dve.wait_ge(k_full, 1)
                    dve.tensor_scalar(keep[:], Y[1][:, 0:E], float(CAP), None, ALU.is_le).then_inc(k_stepped, 1)
                    dve.wait_ge(k_stepped, 2)

                    def weigh(c):
                        wait(dve, comb_turned, c)
                        dve.tensor_tensor(comb[:, 0:S].rearrange("p (j e) -> p j e", e=E),
                                          comb_all[:, c, :].rearrange("p (j e) -> p j e", e=E),
                                          keep[:].unsqueeze(1).broadcast_to([P, NB, E]), ALU.mult).then_inc(comb_ready, 1)
                    each(dve, weigh)
                with dve.Fori(0, E // 2) as q:
                    expert_of_pair(q)
                if shared:
                    dve.wait_ge(wt_loaded[0], 16 * (E // 2) + 16)
                    expert(E, 0)

                def step(c, lag):
                    norm.dve_norm(dve, c, TY)
                    norm.dve_scale(dve, c)
                    if lag is not None and not last:
                        norm.dve_lo(dve, lag, TX)
                lagged(dve, step, lambda c: None if last else norm.dve_lo(dve, c, TX))


def steps(nc, net):
    return [
        lambda: softmax_attention(nc, net, "L0_attn", True),
        lambda: experts_ffn(nc, net, "L0_ffn", P, False, True, 0),
        lambda: gated_recurrence(nc, net),
        lambda: ternary_ffn(nc, net),
        lambda: softmax_attention(nc, net, "L2_attn", False),
        lambda: experts_ffn(nc, net, "L2_ffn", HID, False, False, 0),
        lambda: linear_attention(nc, net),
        lambda: experts_ffn(nc, net, "L3_ffn", HID, True, False, 1, last=True),
    ]


def program(nc, dram):
    with Layer(nc) as ctx:
        net = Net(nc, ctx, dram)
        enter(nc, net)
        for layer in steps(nc, net):
            layer()


def layout(inputs):
    import numpy as np
    a = {k: np.asarray(v) for k, v in inputs.items()}
    f = np.float32
    out = {"x": np.ascontiguousarray(a["L0_attn_x"])}

    def column(v):
        return v.reshape(-1, P).T

    def stacked(wt, lower):
        s = np.zeros((wt.shape[0], GROUPS, GH, QUAD), f)
        v = wt.reshape(wt.shape[0], GROUPS, GH, DH)
        for i in range(3):
            s[:, :, :, i * DH:(i + 1) * DH] = v
        return s.reshape(wt.shape[0], GROUPS * P)

    def softmax_weights(pre, bias, scale):
        w = np.zeros((P, 2 * GROUPS * P + 2 * P + 11), f)
        w[:, 0:GROUPS * P] = stacked(a[pre + "Wq"].T, True)
        w[:, GROUPS * P:2 * GROUPS * P] = stacked(a[pre + "Wk"].T, False)
        w[:, 2 * GROUPS * P:2 * GROUPS * P + P] = a[pre + "Wv"].T
        w[:, 2 * GROUPS * P + P:2 * GROUPS * P + 2 * P] = a[pre + "Wo"].T
        b = 2 * GROUPS * P + 2 * P
        if bias:
            w[:, b:b + 4] = stacked(a[pre + "bq"][None, :], True).reshape(GROUPS, P).T
            w[:, b + 4:b + 8] = stacked(a[pre + "bk"][None, :], False).reshape(GROUPS, P).T
            w[:, b + 8] = a[pre + "bv"]
            w[:, b + 9] = a[pre + "bo"]
            w[:, b + 10] = a[pre + "attn_scale"][0]
        else:
            w[:, b + 10] = f(1.0) / np.sqrt(f(DH))
        for r in range(GH):
            w[QUAD * r + R_MAX:QUAD * r + K_MAX, b + 4:b + 8] = 1.0
        return w

    out["L0_attn_w"] = softmax_weights("L0_attn_", False, None)
    out["L2_attn_w"] = softmax_weights("L2_attn_", True, None)
    out["L1_attn_w"] = np.concatenate([a["L1_attn_W_in"], a["L1_attn_W_out"], column(a["L1_attn_b_in"]),
                                       column(a["L1_attn_b_out"])], axis=1)

    def tiles(wt):
        return wt.reshape(-1, P, wt.shape[1]).transpose(1, 0, 2).reshape(P, -1)

    out["L1_ffn_w"] = np.concatenate([a["L1_ffn_w1_w"].T, a["L1_ffn_w2_w"].T, tiles(a["L1_ffn_h1_w"].T),
                                      tiles(a["L1_ffn_h2_w"].T), tiles(a["L1_ffn_w3_w"].T)], axis=1)
    out["L1_ffn_scales"] = np.concatenate([column(a["L1_ffn_" + k]) for k in ("w1_s", "w2_s", "h1_s", "h2_s", "w3_s")], axis=1)
    block = np.zeros((HEADS, DH, HEADS, QUAD), f)
    for h in range(HEADS):
        block[h, :, h, :] = a["L3_attn_projection"][h].T
    out["L3_attn_w"] = np.concatenate([a["L3_attn_Wq"], a["L3_attn_Wk"], a["L3_attn_Wv"], a["L3_attn_Wo"],
                                       block.reshape(P, HEADS * QUAD)] +
                                      [column(a["L3_attn_" + k]) for k in ("bq", "bk", "bv", "bo")], axis=1)

    def gate(wt, b):
        g = np.zeros((P, P + 1), f)
        g[:, 0:E] = wt
        if b is not None:
            g[0:E, P] = b
        return g

    def experts(w1, b1, w2, b2):
        return np.concatenate([w1, np.stack([tiles(m) for m in w2]), b1.reshape(len(w1), -1, P).transpose(0, 2, 1),
                               b2.reshape(len(w1), P, 1)], axis=2)

    out["L0_ffn_gate"] = gate(a["L0_ffn_gate_w"].T, None)
    out["L0_ffn_w"] = experts(*[a["L0_ffn_" + k] for k in ("W1", "b1", "W2", "b2")])
    out["L2_ffn_gate"] = gate(a["L2_ffn_W_router"], a["L2_ffn_b_router"])
    out["L2_ffn_w"] = experts(*[a["L2_ffn_" + k] for k in ("W1", "b1", "W2", "b2")])
    out["L3_ffn_gate"] = gate(a["L3_ffn_gate_w"], a["L3_ffn_gate_b"])
    out["L3_ffn_w"] = np.concatenate(
        [experts(*[a["L3_ffn_" + k] for k in ("w1", "b1", "w2", "b2")]),
         experts(a["L3_ffn_ws1"][None], a["L3_ffn_bs1"][None], a["L3_ffn_ws2"][None], a["L3_ffn_bs2"][None])], axis=0)

    bf16 = mybir.dt.np(BF16)
    q, k = np.arange(P)[:, None], np.arange(P)[None, :]
    window = [np.where(ok, 0.0, NEG) for ok in (k <= q, k > q)]
    half = P // 2
    chunked = [np.where(((k // half == q // half) & (k <= q)) | (k // half > q // half), 0.0, NEG)] * 2
    for name, m in (("L0_attn_masks", window), ("L2_attn_masks", chunked)):
        out[name] = np.stack([m[0], m[1], m[0].T, m[1].T], axis=1).astype(bf16)
    out["ident"] = np.eye(P, dtype=f)
    out["ident16"] = np.eye(P).astype(bf16)
    c = np.zeros((P, 4), f)
    row = np.arange(P) % QUAD
    c[:, 0] = np.where((row >= DH) & (row < 2 * DH), -1.0, 0.0)
    c[:, 1] = np.where((row >= 2 * DH) & (row < 3 * DH), -1.0, 0.0)
    out["const"] = c
    iota = np.broadcast_to(np.arange(E, dtype=f), (P, NB, E)).copy()
    for name in ("L0_ffn_iota8", "L2_ffn_iota8", "L3_ffn_iota8"):
        out[name] = iota
    own = np.zeros((P, GROUPS, D + HEADS), f)
    for g in range(GROUPS):
        for p in range(P):
            h = GH * g + p // QUAD
            own[p, g, h * DH:(h + 1) * DH] = 1.0
            own[p, g, D + h] = 1.0
    out["L3_attn_own"] = own
    return {n: np.ascontiguousarray(v) for n, v in out.items()}


def build(nc, inputs):
    arrays, dram = {}, {}
    for name, v in layout(inputs).items():
        arrays[f"in_{name}"] = v
        ap = nc.dram_tensor(f"in_{name}", v.shape, mybir.dt.from_np(v.dtype), kind="ExternalInput").ap()
        if name[0] == "L":
            layer, part = name[:name.rindex("_")], name[name.rindex("_") + 1:]
            dram.setdefault(layer, {})[part] = ap
        else:
            dram[name] = ap
    dram["out"] = nc.dram_tensor("out_x", (BATCH, SEQ, D), F32, kind="ExternalOutput").ap()
    program(nc, dram)
    return arrays


def kernel(**inputs):
    import concourse.bacc as bacc
    from concourse.bass_utils import run_bass_kernel_spmd
    nc = bacc.Bacc("TRN2", target_bir_lowering=False, num_devices=1)
    arrays = build(nc, inputs)
    r = run_bass_kernel_spmd(nc, [arrays], core_ids=[0])
    return r.results[0]["out_x"]
```

```python
from contextlib import ExitStack

import concourse.bass as bass
from concourse import mybir
from concourse.alu_op_type import AluOpType as ALU

F32 = mybir.dt.float32
F32R = mybir.dt.float32r
BF16 = mybir.dt.bfloat16
U32 = mybir.dt.uint32
ACT = mybir.ActivationFunctionType
AX = mybir.AxisListType

P = 128
D = 128
BATCH = 8
SEQ = 512
NC = BATCH
CH = SEQ
NB = CH // P
HEADS = 16
DH = D // HEADS
GROUPS = 4
GH = HEADS // GROUPS
QUAD = 32
E = 8
HID = 512
NEG = -1.0e30
EPS = 1e-5
R_MAX = 3 * DH
K_MAX = 3 * DH + 3


def wait(eng, sem, count):
    if isinstance(count, int) and count <= 0:
        return
    eng.wait_ge(sem, count)


def settle(eng, net):
    eng.sem_inc(net.settled, 1)


def at(c):
    return bass.ds(c * CH, CH)


def tile3(ap, n=NB):
    return ap.rearrange("p (j d) -> p j d", j=n)


class Layer(ExitStack):

    def __init__(self, nc):
        super().__init__()
        self.nc, self.sems = nc, []

    def sem(self, name):
        self.sems.append(self.nc.alloc_semaphore(name=name))
        return self.sems[-1]

    def __exit__(self, *failure):
        super().__exit__(*failure)
        self.nc.clear_and_free_semaphores(self.sems)
        self.nc.all_engine_barrier()


class Net:

    def __init__(self, nc, ctx, dram):
        self.nc, self.dram = nc, dram

        def sb(name, shape, dt=F32):
            return ctx.enter_context(nc.sbuf_tensor(name, shape, dt))

        self.settled = ctx.sem("settled")
        self.x_tok = sb("x_tok", [P, NC, CH])
        self.x_hi = sb("x_hi", [P, NC * CH], F32R)
        self.x_lo = sb("x_lo", [P, NC * CH], F32R)
        self.y_stage = sb("y_stage", [P, CH])
        self.res = sb("res", [P, CH])
        self.x_new = sb("x_new", [P, CH])
        self.stats = sb("stats", [P, NB, 6])
        self.mv = sb("mv", [P, NB, 2])
        self.ve = sb("ve", [P, NB])
        self.rstd = sb("rstd", [P, NB])
        self.m_half = sb("m_half", [P, NB])
        self.spare = sb("spare", [P, NB])
        self.ident = sb("ident", [P, P])
        self.ident16 = sb("ident16", [P, P], BF16)
        self.const = sb("const", [P, 4])


class Norm:

    STEPS = 3

    def __init__(self, nc, ctx, net, name, last=False, shared=None):
        self.nc, self.net, self.last, self.shared = nc, net, last, shared

        def sem(n):
            return ctx.sem(f"{name}_{n}")

        self.y_staged = sem("y_staged")
        self.y_turned = sem("y_turned")
        self.y_added = sem("y_added")
        self.stepped = sem("stepped")
        self.rstd_ready = sem("rstd_ready")
        self.xn_ready = sem("xn_ready")
        self.xn_turned = sem("xn_turned")
        self.hi_ready = sem("hi_ready")
        self.lo_ready = sem("lo_ready")
        self.x_saved = sem("x_saved")

    def turn(self, pe, src, bank):
        for j in range(NB):
            mm = pe.transpose(bank[:, j * P:(j + 1) * P], src[:, j * P:(j + 1) * P], self.net.ident[:])
        return mm

    def pe_turn_y(self, pe, c, bank, n=None):
        if n is None:
            pe.wait_ge(self.y_staged, c + 1)
            wait(pe, self.y_added, c)
            self.turn(pe, self.net.y_stage, bank).then_inc(self.y_turned, 1)
        else:
            full, free = self.shared
            pe.wait_ge(free, n)
            self.turn(pe, self.net.y_stage, bank).then_inc(full, 1)

    def dve_norm(self, dve, c, bank, n=None):
        net = self.net
        wait(dve, self.xn_ready, c)
        if n is None:
            dve.wait_ge(self.y_turned, c + 1)
            dve.tensor_tensor(net.res[:], bank[:], net.x_tok[:, c, :], ALU.add).then_inc(self.y_added, 1)
            dve.wait_ge(self.y_added, c + 1)
        else:
            full, free = self.shared
            dve.wait_ge(full, n + 1)
            dve.tensor_tensor(net.res[:], bank[:], net.x_tok[:, c, :], ALU.add).then_inc(free, 1)
            dve.wait_ge(free, n + 1)
        for j in range(NB):
            last = dve.bn_stats(net.stats[:, j, :], net.res[:, j * P:(j + 1) * P])
        last.then_inc(self.stepped, 1)
        dve.wait_ge(self.stepped, self.STEPS * c + 1)
        settle(dve, net)
        for j in range(NB):
            last = dve.bn_aggr(net.mv[:, j, :], net.stats[:, j, :])
        last.then_inc(self.stepped, 1)
        dve.wait_ge(self.stepped, self.STEPS * c + 2)
        wait(dve, self.rstd_ready, c)
        dve.tensor_scalar(net.ve[:], net.mv[:, :, 1], EPS, None, ALU.add).then_inc(self.stepped, 1)

    def pool_root(self, pool, c):
        net = self.net
        pool.wait_ge(self.stepped, self.STEPS * (c + 1))
        wait(pool, self.xn_ready, c)
        pool.tensor_tensor(net.rstd[:], net.ve[:], net.m_half[:, 0:NB], ALU.pow).then_inc(self.rstd_ready, 1)

    def dve_scale(self, dve, c):
        net = self.net
        dve.wait_ge(self.rstd_ready, c + 1)
        wait(dve, self.x_saved, 16 * c)
        if not self.last and self.shared is None:
            wait(dve, self.xn_turned, c)
        for j in range(NB):
            sl = slice(j * P, (j + 1) * P)
            last = dve.tensor_scalar(net.x_new[:, sl], net.res[:, sl], net.mv[:, j, 0:1], net.rstd[:, j:j + 1],
                                     ALU.subtract, ALU.mult)
        last.then_inc(self.xn_ready, 1)

    def pe_turn_x(self, pe, c, bank, n=None):
        pe.wait_ge(self.xn_ready, c + 1)
        if n is None:
            wait(pe, self.lo_ready, c)
            self.turn(pe, self.net.x_new, bank).then_inc(self.xn_turned, 1)
        else:
            full, free = self.shared
            pe.wait_ge(free, n)
            self.turn(pe, self.net.x_new, bank).then_inc(full, 1)

    def act_hi(self, act, c, bank, n=None):
        if n is None:
            act.wait_ge(self.xn_turned, c + 1)
        else:
            act.wait_ge(self.shared[0], n + 1)
        act.activation(self.net.x_hi[:, at(c)], bank[:], ACT.Copy).then_inc(self.hi_ready, 1)

    def dve_lo(self, dve, c, bank, n=None):
        net = self.net
        dve.wait_ge(self.hi_ready, c + 1)
        dve.tensor_tensor(net.x_lo[:, at(c)], bank[:], net.x_hi[:, at(c)].bitcast(F32),
                          ALU.subtract).then_inc(self.lo_ready if n is None else self.shared[1], 1)

    def sp_save(self, sp, c):
        net = self.net
        sp.wait_ge(self.xn_ready, c + 1)
        if self.last:
            dst = net.dram["out"][bass.ds(c, 1)].rearrange("a (j p) d -> p (a j) d", p=P)
            sp.dma_start(dst, tile3(net.x_new[:])).then_inc(self.x_saved, 16)
        else:
            sp.dma_start(net.x_tok[:, bass.ds(c, 1), :], net.x_new[:].rearrange("p (a n) -> p a n", a=1)
                         ).then_inc(self.x_saved, 16)

    def sp_end(self, sp):
        sp.wait_ge(self.x_saved, 16 * NC)


class Weights:

    def __init__(self, nc, ctx, name, dram, width):
        self.dram, self.width = dram, width
        self.raw = ctx.enter_context(nc.sbuf_tensor(f"{name}_w_raw", [P, dram.shape[1]], F32))
        self.hi = ctx.enter_context(nc.sbuf_tensor(f"{name}_w_hi", [P, width], F32R))
        self.lo = ctx.enter_context(nc.sbuf_tensor(f"{name}_w_lo", [P, width], F32R))
        self.loaded = ctx.sem(f"{name}_w_loaded")
        self.hi_ready = ctx.sem(f"{name}_w_hi_ready")
        self.lo_ready = ctx.sem(f"{name}_w_lo_ready")

    def sp_load(self, sp):
        sp.dma_start(self.raw[:], self.dram).then_inc(self.loaded, 16)

    def act_split(self, act):
        act.wait_ge(self.loaded, 16)
        act.activation(self.hi[:], self.raw[:, 0:self.width], ACT.Copy).then_inc(self.hi_ready, 1)

    def dve_split(self, dve):
        dve.wait_ge(self.hi_ready, 1)
        dve.tensor_tensor(self.lo[:], self.raw[:, 0:self.width], self.hi[:].bitcast(F32),
                          ALU.subtract).then_inc(self.lo_ready, 1)


def product3(pe, out, w_hi, w_lo, x_hi, x_lo, start=True, stop=True):
    pe.matmul(out, w_hi, x_hi, start=start, stop=False)
    pe.matmul(out, w_hi, x_lo, start=False, stop=False)
    return pe.matmul(out, w_lo, x_hi, start=False, stop=stop)


def lagged(eng, body, tail):
    body(0, None)
    with eng.Fori(1, NC) as c:
        body(c, c - 1)
    tail(NC - 1)


def each(eng, body):
    body(0)
    with eng.Fori(1, NC) as c:
        body(c)


def enter(nc, net):
    with Layer(nc) as ctx:
        sem = lambda n: ctx.sem(f"in_{n}")
        bank = ctx.enter_context(nc.psum_tensor("in_bank", [P, CH], F32))
        x_loaded = [sem(f"x_loaded{c}") for c in range(NC)]
        const_loaded, made = sem("const_loaded"), sem("made")
        staged, turned, hi_ready, lo_ready = sem("staged"), sem("turned"), sem("hi_ready"), sem("lo_ready")
        with nc.Block() as block:
            @block.sync
            def _(sp):
                sp.dma_start(net.ident[:], net.dram["ident"]).then_inc(const_loaded, 16)
                sp.dma_start(net.ident16[:], net.dram["ident16"]).then_inc(const_loaded, 16)
                sp.dma_start(net.const[:], net.dram["const"]).then_inc(const_loaded, 16)
                for c in range(NC):
                    sp.dma_start(tile3(net.x_tok[:, c, :]),
                                 net.dram["x"][c].rearrange("(j p) d -> p j d", p=P)).then_inc(x_loaded[c], 16)

            @block.gpsimd
            def _(pool):
                pool.memset(net.m_half[:], -0.5).then_inc(made, 1)

            @block.tensor
            def _(pe):
                pe.wait_ge(const_loaded, 48)
                for c in range(NC):
                    pe.wait_ge(x_loaded[c], 16)
                    wait(pe, lo_ready, c)
                    for j in range(NB):
                        mm = pe.transpose(bank[:, j * P:(j + 1) * P], net.x_tok[:, c, j * P:(j + 1) * P], net.ident[:])
                    mm.then_inc(turned, 1)

            @block.scalar
            def _(act):
                act.wait_ge(const_loaded, 48)
                act.activation(net.spare[:, 0:1], net.ident[:, 0:1], ACT.Copy)
                with act.Fori(0, NC) as c:
                    act.wait_ge(turned, c + 1)
                    act.activation(net.x_hi[:, at(c)], bank[:], ACT.Copy).then_inc(hi_ready, 1)

            @block.vector
            def _(dve):
                with dve.Fori(0, NC) as c:
                    dve.wait_ge(hi_ready, c + 1)
                    dve.tensor_tensor(net.x_lo[:, at(c)], bank[:], net.x_hi[:, at(c)].bitcast(F32),
                                      ALU.subtract).then_inc(lo_ready, 1)


def softmax_attention(nc, net, name, windowed):
    dram = net.dram[name]
    WQ, WK, WV, WO = 0, GROUPS * P, 2 * GROUPS * P, 2 * GROUPS * P + P
    WIDTH = WO + P
    BIAS = WIDTH
    if windowed:
        max_slots = [[(0, 0, 2, 0, 0, 1, [(0, 0)]), (1, 0, 2, 256, 0, 2, [(1, 256), (0, 384)])],
                     [(2, 1, 2, 0, 1, 2, [(1, 0), (0, 128)]), (3, 2, 2, 256, 2, 2, [(1, 256), (0, 384)])]]
        exp_slots = [[(0, 0, 2, 0, 0, 2, [(0, 0), (1, 128)]), (1, 1, 2, 256, 1, 2, [(0, 256), (1, 384)])],
                     [(3, 2, 2, 0, 3, 1, [(0, 128)]), (2, 2, 2, 256, 2, 2, [(0, 256), (1, 384)])]]
    else:
        max_slots = [[(0, 0, 4, 0, 0, 4, [(0, 0)])],
                     [(1, 1, 3, 0, 1, 3, [(0, 0)])],
                     [(2, 2, 2, 0, 2, 2, [(0, 0)]), (3, 2, 2, 256, 3, 1, [(0, 384)])]]
        exp_slots = [[(3, 0, 4, 0, 0, 4, [(0, 384)])],
                     [(2, 0, 3, 0, 0, 3, [(0, 256)])],
                     [(1, 0, 2, 0, 0, 2, [(0, 128)]), (0, 0, 2, 256, 0, 1, [(0, 256)])]]
    SLOTS = len(exp_slots)
    N = SLOTS * GH
    NP = 8
    NSE = 3
    NV = N // GH
    AT_PV = 1
    AT_Q, AT_K, AT_O, AT_END = 0, 2, 3, N - 1

    def ahead(s):
        return min(N, s + 2 + (s >= N // 2))

    EVENTS = {
        "A": dict(before=["V", "Q0", "K0", "Q1", "K1"],
                  body=["Q2", "K2", "Q3", "K3", "WO", "Q0", "K0", "V", "Q1", "K1"],
                  lag=["WO"], new=["Q0", "K0", "V", "Q1", "K1"], after=["WO"]),
        "B": dict(before=["VT", "T0"],
                  body=["O3", "T1", "AT", "O0", "T2", "Y", "O1", "T3", "X", "O2", "T0", "VT"],
                  lag=["O3", "AT", "Y", "X"], new=["T0", "VT"], after=["O3", "AT", "Y", "X"]),
    }

    def nth(bank, e, c):
        ev = EVENTS[bank]
        first = [x for x in ev["body"] if x not in ev["lag"]]
        if isinstance(c, int) and c == -1:
            return ev["before"].index(e)
        if isinstance(c, int) and c == 0:
            return len(ev["before"]) + first.index(e)
        done = len(ev["before"]) + len(first) + (c - 1) * len(ev["body"])
        if isinstance(c, int) and c == NC - 1:
            return done + [x for x in ev["body"] if x not in ev["new"]].index(e)
        if isinstance(c, int) and c == NC:
            return done - len(ev["new"]) + ev["after"].index(e)
        return done + ev["body"].index(e)

    with Layer(nc) as ctx:
        sb = lambda n, s, dt=F32: ctx.enter_context(nc.sbuf_tensor(f"{name}_{n}", s, dt))
        ps = lambda n, s: ctx.enter_context(nc.psum_tensor(f"{name}_{n}", s, F32))
        sem = lambda n: ctx.sem(f"{name}_{n}")
        w = Weights(nc, ctx, name, dram["w"], WIDTH)
        masks = sb("masks", [P, 4, P], BF16)
        q_bias = sb("q_bias", [P, GROUPS])
        v_t = sb("v_t", [P, CH])
        vals = sb("vals", [P, NB, HEADS, QUAD])
        v_last = sb("v_last", [P, NB, GH, DH])
        raw = [sb(f"raw{i}", [P, CH]) for i in range(2)]
        raw_hi = [sb(f"raw_hi{i}", [P, CH], F32R) for i in range(2)]
        q_st = [sb(f"q_st{i}", [P, CH], F32R) for i in range(2)]
        qm_st = [sb(f"qm_st{i}", [P, CH], F32R) for i in range(2)]
        k_st = [sb(f"k_st{i}", [P, CH], F32R) for i in range(2)]
        k_head = [sb(f"k_head{g}", [P, GH, CH], F32R) for g in range(GROUPS)]
        mx = sb("mx", [P, HEADS, NB])
        m_rest = sb("m_rest", [P, NB, GH])
        m_stage = sb("m_stage", [P, NB, P], BF16)
        probs = [sb(f"probs{i}", [P, CH]) for i in range(NP)]
        o_t = sb("o_t", [P, CH])
        rden = sb("rden", [P, NB * GH])
        attn = sb("attn", [P, CH])
        a_hi = sb("a_hi", [P, CH], F32R)
        a_lo = sb("a_lo", [P, CH], F32R)
        SM = [ps(f"SM{i}", [P, CH]) for i in range(2)]
        SE = [ps(f"SE{i}", [P, CH]) for i in range(NSE)]
        OT = ps("OT", [P, CH])
        BANK = {b: ps(f"bank_{b}", [P, CH]) for b in "AB"}
        A, B = BANK["A"], BANK["B"]

        masks_loaded, zeroed = sem("masks_loaded"), sem("zeroed")
        full = {b: sem(f"full_{b}") for b in "AB"}
        free = {b: sem(f"free_{b}") for b in "AB"}
        norm = Norm(nc, ctx, net, name, shared=(full["B"], free["B"]))
        split_ready = sem("split_ready")
        k_placed = [sem(f"k_placed{g}") for g in range(GROUPS)]
        smax_full, smax_read = sem("smax_full"), sem("smax_read")
        m_stepped, m_staged = sem("m_stepped"), sem("m_staged")
        sexp_full, exp_done, pv_done = sem("sexp_full"), sem("exp_done"), sem("pv_done")
        ot_read, rden_ready, attn_hi = sem("ot_read"), sem("rden_ready"), sem("attn_hi")
        bias_ready, v_ready = sem("bias_ready"), sem("v_ready")

        def mst(i):
            return m_stage[:, :, R_MAX + i:R_MAX + i + QUAD * (GH - 1) + 1:QUAD]

        def shifted(c, g, by):
            return c + (g + by) // GROUPS, (g + by) % GROUPS

        def start(i):
            return isinstance(i, int) and i == 0

        def chunks(eng, before, body, after):
            before()
            body(0, None, True)
            with eng.Fori(1, NC - 1) as c:
                body(c, c - 1, True)
            body(NC - 1, NC - 2, False)
            after()

        with nc.Block() as block:
            @block.sync
            def _(sp):
                def place(c, g):
                    i = c * GROUPS + g
                    if isinstance(c, int) and c == 0:
                        sp.wait_ge(zeroed, 4 + g)
                    sp.wait_ge(split_ready, 2 * i + 2)
                    for r in range(GH):
                        rows = slice(QUAD * r, QUAD * r + QUAD)
                        sp.dma_start(k_head[g][rows, r, :].bitcast(F32), k_st[g % 2][rows, :].bitcast(F32)).then_inc(k_placed[g], 16)

                def before():
                    place(0, 0)
                    place(0, 1)

                def body(c, lag, more):
                    for g in range(GROUPS):
                        if g < 2 or more:
                            place(*shifted(c, g, 2))
                        if g == 1 and lag is not None:
                            norm.sp_save(sp, lag)

                def after():
                    norm.sp_save(sp, NC - 1)

                w.sp_load(sp)
                sp.dma_start(masks[:], dram["masks"]).then_inc(masks_loaded, 16)
                chunks(sp, before, body, after)
                norm.sp_end(sp)

            @block.gpsimd
            def _(pool):
                pool.memset(m_stage[:], 0.0).then_inc(zeroed, 1)
                pool.memset(vals[:], 0.0).then_inc(zeroed, 1)
                pool.wait_ge(zeroed, 2)
                pool.memset(vals[:, :, :, DH:DH + 1], 1.0).then_inc(zeroed, 1)
                for g in range(GROUPS):
                    pool.memset(k_head[g][:].bitcast(F32), 0.0).then_inc(zeroed, 1)
                each(pool, lambda c: norm.pool_root(pool, c))

            @block.tensor
            def _(pe):
                def claim(bank, e, c):
                    wait(pe, free[bank], nth(bank, e, c))

                def project(e, c, of, col):
                    claim("A", e, c)
                    product3(pe, A[:], w.hi[:, col:col + P], w.lo[:, col:col + P],
                             net.x_hi[:, at(of)], net.x_lo[:, at(of)]).then_inc(full["A"], 1)

                def turn(e, c, src):
                    claim("B", e, c)
                    for j in range(NB):
                        mm = pe.transpose(B[:, j * P:(j + 1) * P], src[:, j * P:(j + 1) * P], net.ident[:])
                    mm.then_inc(full["B"], 1)

                def max_slot(c, g, s):
                    r, slot = s % GH, max_slots[s // GH]
                    i = c * GROUPS + g
                    if s == 0:
                        pe.wait_ge(split_ready, 2 * i + 1)
                        pe.wait_ge(k_placed[g], 16 * GH * (c + 1))
                    if not start(i) or s >= 2:
                        pe.wait_ge(smax_read, i * N + s - 1)
                    for a, b0, nb, col, u0, nu, mk in slot:
                        pe.matmul(SM[s % 2][:, col:col + nb * P], q_st[g % 2][:, a * P:(a + 1) * P],
                                  k_head[g][:, r, b0 * P:(b0 + nb) * P], start=True, stop=False)
                        for k, (table, mcol) in enumerate(mk):
                            mm = pe.matmul(SM[s % 2][:, mcol:mcol + P], net.ident16[:], masks[:, table, :],
                                           start=False, stop=k == len(mk) - 1)
                    mm.then_inc(smax_full, 1)

                def exp_slot(c, g, s):
                    r, slot = s % GH, exp_slots[s // GH]
                    i = c * GROUPS + g
                    ago = NSE if s >= NSE or N % NSE == 0 else s + N - max(t for t in range(N) if t % NSE == s)
                    if s == 0:
                        if g == 0:
                            pe.wait_ge(free["B"], nth("B", "T0", c - 1) + 1)
                        else:
                            pe.wait_ge(free["B"], nth("B", f"T{g}", c) + 1)
                    if not start(i) or s >= NSE:
                        pe.wait_ge(exp_done, i * N + s - ago + 1)
                    for a, b0, nb, col, u0, nu, mk in slot:
                        pe.matmul(SE[s % NSE][:, col:col + nb * P], k_head[g][:, r, a * P:(a + 1) * P],
                                  qm_st[g % 2][:, b0 * P:(b0 + nb) * P], start=True, stop=False)
                        for k, (table, mcol) in enumerate(mk):
                            mm = pe.matmul(SE[s % NSE][:, mcol:mcol + P], net.ident16[:], masks[:, 2 + table, :],
                                           start=False, stop=k == len(mk) - 1)
                    mm.then_inc(sexp_full, 1)

                def pv_batch(c, g, b):
                    i = c * GROUPS + g
                    if b == 0:
                        wait(pe, ot_read, i)
                        if g == 0:
                            pe.wait_ge(free["B"], nth("B", "VT", c - 1) + 1)
                        if g == GROUPS - 1:
                            pe.wait_ge(v_ready, c + 1)
                    pe.wait_ge(exp_done, i * N + (b + 1) * GH)
                    slot = exp_slots[b]
                    for k, (a, b0, nb, col, u0, nu, mk) in enumerate(slot):
                        used = col + (u0 - b0) * P
                        for r in range(GH):
                            mm = pe.matmul(OT[QUAD * r:QUAD * r + QUAD, u0 * P:(u0 + nu) * P], vals[:, a, GH * g + r, :],
                                           probs[(g * N + b * GH + r) % NP][:, used:used + nu * P],
                                           start=b == 0 and k == 0, stop=b == NV - 1 and k == len(slot) - 1,
                                           skip_group_check=True, tile_position=(0, QUAD * r))
                    mm.then_inc(pv_done, 1)

                def turn_max(e, c, i):
                    claim("B", e, c)
                    pe.wait_ge(m_staged, i + 1)
                    for j in range(NB):
                        mm = pe.matmul(B[:, j * P:(j + 1) * P], m_stage[:, j, :], net.ident16[:], start=True, stop=True)
                    mm.then_inc(full["B"], 1)

                def turn_out(e, c, i):
                    pe.wait_ge(ot_read, i + 1)
                    turn(e, c, o_t)

                def turn_attn(c):
                    turn("AT", c, attn)

                def out_proj(c, c_at):
                    claim("A", "WO", c)
                    pe.wait_ge(free["B"], nth("B", "AT", c_at) + 1)
                    product3(pe, A[:], w.hi[:, WO:WO + P], w.lo[:, WO:WO + P], a_hi[:], a_lo[:]).then_inc(full["A"], 1)

                def turn_y(c, lag):
                    pe.wait_ge(free["A"], nth("A", "WO", c) + 1)
                    norm.pe_turn_y(pe, lag, B, nth("B", "Y", c))

                def before():
                    project("V", -1, 0, WV)
                    for g in range(2):
                        project(f"Q{g}", -1, 0, WQ + g * P)
                        project(f"K{g}", -1, 0, WK + g * P)
                        if g == 0:
                            pe.wait_ge(free["A"], 1)
                            turn("VT", -1, v_t)
                    for s in range(N):
                        max_slot(0, 0, s)
                    turn_max("T0", -1, 0)

                def body(c, lag, more):
                    for g in range(GROUPS):
                        i = c * GROUPS + g
                        c1, g1 = shifted(c, g, 1)
                        c2, g2 = shifted(c, g, 2)
                        for s in range(N):
                            if g < 3 or more:
                                for m in range(ahead(s - 1) if s else 0, ahead(s)):
                                    max_slot(c1, g1, m)
                            exp_slot(c, g, s)
                            if s % GH == AT_PV:
                                if s > GH:
                                    pv_batch(c, g, s // GH - 1)
                                elif g:
                                    pv_batch(c, g - 1, NV - 1)
                                elif lag is not None:
                                    pv_batch(lag, GROUPS - 1, NV - 1)
                            if s == AT_Q and (g < 2 or more):
                                project(f"Q{g2}", c, c2, WQ + g2 * P)
                            if s == AT_O and (g or lag is not None):
                                turn_out(f"O{(g - 1) % GROUPS}", c, i - 1)
                            if s == AT_K and (g < 2 or more):
                                project(f"K{g2}", c, c2, WK + g2 * P)
                            if s == AT_O + 1 and g == 1 and lag is not None:
                                out_proj(c, c)
                            if s == AT_O + 1 and g == 2 and more:
                                project("V", c, c + 1, WV)
                            if s == AT_END and (g < 3 or more):
                                turn_max(f"T{g1}", c, i + 1)
                            if s == AT_END and g == 0 and lag is not None:
                                turn_attn(c)
                            if s == AT_END and g == 1 and lag is not None:
                                turn_y(c, lag)
                            if s == AT_END and g == 2 and lag is not None:
                                norm.pe_turn_x(pe, lag, B, nth("B", "X", c))
                            if s == AT_END and g == 3 and more:
                                pe.wait_ge(free["A"], nth("A", "V", c) + 1)
                                turn("VT", c, v_t)

                def after():
                    pv_batch(NC - 1, GROUPS - 1, NV - 1)
                    turn_out("O3", NC, NC * GROUPS - 1)
                    turn_attn(NC)
                    out_proj(NC, NC)
                    turn_y(NC, NC - 1)
                    norm.pe_turn_x(pe, NC - 1, B, nth("B", "X", NC))

                pe.wait_ge(w.lo_ready, 1)
                pe.wait_ge(masks_loaded, 16)
                pe.wait_ge(zeroed, 3)
                chunks(pe, before, body, after)

            @block.scalar
            def _(act):
                def take(bank, e, c):
                    act.wait_ge(full[bank], nth(bank, e, c) + 1)

                def values(c):
                    take("A", "V", c)
                    act.activation(v_t[:], A[:], ACT.Identity, bias=w.raw[:, BIAS + 8:BIAS + 9]).then_inc(free["A"], 1)

                def stage(e, c, i):
                    g, k = int(e[1]), int(e[0] == "K")
                    take("A", e, c)
                    if not start(i):
                        act.wait_ge(split_ready, 2 * i - 1 + k)
                    bias = w.raw[:, BIAS + 4 + g:BIAS + 5 + g] if k else q_bias[:, g:g + 1]
                    scale = 1.0 if k else w.raw[:, BIAS + 10:BIAS + 11]
                    act.activation(raw[k][:], A[:], ACT.Identity, bias=bias, scale=scale)
                    act.activation(raw_hi[k][:], A[:], ACT.Identity, bias=bias, scale=scale).then_inc(free["A"], 1)

                def exps(c, g, s):
                    slot, i = exp_slots[s // GH], c * GROUPS + g
                    lo = min(col + (u0 - b0) * P for _, b0, _, col, u0, _, _ in slot)
                    hi = max(col + (u0 - b0 + nu) * P for _, b0, _, col, u0, nu, _ in slot)
                    act.wait_ge(sexp_full, i * N + s + 1)
                    if not isinstance(i, int) or i * N + s >= NP:
                        act.wait_ge(pv_done, i * NV + (s - NP) // GH + 1)
                    act.activation(probs[(g * N + s) % NP][:, lo:hi], SE[s % NSE][:, lo:hi], ACT.Exp).then_inc(exp_done, 1)

                def outputs(i):
                    act.wait_ge(pv_done, (i + 1) * NV)
                    act.activation(o_t[:], OT[:], ACT.Copy).then_inc(ot_read, 1)

                def attn_upper(c):
                    take("B", "AT", c)
                    act.activation(a_hi[:], B[:], ACT.Copy).then_inc(attn_hi, 1)

                def y(c):
                    take("A", "WO", c)
                    act.activation(net.y_stage[:], A[:], ACT.Identity, bias=w.raw[:, BIAS + 9:BIAS + 10]
                                   ).then_inc(free["A"], 1)

                def before():
                    values(-1)
                    for g in range(2):
                        stage(f"Q{g}", -1, g)
                        stage(f"K{g}", -1, g)

                def body(c, lag, more):
                    for g in range(GROUPS):
                        i = c * GROUPS + g
                        g2 = shifted(c, g, 2)[1]
                        for s in range(N):
                            if s == 2 and (g or lag is not None):
                                outputs(i - 1)
                            exps(c, g, s)
                            if s == AT_Q and (g < 2 or more):
                                stage(f"Q{g2}", c, i + 2)
                            if s == AT_K and (g < 2 or more):
                                stage(f"K{g2}", c, i + 2)
                            if s == AT_O + 1 and g == 1 and lag is not None:
                                y(c)
                            if s == AT_O + 1 and g == 2 and more:
                                values(c)
                            if s == AT_END and g == 0 and lag is not None:
                                attn_upper(c)
                            if s == AT_END and g == 2 and lag is not None:
                                norm.act_hi(act, lag, B, nth("B", "X", c))

                def after():
                    outputs(NC * GROUPS - 1)
                    attn_upper(NC)
                    y(NC)
                    norm.act_hi(act, NC - 1, B, nth("B", "X", NC))

                w.act_split(act)
                act.wait_ge(bias_ready, 1)
                act.activation(net.spare[:, 0:1], w.raw[:, 0:1], ACT.Exp)
                chunks(act, before, body, after)

            @block.vector
            def _(dve):
                def take(e, c):
                    dve.wait_ge(full["B"], nth("B", e, c) + 1)

                def values(c):
                    take("VT", c)
                    v4 = B[:].rearrange("p (j h d) -> p j h d", j=NB, d=DH)
                    n = GH * (GROUPS - 1)
                    dve.tensor_copy(vals[:, :, 0:n, 0:DH], v4[:, :, 0:n, :])
                    dve.tensor_copy(v_last[:], v4[:, :, n:, :]).then_inc(free["B"], 1)

                def values_last(before_c, i):
                    dve.wait_ge(free["B"], nth("B", "VT", before_c) + 1)
                    wait(dve, pv_done, i * NV)
                    dve.tensor_copy(vals[:, :, GH * (GROUPS - 1):, 0:DH], v_last[:]).then_inc(v_ready, 1)

                def split(e, c, placed=None):
                    g, k = int(e[1]), int(e[0] == "K")
                    dve.wait_ge(free["A"], nth("A", e, c) + 1)
                    if placed is not None:
                        dve.wait_ge(k_placed[placed[1]], 16 * GH * (placed[0] + 1))
                    dst = (k_st if k else q_st)[g % 2]
                    dve.scalar_tensor_tensor(out=dst[:], in0=raw_hi[k][:].bitcast(F32), scalar=net.const[:, k:k + 1],
                                             in1=raw[k][:], op0=ALU.mult, op1=ALU.add).then_inc(split_ready, 1)

                def maximum(c, g, s):
                    r, slot = s % GH, max_slots[s // GH]
                    i = c * GROUPS + g
                    dve.wait_ge(smax_full, i * N + s + 1)
                    if s == 0:
                        wait(dve, m_staged, i)
                    for a, b0, nb, col, u0, nu, mk in slot:
                        used = col + (u0 - b0) * P
                        last = dve.tensor_reduce(mx[:, GH * g + r, a:a + 1], SM[s % 2][:, used:used + nu * P],
                                                 AX.X, ALU.max)
                    last.then_inc(smax_read, 1)

                def stage_max(g, i):
                    mg = mx[:, GH * g:GH * g + GH, :].rearrange("p h j -> p j h")
                    dve.wait_ge(smax_read, (i + 1) * N)
                    dve.tensor_scalar(mst(0), mg, -1.0, None, ALU.mult).then_inc(m_stepped, 1)
                    dve.wait_ge(m_stepped, 3 * i + 1)
                    dve.scalar_tensor_tensor(out=m_rest[:], in0=mg, scalar=-1.0, in1=mst(0),
                                             op0=ALU.mult, op1=ALU.subtract).then_inc(m_stepped, 1)
                    dve.wait_ge(m_stepped, 3 * i + 2)
                    dve.tensor_copy(mst(1), m_rest[:]).then_inc(m_stepped, 1)
                    dve.wait_ge(m_stepped, 3 * i + 3)
                    dve.tensor_tensor(mst(2), m_rest[:], mst(1), ALU.subtract).then_inc(m_staged, 1)

                def add_max(e, c):
                    g = int(e[1])
                    take(e, c)
                    dve.tensor_tensor(qm_st[g % 2][:], q_st[g % 2][:].bitcast(F32), B[:], ALU.add).then_inc(free["B"], 1)

                def outputs(e, c, i):
                    g = int(e[1])
                    take(e, c)
                    o4 = B[:].rearrange("p (j r w) -> p j r w", j=NB, w=QUAD)
                    r3 = rden[:].rearrange("p (j r) -> p j r", r=GH)
                    dve.reciprocal(r3, o4[:, :, :, DH]).then_inc(rden_ready, 1)
                    dve.wait_ge(rden_ready, i + 1)
                    a4 = attn[:].rearrange("p (j g r d) -> p j g r d", j=NB, g=GROUPS, d=DH)[:, :, g]
                    dve.tensor_tensor(a4, o4[:, :, :, 0:DH], r3.unsqueeze(3).broadcast_to([P, NB, GH, DH]),
                                      ALU.mult).then_inc(free["B"], 1)

                def attn_lower(c, lag):
                    dve.wait_ge(attn_hi, lag + 1)
                    dve.tensor_tensor(a_lo[:], B[:], a_hi[:].bitcast(F32), ALU.subtract).then_inc(free["B"], 1)

                def before():
                    split("Q0", -1)
                    split("K0", -1)
                    values(-1)
                    split("Q1", -1)
                    split("K1", -1)
                    for s in range(N):
                        maximum(0, 0, s)
                    stage_max(0, 0)
                    add_max("T0", -1)

                def body(c, lag, more):
                    for g in range(GROUPS):
                        i = c * GROUPS + g
                        c1, g1 = shifted(c, g, 1)
                        g2 = shifted(c, g, 2)[1]
                        for s in range(N):
                            if g < 3 or more:
                                for m in range(ahead(s - 1) if s else 0, ahead(s)):
                                    maximum(c1, g1, m)
                                if ahead(s) == N and ahead(s - 1) < N:
                                    stage_max(g1, i + 1)
                            if s == AT_Q + 1 and (g < 2 or more):
                                split(f"Q{g2}", c)
                            if s == 2 and g == 2 and lag is not None:
                                norm.dve_scale(dve, lag)
                            if s == 2 and g == 0:
                                values_last(c - 1 if lag is not None else -1, i)
                            if s == AT_K + 1 and (g < 2 or more):
                                split(f"K{g2}", c, (c, g))
                            if s == AT_O + 1 and (g or lag is not None):
                                outputs(f"O{(g - 1) % GROUPS}", c, i - 1)
                            if s == AT_END and (g < 3 or more):
                                add_max(f"T{g1}", c)
                            if s == AT_END and g == 0 and lag is not None:
                                attn_lower(c, lag)
                            if s == AT_END and g == 1 and lag is not None:
                                norm.dve_norm(dve, lag, B, nth("B", "Y", c))
                            if s == AT_END and g == 2 and lag is not None:
                                norm.dve_lo(dve, lag, B, nth("B", "X", c))
                            if s == AT_END and g == 3 and more:
                                values(c)

                def after():
                    outputs("O3", NC, NC * GROUPS - 1)
                    attn_lower(NC, NC - 1)
                    norm.dve_norm(dve, NC - 1, B, nth("B", "Y", NC))
                    norm.dve_scale(dve, NC - 1)
                    norm.dve_lo(dve, NC - 1, B, nth("B", "X", NC))

                w.dve_split(dve)
                dve.tensor_scalar(q_bias[:], w.raw[:, BIAS:BIAS + 4], w.raw[:, BIAS + 10:BIAS + 11], None,
                                  ALU.mult).then_inc(bias_ready, 1)
                dve.wait_ge(zeroed, 3)
                chunks(dve, before, body, after)


def gated_recurrence(nc, net):
    dram = net.dram["L1_attn"]
    WG, WH, WO = 0, P, 2 * P
    WIDTH = 3 * P
    BIAS = WIDTH
    with Layer(nc) as ctx:
        sb = lambda n, s, dt=F32: ctx.enter_context(nc.sbuf_tensor(f"rec_{n}", s, dt))
        ps = lambda n: ctx.enter_context(nc.psum_tensor(f"rec_{n}", [P, CH], F32))
        sem = lambda n: ctx.sem(f"rec_{n}")
        w = Weights(nc, ctx, "rec", dram["w"], WIDTH)
        norm = Norm(nc, ctx, net, "rec")
        bias = sb("bias", [P, 3])
        t_gate, t_hid, hid = sb("t_gate", [P, CH]), sb("t_hid", [P, CH]), sb("hid", [P, CH])
        u, v, h = sb("u", [P, CH]), sb("v", [P, CH]), sb("h", [P, CH])
        h_hi, h_lo = sb("h_hi", [P, CH], F32R), sb("h_lo", [P, CH], F32R)
        decay = sb("decay", [P, CH])
        GATE, HIDB, OUT, TY, TX = ps("GATE"), ps("HIDB"), ps("OUT"), ps("TY"), ps("TX")
        made, bias_ready = sem("made"), sem("bias_ready")
        gate_full, hid_full, gate_read, hid_read = sem("gate_full"), sem("hid_full"), sem("gate_read"), sem("hid_read")
        u_ready, v_ready, h_ready = sem("u_ready"), sem("v_ready"), sem("h_ready")
        h_hi_ready, h_lo_ready, out_full = sem("h_hi_ready"), sem("h_lo_ready"), sem("out_full")
        with nc.Block() as block:
            @block.sync
            def _(sp):
                w.sp_load(sp)
                with sp.Fori(0, NC) as c:
                    norm.sp_save(sp, c)
                norm.sp_end(sp)

            @block.gpsimd
            def _(pool):
                pool.memset(decay[:], 0.9).then_inc(made, 1)
                each(pool, lambda c: norm.pool_root(pool, c))

            @block.tensor
            def _(pe):
                def body(c, lag):
                    xh, xl = net.x_hi[:, at(c)], net.x_lo[:, at(c)]
                    wait(pe, gate_read, c)
                    product3(pe, GATE[:], w.hi[:, WG:WG + P], w.lo[:, WG:WG + P], xh, xl).then_inc(gate_full, 1)
                    wait(pe, hid_read, c)
                    product3(pe, HIDB[:], w.hi[:, WH:WH + P], w.lo[:, WH:WH + P], xh, xl).then_inc(hid_full, 1)
                    if lag is not None:
                        norm.pe_turn_y(pe, lag, TY)
                    pe.wait_ge(h_lo_ready, c + 1)
                    wait(pe, norm.y_staged, c)
                    product3(pe, OUT[:], w.hi[:, WO:WO + P], w.lo[:, WO:WO + P], h_hi[:], h_lo[:]).then_inc(out_full, 1)
                    if lag is not None:
                        norm.pe_turn_x(pe, lag, TX)

                def tail(c):
                    norm.pe_turn_y(pe, c, TY)
                    norm.pe_turn_x(pe, c, TX)

                pe.wait_ge(w.lo_ready, 1)
                lagged(pe, body, tail)

            @block.scalar
            def _(act):
                def body(c, lag):
                    act.wait_ge(gate_full, c + 1)
                    wait(act, v_ready, c)
                    act.activation(t_gate[:], GATE[:], ACT.Tanh, bias=bias[:, 0:1], scale=0.5).then_inc(gate_read, 1)
                    act.wait_ge(hid_full, c + 1)
                    act.activation(t_hid[:], HIDB[:], ACT.Tanh, bias=bias[:, 1:2], scale=0.5)
                    act.activation(hid[:], HIDB[:], ACT.Identity, bias=bias[:, 2:3], scale=0.025).then_inc(hid_read, 1)
                    act.wait_ge(h_ready, c + 1)
                    wait(act, out_full, c)
                    act.activation(h_hi[:], h[:], ACT.Copy).then_inc(h_hi_ready, 1)
                    if lag is not None:
                        norm.act_hi(act, lag, TX)
                    act.wait_ge(out_full, c + 1)
                    wait(act, norm.y_turned, c)
                    act.activation(net.y_stage[:], OUT[:], ACT.Identity,
                                   bias=w.raw[:, BIAS + 2:BIAS + 3]).then_inc(norm.y_staged, 1)

                w.act_split(act)
                act.wait_ge(bias_ready, 1)
                act.activation(net.spare[:, 0:1], bias[:, 0:1], ACT.Tanh)
                lagged(act, body, lambda c: norm.act_hi(act, c, TX))

            @block.vector
            def _(dve):
                def body(c, lag):
                    if lag is not None:
                        norm.dve_norm(dve, lag, TY)
                    dve.wait_ge(gate_read, c + 1)
                    dve.wait_ge(hid_read, c + 1)
                    dve.scalar_tensor_tensor(out=u[:], in0=t_hid[:], scalar=1.0, in1=hid[:],
                                             op0=ALU.add, op1=ALU.mult).then_inc(u_ready, 1)
                    dve.wait_ge(u_ready, c + 1)
                    dve.scalar_tensor_tensor(out=v[:], in0=t_gate[:], scalar=1.0, in1=u[:],
                                             op0=ALU.add, op1=ALU.mult).then_inc(v_ready, 1)
                    dve.wait_ge(v_ready, c + 1)
                    wait(dve, h_hi_ready, c)
                    dve.tensor_tensor_scan(h[:], decay[:], v[:], 0.0, ALU.mult, ALU.add).then_inc(h_ready, 1)
                    if lag is not None:
                        norm.dve_scale(dve, lag)
                    dve.wait_ge(h_hi_ready, c + 1)
                    wait(dve, out_full, c)
                    dve.tensor_tensor(h_lo[:], h[:], h_hi[:].bitcast(F32), ALU.subtract).then_inc(h_lo_ready, 1)
                    if lag is not None:
                        norm.dve_lo(dve, lag, TX)

                def tail(c):
                    norm.dve_norm(dve, c, TY)
                    norm.dve_scale(dve, c)
                    norm.dve_lo(dve, c, TX)

                w.dve_split(dve)
                dve.tensor_scalar(bias[:, 0:2], w.raw[:, BIAS:BIAS + 2], 0.5, None, ALU.mult)
                dve.tensor_scalar(bias[:, 2:3], w.raw[:, BIAS + 1:BIAS + 2], 0.025, None, ALU.mult).then_inc(bias_ready, 1)
                dve.wait_ge(made, 1)
                lagged(dve, body, tail)


def ternary_ffn(nc, net):
    dram = net.dram["L1_ffn"]
    KT = HID // P
    W1, W2 = 0, HID
    H1, H2 = 2 * HID, 2 * HID + KT * HID
    W3 = 2 * HID + 2 * KT * HID
    WIDTH = W3 + KT * P
    S1, S2, SH1, SH2, S3 = 0, KT, 2 * KT, 3 * KT, 4 * KT
    UNITS = 3 * KT
    with Layer(nc) as ctx:
        sb = lambda n, s, dt=F32: ctx.enter_context(nc.sbuf_tensor(f"ter_{n}", s, dt))
        ps = lambda n: ctx.enter_context(nc.psum_tensor(f"ter_{n}", [P, CH], F32))
        sem = lambda n: ctx.sem(f"ter_{n}")
        norm = Norm(nc, ctx, net, "ter")
        w_hi, w_lo = sb("w_hi", [P, WIDTH], F32R), sb("w_lo", [P, WIDTH], F32R)
        PIECES = [(0, H1), (H1, H2), (H2, W3), (W3, WIDTH)]
        w_raw = [sb(f"w_raw{i}", [P, KT * HID]) for i in range(2)]
        scales = sb("scales", [P, 4 * KT + 1])
        half = sb("half", [P, KT])
        t_silu = [sb(f"t_silu{i}", [P, CH]) for i in range(2)]
        z_half = [sb(f"z_half{i}", [P, CH]) for i in range(2)]
        silu = [sb(f"silu{i}", [P, CH]) for i in range(2)]
        hid = [sb(f"hid{i}", [P, CH]) for i in range(2)]
        h_hi = [sb(f"h_hi{i}", [P, KT, CH], F32R) for i in range(2)]
        h_lo = [sb(f"h_lo{i}", [P, KT, CH], F32R) for i in range(2)]
        B = [ps(f"B{i}") for i in range(4)]
        OUT, TY, TX = ps("OUT"), ps("TY"), ps("TX")
        w_loaded = [sem(f"w_loaded{i}") for i in range(len(PIECES))]
        scales_loaded, w_hi_ready, w_lo_ready, half_ready = (sem("scales_loaded"), sem("w_hi_ready"),
                                                             sem("w_lo_ready"), sem("half_ready"))
        a_full, b_full, a_read = sem("a_full"), sem("b_full"), sem("a_read")
        silu_ready, hid_made = sem("silu_ready"), sem("hid_made")
        g_full, g_made = sem("g_full"), sem("g_made")
        hi_made, lo_made, out_full = sem("hi_made"), sem("lo_made"), sem("out_full")
        with nc.Block() as block:
            @block.sync
            def _(sp):
                for i, (a, b) in enumerate(PIECES):
                    if i >= 2:
                        sp.wait_ge(w_lo_ready, i - 1)
                    sp.dma_start(w_raw[i % 2][:, 0:b - a], dram["w"][:, a:b]).then_inc(w_loaded[i], 16)
                    if i == 0:
                        sp.dma_start(scales[:], dram["scales"]).then_inc(scales_loaded, 16)
                with sp.Fori(0, NC) as c:
                    norm.sp_save(sp, c)
                norm.sp_end(sp)

            @block.gpsimd
            def _(pool):
                each(pool, lambda c: norm.pool_root(pool, c))

            @block.tensor
            def _(pe):
                def first(c):
                    xh, xl = net.x_hi[:, at(c)], net.x_lo[:, at(c)]
                    for t in range(KT):
                        a, b = B[t % 2], B[2 + t % 2]
                        if t < 2:
                            wait(pe, g_made, 2 * KT * c)
                        else:
                            pe.wait_ge(a_read, KT * c + t - 1)
                        col = W1 + t * P
                        product3(pe, a[:], w_hi[:, col:col + P], w_lo[:, col:col + P], xh, xl).then_inc(a_full, 1)
                        if t >= 2:
                            pe.wait_ge(hid_made, KT * c + t - 1)
                        col = W2 + t * P
                        product3(pe, b[:], w_hi[:, col:col + P], w_lo[:, col:col + P], xh, xl).then_inc(b_full, 1)

                def hidden(c, layer):
                    src, base = (layer - 1) % 2, (H1, H2)[layer - 1]
                    for k in range(KT):
                        pe.wait_ge(lo_made, UNITS * c + KT * (layer - 1) + k + 1)
                        for t in range(KT):
                            if k == 0:
                                if layer == 1:
                                    pe.wait_ge(a_read, KT * (c + 1))
                                    pe.wait_ge(hid_made, KT * (c + 1))
                                else:
                                    pe.wait_ge(g_made, 2 * KT * c + t + 1)
                            col = base + k * HID + t * P
                            mm = product3(pe, B[t][:], w_hi[:, col:col + P], w_lo[:, col:col + P],
                                          h_hi[src][:, k, :], h_lo[src][:, k, :], start=k == 0, stop=k == KT - 1)
                            if k == KT - 1:
                                mm.then_inc(g_full, 1)

                def out(c):
                    wait(pe, norm.y_staged, c)
                    for k in range(KT):
                        pe.wait_ge(lo_made, UNITS * c + 2 * KT + k + 1)
                        col = W3 + k * P
                        mm = product3(pe, OUT[:], w_hi[:, col:col + P], w_lo[:, col:col + P],
                                      h_hi[0][:, k, :], h_lo[0][:, k, :], start=k == 0, stop=k == KT - 1)
                    mm.then_inc(out_full, 1)

                def body(c, lag):
                    if isinstance(c, int):
                        pe.wait_ge(w_lo_ready, 1)
                    first(c)
                    if lag is not None:
                        norm.pe_turn_y(pe, lag, TY)
                    if isinstance(c, int):
                        pe.wait_ge(w_lo_ready, 2)
                    hidden(c, 1)
                    if lag is not None:
                        norm.pe_turn_x(pe, lag, TX)
                    if isinstance(c, int):
                        pe.wait_ge(w_lo_ready, 3)
                    hidden(c, 2)
                    if isinstance(c, int):
                        pe.wait_ge(w_lo_ready, 4)
                    out(c)

                def tail(c):
                    norm.pe_turn_y(pe, c, TY)
                    norm.pe_turn_x(pe, c, TX)

                lagged(pe, body, tail)

            @block.scalar
            def _(act):
                def upper(c, n):
                    layer, k = n // KT, n % KT
                    if layer == 0:
                        act.wait_ge(hid_made, KT * c + k + 1)
                    else:
                        act.wait_ge(g_made, 2 * KT * c + n - KT + 1)
                    if layer == 0:
                        wait(act, out_full, c)
                    elif layer == 1:
                        wait(act, g_full, 2 * KT * c)
                    else:
                        act.wait_ge(g_full, 2 * KT * c + KT)
                    act.activation(h_hi[layer % 2][:, k, :], hid[n % 2][:], ACT.Copy).then_inc(hi_made, 1)

                def first(c):
                    for t in range(KT):
                        act.wait_ge(a_full, KT * c + t + 1)
                        if not (isinstance(c, int) and c == 0 and t < 2):
                            act.wait_ge(silu_ready, KT * c + t - 1)
                        act.activation(t_silu[t % 2][:], B[t % 2][:], ACT.Tanh, scale=half[:, t:t + 1])
                        act.activation(z_half[t % 2][:], B[t % 2][:], ACT.Copy,
                                       scale=half[:, t:t + 1]).then_inc(a_read, 1)
                        if t:
                            upper(c, t - 1)
                    upper(c, KT - 1)

                def hidden(c, layer):
                    for t in range(KT):
                        n = KT * layer + t
                        act.wait_ge(g_full, 2 * KT * c + n - KT + 1)
                        act.wait_ge(lo_made, UNITS * c + n - 1)
                        act.activation(hid[n % 2][:], B[t][:], ACT.Gelu,
                                       scale=scales[:, KT * (layer + 1) + t:KT * (layer + 1) + t + 1]).then_inc(g_made, 1)
                        upper(c, n)

                def body(c, lag):
                    first(c)
                    hidden(c, 1)
                    if lag is not None:
                        norm.act_hi(act, lag, TX)
                    hidden(c, 2)
                    act.wait_ge(out_full, c + 1)
                    wait(act, norm.y_turned, c)
                    act.activation(net.y_stage[:], OUT[:], ACT.Copy, scale=scales[:, S3:S3 + 1]).then_inc(norm.y_staged, 1)

                for i, (a, b) in enumerate(PIECES):
                    act.wait_ge(w_loaded[i], 16)
                    act.activation(w_hi[:, a:b], w_raw[i % 2][:, 0:b - a], ACT.Copy).then_inc(w_hi_ready, 1)
                act.wait_ge(half_ready, 1)
                act.activation(net.spare[:, 0:1], half[:, 0:1], ACT.Gelu)
                lagged(act, body, lambda c: norm.act_hi(act, c, TX))

            @block.vector
            def _(dve):
                def lower(c, n):
                    layer, k = n // KT, n % KT
                    dve.wait_ge(hi_made, UNITS * c + n + 1)
                    dve.tensor_tensor(h_lo[layer % 2][:, k, :], hid[n % 2][:], h_hi[layer % 2][:, k, :].bitcast(F32),
                                      ALU.subtract).then_inc(lo_made, 1)

                def first(c):
                    for t in range(KT):
                        dve.wait_ge(a_read, KT * c + t + 1)
                        if not (isinstance(c, int) and c == 0 and t < 2):
                            dve.wait_ge(hid_made, KT * c + t - 1)
                        dve.scalar_tensor_tensor(out=silu[t % 2][:], in0=t_silu[t % 2][:], scalar=1.0,
                                                 in1=z_half[t % 2][:], op0=ALU.add, op1=ALU.mult).then_inc(silu_ready, 1)
                        dve.wait_ge(b_full, KT * c + t + 1)
                        dve.wait_ge(silu_ready, KT * c + t + 1)
                        if not (isinstance(c, int) and c == 0 and t < 2):
                            dve.wait_ge(lo_made, UNITS * c + t - 1)
                        dve.scalar_tensor_tensor(out=hid[t % 2][:], in0=B[2 + t % 2][:], scalar=scales[:, S2 + t:S2 + t + 1],
                                                 in1=silu[t % 2][:], op0=ALU.mult, op1=ALU.mult).then_inc(hid_made, 1)
                        if t:
                            lower(c, t - 1)
                    lower(c, KT - 1)

                def body(c, lag):
                    first(c)
                    if lag is not None:
                        norm.dve_norm(dve, lag, TY)
                        norm.dve_scale(dve, lag)
                    for n in range(KT, 2 * KT):
                        lower(c, n)
                    if lag is not None:
                        norm.dve_lo(dve, lag, TX)
                    for n in range(2 * KT, UNITS):
                        lower(c, n)

                def tail(c):
                    norm.dve_norm(dve, c, TY)
                    norm.dve_scale(dve, c)
                    norm.dve_lo(dve, c, TX)

                dve.wait_ge(scales_loaded, 16)
                dve.tensor_scalar(half[:], scales[:, S1:S1 + KT], 0.5, None, ALU.mult).then_inc(half_ready, 1)
                for i, (a, b) in enumerate(PIECES):
                    dve.wait_ge(w_hi_ready, i + 1)
                    dve.tensor_tensor(w_lo[:, a:b], w_raw[i % 2][:, 0:b - a], w_hi[:, a:b].bitcast(F32),
                                      ALU.subtract).then_inc(w_lo_ready, 1)
                lagged(dve, body, tail)


def linear_attention(nc, net):
    dram = net.dram["L3_attn"]
    FEATS = 32
    FW = GH * FEATS
    VW = D + HEADS
    YAT = 0.1
    WQ, WK, WV, WO, WP = 0, P, 2 * P, 3 * P, 4 * P
    WIDTH = WP + GROUPS * FW
    BIAS = WIDTH
    AT_, WO_, Y_, X_ = range(4)
    with Layer(nc) as ctx:
        sb = lambda n, s, dt=F32: ctx.enter_context(nc.sbuf_tensor(f"lin_{n}", s, dt))
        ps = lambda n: ctx.enter_context(nc.psum_tensor(f"lin_{n}", [P, CH], F32))
        sem = lambda n: ctx.sem(f"lin_{n}")
        w = Weights(nc, ctx, "lin", dram["w"], WIDTH)
        own = sb("own", [P, GROUPS, VW])
        qkv_t = [sb(f"qkv_t{i}", [P, CH]) for i in range(3)]
        sq = [sb(f"sq{i}", [P, CH]) for i in range(2)]
        ss, nrm, nrm_e, rinv = (sb("ss", [P, 2 * NB * HEADS]), sb("nrm", [P, 2 * NB * HEADS]),
                                sb("nrm_e", [P, 2 * NB * HEADS]), sb("rinv", [P, 2 * NB * HEADS]))
        root, root_g = sb("root", [P, 2 * NB * HEADS]), sb("root_g", [P, 2 * NB * HEADS])
        N_STEPS = 6
        normed = [sb(f"normed{i}", [P, CH]) for i in range(2)]
        n_hi = [sb(f"n_hi{i}", [P, CH], F32R) for i in range(2)]
        n_lo = [sb(f"n_lo{i}", [P, CH], F32R) for i in range(2)]
        vals = sb("vals", [P, NB, VW])
        k_feat = sb("k_feat", [P, NB, GROUPS * FW])
        q_relu = [sb(f"q_relu{i}", [P, CH]) for i in range(2)]
        q_feat = sb("q_feat", [P, GROUPS, CH])
        kv = sb("kv", [P, GROUPS, VW])
        den, rden = sb("den", [P, NB, HEADS]), sb("rden", [P, NB, HEADS])
        attn = sb("attn", [P, CH])
        a_hi, a_lo = sb("a_hi", [P, CH], F32R), sb("a_lo", [P, CH], F32R)
        A = [ps(f"A{i}") for i in range(3)]
        F = [ps(f"F{i}") for i in range(2)]
        KV = [ps(f"KV{i}") for i in range(2)]
        TB = ps("TB")
        norm_sems = sem("tb_full"), sem("tb_free")
        tb_full, tb_free = norm_sems
        norm = Norm(nc, ctx, net, "lin", shared=norm_sems)
        own_loaded, ones_made = sem("own_loaded"), sem("ones_made")
        proj_full, staged, turned = sem("proj_full"), sem("staged"), sem("turned")
        sq_ready, ss_ready, root_ready, n_stepped = sem("sq_ready"), sem("ss_ready"), sem("root_ready"), sem("n_stepped")
        normed_ready, vals_ready, back, n_hi_ready, n_lo_ready = (sem("normed_ready"), sem("vals_ready"), sem("back"),
                                                                  sem("n_hi_ready"), sem("n_lo_ready"))
        kf_full, kf_ready, qf_full, qr_ready, qf_ready = (sem("kf_full"), sem("kf_ready"), sem("qf_full"),
                                                          sem("qr_ready"), sem("qf_ready"))
        kv_full, kv_ready, o_full, o_stepped, attn_ready, attn_hi = (sem("kv_full"), sem("kv_ready"), sem("o_full"),
                                                                     sem("o_stepped"), sem("attn_ready"), sem("attn_hi"))
        with nc.Block() as block:
            @block.sync
            def _(sp):
                w.sp_load(sp)
                sp.dma_start(own[:], dram["own"]).then_inc(own_loaded, 16)
                with sp.Fori(0, NC) as c:
                    norm.sp_save(sp, c)
                norm.sp_end(sp)

            @block.gpsimd
            def _(pool):
                pool.memset(vals[:, :, D:VW], 1.0).then_inc(ones_made, 1)

                each(pool, lambda c: norm.pool_root(pool, c))

            @block.tensor
            def _(pe):
                def turn(src, bank):
                    for j in range(NB):
                        mm = pe.transpose(bank[:, j * P:(j + 1) * P], src[:, j * P:(j + 1) * P], net.ident[:])
                    return mm

                def attn_t(lag):
                    pe.wait_ge(attn_ready, 2 * (lag + 1))
                    wait(pe, tb_free, 4 * lag)
                    turn(attn, TB).then_inc(tb_full, 1)

                def out_proj(lag):
                    pe.wait_ge(tb_free, 4 * lag + WO_)
                    product3(pe, TB[:], w.hi[:, WO:WO + P], w.lo[:, WO:WO + P], a_hi[:], a_lo[:]).then_inc(tb_full, 1)

                def body(c, lag):
                    for i, col in enumerate((WQ, WK, WV)):
                        if i < 2:
                            wait(pe, n_lo_ready, 2 * c)
                        else:
                            wait(pe, vals_ready, c)
                        product3(pe, A[i][:], w.hi[:, col:col + P], w.lo[:, col:col + P],
                                 net.x_hi[:, at(c)], net.x_lo[:, at(c)]).then_inc(proj_full, 1)
                    if lag is not None:
                        attn_t(lag)
                    for i in range(3):
                        pe.wait_ge(staged, 3 * c + i + 1)
                        turn(qkv_t[i], A[i]).then_inc(turned, 1)
                    if lag is not None:
                        out_proj(lag)
                    for i in range(2):
                        pe.wait_ge(normed_ready, 2 * c + i + 1)
                        turn(normed[i], A[i]).then_inc(back, 1)
                    if lag is not None:
                        norm.pe_turn_y(pe, lag, TB, 4 * lag + Y_)
                    pe.wait_ge(n_lo_ready, 2 * c + 2)
                    for j in range(NB):
                        if j < 2:
                            wait(pe, qr_ready, GROUPS * c)
                        else:
                            pe.wait_ge(kf_ready, NB * c + j - 1)
                        sl = slice(j * P, (j + 1) * P)
                        ph, pl = w.hi[:, WP:WIDTH], w.lo[:, WP:WIDTH]
                        pe.matmul(F[j % 2][:], n_hi[1][:, sl], ph, start=True, stop=False)
                        pe.matmul(F[j % 2][:], n_lo[1][:, sl], ph, start=False, stop=False)
                        pe.matmul(F[j % 2][:], n_hi[1][:, sl], pl, start=False, stop=True).then_inc(kf_full, 1)
                    for g in range(GROUPS):
                        if g < 2:
                            pe.wait_ge(kf_ready, NB * c + NB - 1 + g)
                        else:
                            pe.wait_ge(qr_ready, GROUPS * c + g - 1)
                        col = WP + g * FW
                        product3(pe, F[g % 2][:], w.hi[:, col:col + FW], w.lo[:, col:col + FW],
                                 n_hi[0][:], n_lo[0][:]).then_inc(qf_full, 1)
                    if lag is not None:
                        norm.pe_turn_x(pe, lag, TB, 4 * lag + X_)
                    pe.wait_ge(vals_ready, c + 1)
                    pe.wait_ge(kf_ready, NB * (c + 1))
                    wait(pe, attn_ready, 2 * c)
                    for g in range(GROUPS):
                        for j in range(NB):
                            mm = pe.matmul(KV[g // 2][:, (g % 2) * VW:(g % 2 + 1) * VW], k_feat[:, j, g * FW:(g + 1) * FW],
                                           vals[:, j, :], start=j == 0, stop=j == NB - 1)
                        if g % 2:
                            mm.then_inc(kv_full, 1)
                    pe.wait_ge(kv_ready, 2 * c + 2)
                    pe.wait_ge(qf_ready, GROUPS * (c + 1))
                    for j in range(NB):
                        for g in range(GROUPS):
                            mm = pe.matmul(KV[j // 2][:, (j % 2) * VW:(j % 2 + 1) * VW], q_feat[:, g, j * P:(j + 1) * P],
                                           kv[:, g, :], start=g == 0, stop=g == GROUPS - 1)
                        if j % 2:
                            mm.then_inc(o_full, 1)

                def tail(c):
                    attn_t(c)
                    out_proj(c)
                    norm.pe_turn_y(pe, c, TB, 4 * c + Y_)
                    norm.pe_turn_x(pe, c, TB, 4 * c + X_)

                pe.wait_ge(w.lo_ready, 1)
                pe.wait_ge(ones_made, 1)
                lagged(pe, body, tail)

            @block.scalar
            def _(act):
                def attn_upper(lag):
                    act.wait_ge(tb_full, 4 * lag + AT_ + 1)
                    act.activation(a_hi[:], TB[:], ACT.Copy).then_inc(attn_hi, 1)

                def y(lag):
                    act.wait_ge(tb_full, 4 * lag + WO_ + 1)
                    act.activation(net.y_stage[:], TB[:], ACT.Identity, bias=w.raw[:, BIAS + 3:BIAS + 4]).then_inc(tb_free, 1)

                def body(c, lag):
                    for i in range(3):
                        act.wait_ge(proj_full, 3 * c + i + 1)
                        act.activation(qkv_t[i][:], A[i][:], ACT.Identity,
                                       bias=w.raw[:, BIAS + i:BIAS + i + 1]).then_inc(staged, 1)
                    if lag is not None:
                        attn_upper(lag)
                    for i in range(2):
                        act.wait_ge(turned, 3 * c + i + 1)
                        wait(act, ss_ready, c)
                        act.activation(sq[i][:], A[i][:], ACT.Square).then_inc(sq_ready, 1)
                    act.wait_ge(ss_ready, c + 1)
                    act.activation(root[:], ss[:], ACT.Sqrt).then_inc(root_ready, 1)
                    act.wait_ge(turned, 3 * c + 3)
                    act.activation(vals[:, :, 0:D], tile3(A[2][:]), ACT.Copy).then_inc(vals_ready, 1)
                    if lag is not None:
                        y(lag)
                    for i in range(2):
                        act.wait_ge(back, 2 * c + i + 1)
                        act.activation(n_hi[i][:], A[i][:], ACT.Copy).then_inc(n_hi_ready, 1)
                    for g in range(GROUPS):
                        act.wait_ge(qf_full, GROUPS * c + g + 1)
                        if not (isinstance(c, int) and c == 0 and g < 2):
                            act.wait_ge(qf_ready, GROUPS * c + g - 1)
                        act.activation(q_relu[g % 2][:], F[g % 2][:], ACT.Relu).then_inc(qr_ready, 1)
                        act.wait_ge(qr_ready, GROUPS * c + g + 1)
                        act.activation(q_feat[:, g, :], q_relu[g % 2][:], ACT.Copy, bias=YAT).then_inc(qf_ready, 1)
                    if lag is not None:
                        norm.act_hi(act, lag, TB, 4 * lag + X_)

                def tail(c):
                    attn_upper(c)
                    y(c)
                    norm.act_hi(act, c, TB, 4 * c + X_)

                w.act_split(act)
                act.activation(net.spare[:, 0:1], net.ident[:, 0:1], ACT.Sqrt)
                lagged(act, body, tail)

            @block.vector
            def _(dve):
                def attn_lower(lag):
                    dve.wait_ge(attn_hi, lag + 1)
                    dve.tensor_tensor(a_lo[:], TB[:], a_hi[:].bitcast(F32), ALU.subtract).then_inc(tb_free, 1)

                def body(c, lag):
                    if lag is not None:
                        attn_lower(lag)
                    for i in range(2):
                        dve.wait_ge(sq_ready, 2 * c + i + 1)
                        last = dve.tensor_reduce(ss[:, i * 64:(i + 1) * 64], sq[i][:].rearrange("p (n d) -> p n d", d=DH),
                                                 AX.X, ALU.add)
                    last.then_inc(ss_ready, 1)
                    dve.wait_ge(root_ready, c + 1)
                    dve.tensor_scalar(root_g[:], root[:], 1e-30, None, ALU.max).then_inc(n_stepped, 1)
                    dve.wait_ge(n_stepped, N_STEPS * c + 1)
                    dve.reciprocal(rinv[:], root_g[:]).then_inc(n_stepped, 1)
                    dve.wait_ge(n_stepped, N_STEPS * c + 2)
                    dve.tensor_tensor(nrm[:], ss[:], rinv[:], ALU.mult).then_inc(n_stepped, 1)
                    dve.wait_ge(n_stepped, N_STEPS * c + 3)
                    dve.tensor_tensor(nrm_e[:], nrm[:], root_g[:], ALU.add).then_inc(n_stepped, 1)
                    dve.wait_ge(n_stepped, N_STEPS * c + 4)
                    dve.tensor_scalar(nrm[:], nrm_e[:], 0.5, 1e-8, ALU.mult, ALU.add).then_inc(n_stepped, 1)
                    dve.wait_ge(n_stepped, N_STEPS * c + 5)
                    dve.reciprocal(rinv[:], nrm[:]).then_inc(n_stepped, 1)
                    dve.wait_ge(n_stepped, N_STEPS * c + 6)
                    for i in range(2):
                        r3 = rinv[:, i * 64:(i + 1) * 64].unsqueeze(2).broadcast_to([P, 64, DH])
                        dve.tensor_tensor(normed[i][:].rearrange("p (n d) -> p n d", d=DH),
                                          A[i][:].rearrange("p (n d) -> p n d", d=DH), r3, ALU.mult).then_inc(normed_ready, 1)
                    if lag is not None:
                        norm.dve_norm(dve, lag, TB, 4 * lag + Y_)
                    for i in range(2):
                        dve.wait_ge(n_hi_ready, 2 * c + i + 1)
                        dve.tensor_tensor(n_lo[i][:], A[i][:], n_hi[i][:].bitcast(F32), ALU.subtract).then_inc(n_lo_ready, 1)
                    for j in range(NB):
                        dve.wait_ge(kf_full, NB * c + j + 1)
                        dve.tensor_scalar(k_feat[:, j, :], F[j % 2][:], YAT, YAT, ALU.add, ALU.max).then_inc(kf_ready, 1)
                    if lag is not None:
                        norm.dve_scale(dve, lag)
                        norm.dve_lo(dve, lag, TB, 4 * lag + X_)
                    for i in range(2):
                        dve.wait_ge(kv_full, 2 * c + i + 1)
                        dve.tensor_tensor(kv[:, 2 * i:2 * i + 2, :], tile3(KV[i][:, 0:2 * VW], 2), own[:, 2 * i:2 * i + 2, :],
                                          ALU.mult).then_inc(kv_ready, 1)
                    for i in range(2):
                        o3 = tile3(KV[i][:, 0:2 * VW], 2)
                        dsl, rsl = den[:, 2 * i:2 * i + 2, :], rden[:, 2 * i:2 * i + 2, :]
                        dve.wait_ge(o_full, 2 * c + i + 1)
                        dve.tensor_scalar(dsl, o3[:, :, D:VW], 1e-6, None, ALU.max).then_inc(o_stepped, 1)
                        dve.wait_ge(o_stepped, 4 * c + 2 * i + 1)
                        dve.reciprocal(rsl, dsl).then_inc(o_stepped, 1)
                        dve.wait_ge(o_stepped, 4 * c + 2 * i + 2)
                        a4 = attn[:, i * 2 * P:(i + 1) * 2 * P].rearrange("p (j h d) -> p j h d", j=2, d=DH)
                        dve.tensor_tensor(a4, o3[:, :, 0:D].rearrange("p j (h d) -> p j h d", d=DH),
                                          rsl.unsqueeze(3).broadcast_to([P, 2, HEADS, DH]), ALU.mult).then_inc(attn_ready, 1)

                def tail(c):
                    attn_lower(c)
                    norm.dve_norm(dve, c, TB, 4 * c + Y_)
                    norm.dve_scale(dve, c)
                    norm.dve_lo(dve, c, TB, 4 * c + X_)

                w.dve_split(dve)
                dve.wait_ge(own_loaded, 16)
                lagged(dve, body, tail)


def experts_ffn(nc, net, name, hid, gelu, by_probs, shared, last=False):
    dram = net.dram[name]
    KT = hid // P
    NE = E + shared
    ROUND = 4
    CB = max(2, ROUND // KT)
    UNITS = CB * KT
    TURNS = NC // CB
    EW = 2 * KT * P
    B1, B2 = EW, EW + KT
    G_BIAS = P
    CAP = int(1.25 * NC * CH / E)
    S = NB * E
    with Layer(nc) as ctx:
        sb = lambda n, s, dt=F32: ctx.enter_context(nc.sbuf_tensor(f"{name}_{n}", s, dt))
        ps = lambda n: ctx.enter_context(nc.psum_tensor(f"{name}_{n}", [P, CH], F32))
        sem = lambda n: ctx.sem(f"{name}_{n}")
        norm = Norm(nc, ctx, net, name, last=last)
        gate = Weights(nc, ctx, f"{name}_gate", dram["gate"], P)
        weight_rows = nc.dram_tensor(f"{name}_weight_rows", [NE, NC, NB, P], F32, kind="Internal").ap()
        acc = sb("acc", [P, NC * CH])
        e_raw = [sb(f"e_raw{i}", [P, B2 + 1]) for i in range(2)]
        e_bias = [sb(f"e_bias{i}", [P, KT + 1]) for i in range(2)]
        e_hi = [sb(f"e_hi{i}", [P, EW], F32R) for i in range(2)]
        e_lo = [sb(f"e_lo{i}", [P, EW], F32R) for i in range(2)]
        wt = [sb(f"wt{i}", [P, NC * CH]) for i in range(2)]
        h = [sb(f"h{i}", [P, CH]) for i in range(ROUND)]
        h_hi = [sb(f"h_hi{i}", [P, CH], F32R) for i in range(ROUND)]
        h_lo = [sb(f"h_lo{i}", [P, CH], F32R) for i in range(ROUND)]
        yw = [sb(f"yw{i}", [P, CH]) for i in range(CB)]
        lg_t = sb("lg_t", [P, CH])
        iota8 = sb("iota8", [P, NB, E])
        lg = sb("lg", [P, NB, E])
        top, idx = sb("top", [P, NB, 8]), sb("idx", [P, NB, 8], U32)
        idxf, d2, e2 = sb("idxf", [P, NB, 2]), sb("d2", [P, NB, 2]), sb("e2", [P, NB, 2])
        pr, d8, d8b = sb("pr", [P, NB, E]), sb("d8", [P, NB, E]), sb("d8b", [P, NB, E])
        s1, r1 = sb("s1", [P, NB]), sb("r1", [P, NB])
        w2 = sb("w2", [P, NB, 2])
        oh = [sb(f"oh{i}", [P, NB, E]) for i in range(2)]
        pick = [sb(f"pick{i}", [P, NB, E]) for i in range(2)]
        comb_all = sb("comb_all", [P, NC, S])
        count = sb("count", [P, S])
        count8, keep = sb("count8", [P, E]), sb("keep", [P, E])
        ones = sb("ones", [P, P])
        comb = sb("comb", [P, P])
        comb_t = sb("comb_t", [P, NC, P])
        one_row = sb("one_row", [NC * NB, P])

        H = [ps(f"H{i}") for i in range(ROUND)]
        TY, TX = ps("TY"), ps("TX")
        Y = [ps("Y0"), ps("Y1"), TY, TX]

        made, iota_loaded = sem("made"), sem("iota_loaded")
        lg_full, lg_staged, lg_turned = sem("lg_full"), sem("lg_staged"), sem("lg_turned")
        g_stepped, g_exp, comb_ready, comb_turned, comb_saved = (sem("g_stepped"), sem("g_exp"), sem("comb_ready"),
                                                                 sem("comb_turned"), sem("comb_saved"))
        k_stepped, k_full, rows_out = sem("k_stepped"), sem("k_full"), sem("rows_out")
        e_loaded, wt_loaded = [sem(f"e_loaded{i}") for i in range(2)], [sem(f"wt_loaded{i}") for i in range(2)]
        e_hi_ready, e_ready = sem("e_hi_ready"), sem("e_ready")
        h_full, h_ready, h_hi_ready, h_lo_ready = sem("h_full"), sem("h_ready"), sem("h_hi_ready"), sem("h_lo_ready")
        y_full, yw_ready, acc_ready = sem("y_full"), sem("yw_ready"), sem("acc_ready")

        STEPS = 15 if by_probs else 10

        def experts(eng, body):
            with eng.Fori(0, E // 2) as q:
                for i in range(2):
                    body(2 * q + i, i)
            if shared:
                body(E, 0)

        with nc.Block() as block:
            @block.sync
            def _(sp):
                gate.sp_load(sp)
                sp.dma_start(iota8[:], dram["iota8"]).then_inc(iota_loaded, 16)
                sp.wait_ge(comb_saved, NC)
                sp.wait_ge(made, 6)
                for j in range(NB):
                    sp.dma_start(weight_rows[0:E, :, j, :], comb_t[j * E:(j + 1) * E, :, :]).then_inc(rows_out, 16)
                if shared:
                    sp.dma_start(weight_rows[E].rearrange("c j p -> (c j) p"), one_row[:]).then_inc(rows_out, 16)
                sp.wait_ge(rows_out, 16 * (NB + shared))

                def load(e, i):
                    src = dram["w"][bass.ds(e, 1)].rearrange("a p n -> p (a n)")
                    row = weight_rows[bass.ds(e, 1)].rearrange("a c j p -> a (c j p)")
                    wait(sp, e_ready, e - 1)
                    sp.dma_start(e_raw[i][:], src).then_inc(e_loaded[i], 16)
                    wait(sp, yw_ready, 1 + (e - 1) * NC)
                    sp.dma_start(wt[i][:], row.broadcast_to([P, NC * CH])).then_inc(wt_loaded[i], 16)

                load(0, 0)
                load(1, 1)
                with sp.Fori(1, E // 2) as q:
                    for i in range(2):
                        load(2 * q + i, i)
                if shared:
                    load(E, 0)
                with sp.Fori(0, NC) as c:
                    norm.sp_save(sp, c)
                norm.sp_end(sp)

            @block.gpsimd
            def _(pool):
                pool.memset(comb[:], 0.0).then_inc(made, 1)
                pool.memset(count[:], 0.0).then_inc(made, 1)
                pool.memset(ones[:], 1.0).then_inc(made, 1)
                pool.memset(one_row[:], 1.0).then_inc(made, 1)
                pool.memset(acc[:, 0:NC * CH // 2], 0.0).then_inc(made, 1)
                pool.memset(acc[:, NC * CH // 2:], 0.0).then_inc(made, 1)
                pool.sem_inc(acc_ready, 1)
                pool.wait_ge(made, 6)

                def split(e, i, turn):
                    pool.wait_ge(e_loaded[i], 16 * turn + 16)
                    wait(pool, yw_ready, 1 + (e - 1) * NC)
                    settle(pool, net)
                    pool.tensor_copy(e_hi[i][:], e_raw[i][:, 0:EW])
                    pool.tensor_copy(e_bias[i][:], e_raw[i][:, EW:B2 + 1]).then_inc(e_hi_ready, 1)
                    pool.wait_ge(e_hi_ready, e + 1)
                    pool.tensor_tensor(e_lo[i][:], e_raw[i][:, 0:EW], e_hi[i][:].bitcast(F32),
                                       ALU.subtract).then_inc(e_ready, 1)

                def gather(e):
                    with pool.Fori(0, TURNS) as b:
                        for k in range(CB):
                            c = b * CB + k
                            pool.wait_ge(yw_ready, 1 + e * NC + c + 1)
                            pool.tensor_tensor(acc[:, at(c)], acc[:, at(c)], yw[k][:], ALU.add).then_inc(acc_ready, 1)

                split(0, 0, 0)
                split(1, 1, 0)
                gather(0)
                with pool.Fori(1, E // 2) as q:
                    split(2 * q, 0, q)
                    gather(2 * q - 1)
                    split(2 * q + 1, 1, q)
                    gather(2 * q)
                if shared:
                    split(E, 0, E // 2)
                gather(E - 1)
                if shared:
                    gather(E)
                each(pool, lambda c: norm.pool_root(pool, c))

            @block.tensor
            def _(pe):
                def turn_weights(c):
                    pe.wait_ge(comb_ready, c + 1)
                    wait(pe, comb_saved, c)
                    pe.transpose(Y[0][:, 0:P], comb[:], net.ident[:]).then_inc(comb_turned, 1)

                def gates(c, lag):
                    wait(pe, lg_staged, c)
                    product3(pe, TY[:], gate.hi[:], gate.lo[:], net.x_hi[:, at(c)], net.x_lo[:, at(c)]
                             ).then_inc(lg_full, 1)
                    if lag is not None and not by_probs:
                        turn_weights(lag)
                    pe.wait_ge(lg_staged, c + 1)
                    if lag is not None:
                        pe.wait_ge(g_stepped, STEPS * lag + 1)
                    for j in range(NB):
                        mm = pe.transpose(TX[:, j * P:(j + 1) * P], lg_t[:, j * P:(j + 1) * P], net.ident[:])
                    mm.then_inc(lg_turned, 1)

                def expert(e, i):
                    pe.wait_ge(e_ready, e + 1)
                    settle(pe, net)
                    w_up, w_down = (e_hi[i], e_lo[i]), KT * P
                    with pe.Fori(0, TURNS) as b:
                        for rnd in range(UNITS // ROUND):
                            for r in range(ROUND):
                                u = rnd * ROUND + r
                                c, t = b * CB + u // KT, u % KT
                                sl = slice(t * P, (t + 1) * P)
                                product3(pe, H[r][:], e_hi[i][:, sl], e_lo[i][:, sl],
                                         net.x_hi[:, at(c)], net.x_lo[:, at(c)]).then_inc(h_full, 1)
                            for r in range(ROUND):
                                u = rnd * ROUND + r
                                k, t = u // KT, u % KT
                                if u == 0:
                                    pe.wait_ge(yw_ready, 1 + e * NC + b * CB)
                                pe.wait_ge(h_lo_ready, (e * NC + b * CB) * KT + u + 1)
                                sl = slice(w_down + t * P, w_down + (t + 1) * P)
                                mm = product3(pe, Y[k][:], e_hi[i][:, sl], e_lo[i][:, sl], h_hi[r][:], h_lo[r][:],
                                              start=t == 0, stop=t == KT - 1)
                                if t == KT - 1:
                                    mm.then_inc(y_full, 1)

                pe.wait_ge(gate.lo_ready, 1)
                pe.wait_ge(made, 6)
                lagged(pe, gates, turn_weights if not by_probs else lambda c: None)
                if by_probs:
                    pe.wait_ge(k_stepped, 1)
                    pe.matmul(Y[1][:, 0:E], ones[:], count8[:], start=True, stop=True).then_inc(k_full, 1)
                    each(pe, turn_weights)
                pe.wait_ge(comb_saved, NC)
                pe.wait_ge(g_stepped, STEPS * NC)
                experts(pe, expert)
                pe.wait_ge(yw_ready, 1 + NE * NC)

                def step(c, lag):
                    norm.pe_turn_y(pe, c, TY)
                    if lag is not None and not last:
                        norm.pe_turn_x(pe, lag, TX)
                lagged(pe, step, lambda c: None if last else norm.pe_turn_x(pe, c, TX))

            @block.scalar
            def _(act):
                def save_weights(c):
                    act.wait_ge(comb_turned, c + 1)
                    act.activation(comb_t[:, c, :], Y[0][:, 0:P], ACT.Copy).then_inc(comb_saved, 1)

                def gates(c, lag):
                    act.wait_ge(lg_full, c + 1)
                    wait(act, lg_turned, c)
                    act.activation(lg_t[:], TY[:], ACT.Identity, bias=gate.raw[:, G_BIAS:G_BIAS + 1]).then_inc(lg_staged, 1)
                    if lag is not None and not by_probs:
                        save_weights(lag)
                    if by_probs:
                        act.wait_ge(g_stepped, STEPS * c + 3)
                        act.activation(pr[:], d8[:], ACT.Exp).then_inc(g_exp, 1)
                    else:
                        act.wait_ge(g_stepped, STEPS * c + 4)
                        act.activation(e2[:, :, 0], d2[:, :, 0], ACT.Exp).then_inc(g_exp, 1)

                def expert(e, i):
                    func = ACT.Gelu if gelu else ACT.Relu
                    act.wait_ge(e_ready, e + 1)
                    with act.Fori(0, TURNS) as b:
                        for u in range(UNITS):
                            r, t = u % ROUND, u % KT
                            act.wait_ge(h_full, (e * NC + b * CB) * KT + u + 1)
                            act.activation(h[r][:], H[r][:], func, bias=e_bias[i][:, t:t + 1])
                            act.activation(h_hi[r][:], H[r][:], func, bias=e_bias[i][:, t:t + 1]).then_inc(h_hi_ready, 1)

                gate.act_split(act)
                act.activation(net.spare[:], gate.raw[:, 0:NB], ACT.Exp)
                lagged(act, gates, save_weights if not by_probs else lambda c: None)
                if by_probs:
                    with act.Fori(0, NC) as c:
                        save_weights(c)
                if gelu:
                    act.activation(net.spare[:, 0:1], gate.raw[:, 0:1], ACT.Gelu)
                experts(act, expert)
                act.wait_ge(acc_ready, 1 + NE * NC)

                def step(c, lag):
                    wait(act, norm.y_turned, c)
                    act.activation(net.y_stage[:], acc[:, at(c)], ACT.Copy).then_inc(norm.y_staged, 1)
                    if lag is not None and not last:
                        norm.act_hi(act, lag, TX)
                lagged(act, step, lambda c: None if last else norm.act_hi(act, c, TX))

            @block.vector
            def _(dve):
                def bc(ap):
                    return ap.unsqueeze(2).broadcast_to([P, NB, E])

                def gates(c, lag):
                    k = [0]

                    def link(ins):
                        k[0] += 1
                        ins.then_inc(g_stepped, 1)
                        dve.wait_ge(g_stepped, STEPS * c + k[0])
                        settle(dve, net)

                    dve.wait_ge(lg_turned, c + 1)
                    link(dve.tensor_copy(lg[:], tile3(TX[:])[:, :, 0:E]))
                    for j in range(NB):
                        ins = dve.max(top[:, j, :], lg[:, j, :])
                    link(ins)
                    if by_probs:
                        wait(dve, g_exp, c)
                        link(dve.tensor_tensor(d8[:], lg[:], bc(top[:, :, 0]), ALU.subtract))
                        dve.wait_ge(g_exp, c + 1)
                        link(dve.tensor_reduce(s1[:], pr[:], AX.X, ALU.add))
                        link(dve.reciprocal(r1[:], s1[:]))
                        link(dve.tensor_tensor(lg[:], pr[:], bc(r1[:]), ALU.mult))
                        for j in range(NB):
                            ins = dve.max(top[:, j, :], lg[:, j, :])
                        link(ins)
                    for j in range(NB):
                        ins = dve.max_index(idx[:, j, :], top[:, j, :], lg[:, j, :])
                    link(ins)
                    dve.tensor_copy(idxf[:], idx[:, :, 0:2])
                    if not by_probs:
                        wait(dve, g_exp, c)
                    link(dve.tensor_tensor(d2[:, :, 0], top[:, :, 1], top[:, :, 0], ALU.subtract))
                    for i in range(2):
                        ins = dve.tensor_tensor(oh[i][:], iota8[:], bc(idxf[:, :, i]), ALU.is_equal)
                    link(ins)
                    if by_probs:
                        w_first, w_second = top[:, :, 0], top[:, :, 1]
                    else:
                        dve.wait_ge(g_exp, c + 1)
                        link(dve.tensor_scalar(s1[:], e2[:, :, 0], 1.0, None, ALU.add))
                        link(dve.reciprocal(w2[:, :, 0], s1[:]))
                        link(dve.tensor_tensor(w2[:, :, 1], e2[:, :, 0], w2[:, :, 0], ALU.mult))
                        w_first, w_second = w2[:, :, 0], w2[:, :, 1]
                    dve.tensor_tensor(pick[0][:], oh[0][:], bc(w_first), ALU.mult)
                    link(dve.tensor_tensor(pick[1][:], oh[1][:], bc(w_second), ALU.mult))
                    if by_probs:
                        link(dve.tensor_tensor(comb_all[:, c, :].rearrange("p (j e) -> p j e", e=E), pick[0][:], pick[1][:], ALU.add))
                        link(dve.tensor_tensor(d8b[:], oh[0][:], oh[1][:], ALU.add))
                        link(dve.tensor_tensor(count[:], count[:], d8b[:].rearrange("p j e -> p (j e)"), ALU.add))
                        link(dve.nop())
                    else:
                        wait(dve, comb_turned, c)
                        dve.tensor_tensor(comb[:, 0:S].rearrange("p (j e) -> p j e", e=E), pick[0][:], pick[1][:],
                                          ALU.add).then_inc(comb_ready, 1)
                        dve.wait_ge(comb_ready, c + 1)
                        link(dve.nop())
                    assert k[0] == STEPS

                def expert(e, i):
                    with dve.Fori(0, TURNS) as b:
                        for rnd in range(UNITS // ROUND):
                            for r in range(ROUND):
                                dve.wait_ge(h_hi_ready, (e * NC + b * CB) * KT + rnd * ROUND + r + 1)
                                dve.tensor_tensor(h_lo[r][:], h[r][:], h_hi[r][:].bitcast(F32),
                                                  ALU.subtract).then_inc(h_lo_ready, 1)
                            for k in range(rnd * ROUND // KT, (rnd + 1) * ROUND // KT):
                                if k == 0:
                                    dve.wait_ge(acc_ready, 1 + e * NC + b * CB)
                                c = b * CB + k
                                dve.wait_ge(y_full, e * NC + c + 1)
                                dve.scalar_tensor_tensor(out=yw[k][:], in0=Y[k][:], scalar=e_bias[i][:, KT:KT + 1],
                                                         in1=wt[i][:, at(c)], op0=ALU.add, op1=ALU.mult).then_inc(yw_ready, 1)

                def expert_of_pair(q):
                    for i in range(2):
                        dve.wait_ge(wt_loaded[i], 16 * q + 16)
                        settle(dve, net)
                        expert(2 * q + i, i)

                dve.sem_inc(yw_ready, 1)
                gate.dve_split(dve)
                dve.wait_ge(made, 6)
                dve.wait_ge(iota_loaded, 16)
                lagged(dve, gates, lambda c: None)
                if by_probs:
                    dve.tensor_reduce(count8[:], count[:].rearrange("p (j e) -> p e j", e=E), AX.X, ALU.add).then_inc(k_stepped, 1)
                    dve.wait_ge(k_full, 1)
                    dve.tensor_scalar(keep[:], Y[1][:, 0:E], float(CAP), None, ALU.is_le).then_inc(k_stepped, 1)
                    dve.wait_ge(k_stepped, 2)

                    def weigh(c):
                        wait(dve, comb_turned, c)
                        dve.tensor_tensor(comb[:, 0:S].rearrange("p (j e) -> p j e", e=E),
                                          comb_all[:, c, :].rearrange("p (j e) -> p j e", e=E),
                                          keep[:].unsqueeze(1).broadcast_to([P, NB, E]), ALU.mult).then_inc(comb_ready, 1)
                    each(dve, weigh)
                with dve.Fori(0, E // 2) as q:
                    expert_of_pair(q)
                if shared:
                    dve.wait_ge(wt_loaded[0], 16 * (E // 2) + 16)
                    expert(E, 0)

                def step(c, lag):
                    norm.dve_norm(dve, c, TY)
                    norm.dve_scale(dve, c)
                    if lag is not None and not last:
                        norm.dve_lo(dve, lag, TX)
                lagged(dve, step, lambda c: None if last else norm.dve_lo(dve, c, TX))


def steps(nc, net):
    return [
        lambda: softmax_attention(nc, net, "L0_attn", True),
        lambda: experts_ffn(nc, net, "L0_ffn", P, False, True, 0),
        lambda: gated_recurrence(nc, net),
        lambda: ternary_ffn(nc, net),
        lambda: softmax_attention(nc, net, "L2_attn", False),
        lambda: experts_ffn(nc, net, "L2_ffn", HID, False, False, 0),
        lambda: linear_attention(nc, net),
        lambda: experts_ffn(nc, net, "L3_ffn", HID, True, False, 1, last=True),
    ]


def program(nc, dram):
    with Layer(nc) as ctx:
        net = Net(nc, ctx, dram)
        enter(nc, net)
        for layer in steps(nc, net):
            layer()


def layout(inputs):
    import numpy as np
    a = {k: np.asarray(v) for k, v in inputs.items()}
    f = np.float32
    out = {"x": np.ascontiguousarray(a["L0_attn_x"])}

    def column(v):
        return v.reshape(-1, P).T

    def stacked(wt, lower):
        s = np.zeros((wt.shape[0], GROUPS, GH, QUAD), f)
        v = wt.reshape(wt.shape[0], GROUPS, GH, DH)
        for i in range(3):
            s[:, :, :, i * DH:(i + 1) * DH] = v
        return s.reshape(wt.shape[0], GROUPS * P)

    def softmax_weights(pre, bias, scale):
        w = np.zeros((P, 2 * GROUPS * P + 2 * P + 11), f)
        w[:, 0:GROUPS * P] = stacked(a[pre + "Wq"].T, True)
        w[:, GROUPS * P:2 * GROUPS * P] = stacked(a[pre + "Wk"].T, False)
        w[:, 2 * GROUPS * P:2 * GROUPS * P + P] = a[pre + "Wv"].T
        w[:, 2 * GROUPS * P + P:2 * GROUPS * P + 2 * P] = a[pre + "Wo"].T
        b = 2 * GROUPS * P + 2 * P
        if bias:
            w[:, b:b + 4] = stacked(a[pre + "bq"][None, :], True).reshape(GROUPS, P).T
            w[:, b + 4:b + 8] = stacked(a[pre + "bk"][None, :], False).reshape(GROUPS, P).T
            w[:, b + 8] = a[pre + "bv"]
            w[:, b + 9] = a[pre + "bo"]
            w[:, b + 10] = a[pre + "attn_scale"][0]
        else:
            w[:, b + 10] = f(1.0) / np.sqrt(f(DH))
        for r in range(GH):
            w[QUAD * r + R_MAX:QUAD * r + K_MAX, b + 4:b + 8] = 1.0
        return w

    out["L0_attn_w"] = softmax_weights("L0_attn_", False, None)
    out["L2_attn_w"] = softmax_weights("L2_attn_", True, None)
    out["L1_attn_w"] = np.concatenate([a["L1_attn_W_in"], a["L1_attn_W_out"], column(a["L1_attn_b_in"]),
                                       column(a["L1_attn_b_out"])], axis=1)

    def tiles(wt):
        return wt.reshape(-1, P, wt.shape[1]).transpose(1, 0, 2).reshape(P, -1)

    out["L1_ffn_w"] = np.concatenate([a["L1_ffn_w1_w"].T, a["L1_ffn_w2_w"].T, tiles(a["L1_ffn_h1_w"].T),
                                      tiles(a["L1_ffn_h2_w"].T), tiles(a["L1_ffn_w3_w"].T)], axis=1)
    out["L1_ffn_scales"] = np.concatenate([column(a["L1_ffn_" + k]) for k in ("w1_s", "w2_s", "h1_s", "h2_s", "w3_s")], axis=1)
    block = np.zeros((HEADS, DH, HEADS, QUAD), f)
    for h in range(HEADS):
        block[h, :, h, :] = a["L3_attn_projection"][h].T
    out["L3_attn_w"] = np.concatenate([a["L3_attn_Wq"], a["L3_attn_Wk"], a["L3_attn_Wv"], a["L3_attn_Wo"],
                                       block.reshape(P, HEADS * QUAD)] +
                                      [column(a["L3_attn_" + k]) for k in ("bq", "bk", "bv", "bo")], axis=1)

    def gate(wt, b):
        g = np.zeros((P, P + 1), f)
        g[:, 0:E] = wt
        if b is not None:
            g[0:E, P] = b
        return g

    def experts(w1, b1, w2, b2):
        return np.concatenate([w1, np.stack([tiles(m) for m in w2]), b1.reshape(len(w1), -1, P).transpose(0, 2, 1),
                               b2.reshape(len(w1), P, 1)], axis=2)

    out["L0_ffn_gate"] = gate(a["L0_ffn_gate_w"].T, None)
    out["L0_ffn_w"] = experts(*[a["L0_ffn_" + k] for k in ("W1", "b1", "W2", "b2")])
    out["L2_ffn_gate"] = gate(a["L2_ffn_W_router"], a["L2_ffn_b_router"])
    out["L2_ffn_w"] = experts(*[a["L2_ffn_" + k] for k in ("W1", "b1", "W2", "b2")])
    out["L3_ffn_gate"] = gate(a["L3_ffn_gate_w"], a["L3_ffn_gate_b"])
    out["L3_ffn_w"] = np.concatenate(
        [experts(*[a["L3_ffn_" + k] for k in ("w1", "b1", "w2", "b2")]),
         experts(a["L3_ffn_ws1"][None], a["L3_ffn_bs1"][None], a["L3_ffn_ws2"][None], a["L3_ffn_bs2"][None])], axis=0)

    bf16 = mybir.dt.np(BF16)
    q, k = np.arange(P)[:, None], np.arange(P)[None, :]
    window = [np.where(ok, 0.0, NEG) for ok in (k <= q, k > q)]
    half = P // 2
    chunked = [np.where(((k // half == q // half) & (k <= q)) | (k // half > q // half), 0.0, NEG)] * 2
    for name, m in (("L0_attn_masks", window), ("L2_attn_masks", chunked)):
        out[name] = np.stack([m[0], m[1], m[0].T, m[1].T], axis=1).astype(bf16)
    out["ident"] = np.eye(P, dtype=f)
    out["ident16"] = np.eye(P).astype(bf16)
    c = np.zeros((P, 4), f)
    row = np.arange(P) % QUAD
    c[:, 0] = np.where((row >= DH) & (row < 2 * DH), -1.0, 0.0)
    c[:, 1] = np.where((row >= 2 * DH) & (row < 3 * DH), -1.0, 0.0)
    out["const"] = c
    iota = np.broadcast_to(np.arange(E, dtype=f), (P, NB, E)).copy()
    for name in ("L0_ffn_iota8", "L2_ffn_iota8", "L3_ffn_iota8"):
        out[name] = iota
    own = np.zeros((P, GROUPS, D + HEADS), f)
    for g in range(GROUPS):
        for p in range(P):
            h = GH * g + p // QUAD
            own[p, g, h * DH:(h + 1) * DH] = 1.0
            own[p, g, D + h] = 1.0
    out["L3_attn_own"] = own
    return {n: np.ascontiguousarray(v) for n, v in out.items()}


def build(nc, inputs):
    arrays, dram = {}, {}
    for name, v in layout(inputs).items():
        arrays[f"in_{name}"] = v
        ap = nc.dram_tensor(f"in_{name}", v.shape, mybir.dt.from_np(v.dtype), kind="ExternalInput").ap()
        if name[0] == "L":
            layer, part = name[:name.rindex("_")], name[name.rindex("_") + 1:]
            dram.setdefault(layer, {})[part] = ap
        else:
            dram[name] = ap
    dram["out"] = nc.dram_tensor("out_x", (BATCH, SEQ, D), F32, kind="ExternalOutput").ap()
    program(nc, dram)
    return arrays


def kernel(**inputs):
    import concourse.bacc as bacc
    from concourse.bass_utils import run_bass_kernel_spmd
    nc = bacc.Bacc("TRN2", target_bir_lowering=False, num_devices=1)
    arrays = build(nc, inputs)
    r = run_bass_kernel_spmd(nc, [arrays], core_ids=[0])
    return r.results[0]["out_x"]
```

```python
from contextlib import ExitStack

import numpy as np

import concourse.bass as bass
from concourse import mybir
from concourse.alu_op_type import AluOpType as ALU

F32 = mybir.dt.float32
F32R = mybir.dt.float32r
BF16 = mybir.dt.bfloat16
U32 = mybir.dt.uint32
ACT = mybir.ActivationFunctionType
AX = mybir.AxisListType

P = 128
D = 128
BATCH = 8
SEQ = 512
NC = BATCH
CH = SEQ
NB = CH // P
HEADS = 16
DH = D // HEADS
GROUPS = 4
GH = HEADS // GROUPS
QUAD = 32
E = 8
HID = 512
NEG = -1.0e30
EPS = 1e-5
R_MAX = 3 * DH
K_MAX = 3 * DH + 3


def wait(eng, sem, count):
    if isinstance(count, int) and count <= 0:
        return
    eng.wait_ge(sem, count)


def settle(eng, net):
    eng.sem_inc(net.settled, 1)


def at(c):
    return bass.ds(c * CH, CH)


def tile3(ap, n=NB):
    return ap.rearrange("p (j d) -> p j d", j=n)


class Layer(ExitStack):

    def __init__(self, nc):
        super().__init__()
        self.nc, self.sems = nc, []

    def sem(self, name):
        self.sems.append(self.nc.alloc_semaphore(name=name))
        return self.sems[-1]

    def __exit__(self, *failure):
        super().__exit__(*failure)
        self.nc.clear_and_free_semaphores(self.sems)
        self.nc.all_engine_barrier()


WEIGHTS = [("L0_attn", "w"), ("L0_ffn", "gate"), ("L1_attn", "w"), ("L1_ffn", "w"), ("L2_attn", "w"),
           ("L2_ffn", "gate"), ("L3_attn", "w"), ("L3_ffn", "gate")]


class Net:

    def __init__(self, nc, ctx, dram):
        self.nc, self.dram = nc, dram

        def sb(name, shape, dt=F32):
            return ctx.enter_context(nc.sbuf_tensor(name, shape, dt))

        self.settled = ctx.sem("settled")
        self.x_tok = sb("x_tok", [P, NC, CH])
        self.x_hi = sb("x_hi", [P, NC * CH], F32R)
        self.x_lo = sb("x_lo", [P, NC * CH], F32R)
        self.y_stage = sb("y_stage", [P, CH])
        self.res = sb("res", [P, CH])
        self.x_new = sb("x_new", [P, CH])
        self.stats = sb("stats", [P, NB, 6])
        self.mv = sb("mv", [P, NB, 2])
        self.ve = sb("ve", [P, NB])
        self.rstd = sb("rstd", [P, NB])
        self.m_half = sb("m_half", [P, NB])
        self.spare = sb("spare", [P, NB])
        self.ident = sb("ident", [P, P])
        self.ident16 = sb("ident16", [P, P], BF16)
        self.const = sb("const", [P, 4])
        self.raw, self.raw_loaded = {}, {}
        for layer, part in WEIGHTS:
            self.raw[layer] = sb(f"{layer}_raw", [P, dram[layer][part].shape[1]])
            self.raw_loaded[layer] = ctx.sem(f"{layer}_raw_loaded")


class Norm:

    STEPS = 3

    def __init__(self, nc, ctx, net, name, last=False, shared=None):
        self.nc, self.net, self.last, self.shared = nc, net, last, shared

        def sem(n):
            return ctx.sem(f"{name}_{n}")

        self.y_staged = sem("y_staged")
        self.y_turned = sem("y_turned")
        self.y_added = sem("y_added")
        self.stepped = sem("stepped")
        self.rstd_ready = sem("rstd_ready")
        self.xn_ready = sem("xn_ready")
        self.xn_turned = sem("xn_turned")
        self.hi_ready = sem("hi_ready")
        self.lo_ready = sem("lo_ready")
        self.x_saved = sem("x_saved")

    def turn(self, pe, src, bank):
        for j in range(NB):
            mm = pe.transpose(bank[:, j * P:(j + 1) * P], src[:, j * P:(j + 1) * P], self.net.ident[:])
        return mm

    def pe_turn_y(self, pe, c, bank, n=None):
        if n is None:
            pe.wait_ge(self.y_staged, c + 1)
            wait(pe, self.y_added, c)
            self.turn(pe, self.net.y_stage, bank).then_inc(self.y_turned, 1)
        else:
            full, free = self.shared
            pe.wait_ge(free, n)
            self.turn(pe, self.net.y_stage, bank).then_inc(full, 1)

    def dve_norm(self, dve, c, bank, n=None):
        net = self.net
        wait(dve, self.xn_ready, c)
        if n is None:
            dve.wait_ge(self.y_turned, c + 1)
            dve.tensor_tensor(net.res[:], bank[:], net.x_tok[:, c, :], ALU.add).then_inc(self.y_added, 1)
            dve.wait_ge(self.y_added, c + 1)
        else:
            full, free = self.shared
            dve.wait_ge(full, n + 1)
            dve.tensor_tensor(net.res[:], bank[:], net.x_tok[:, c, :], ALU.add).then_inc(free, 1)
            dve.wait_ge(free, n + 1)
        for j in range(NB):
            last = dve.bn_stats(net.stats[:, j, :], net.res[:, j * P:(j + 1) * P])
        last.then_inc(self.stepped, 1)
        dve.wait_ge(self.stepped, self.STEPS * c + 1)
        settle(dve, net)
        for j in range(NB):
            last = dve.bn_aggr(net.mv[:, j, :], net.stats[:, j, :])
        last.then_inc(self.stepped, 1)
        dve.wait_ge(self.stepped, self.STEPS * c + 2)
        wait(dve, self.rstd_ready, c)
        dve.tensor_scalar(net.ve[:], net.mv[:, :, 1], EPS, None, ALU.add).then_inc(self.stepped, 1)

    def pool_root(self, pool, c):
        net = self.net
        pool.wait_ge(self.stepped, self.STEPS * (c + 1))
        wait(pool, self.xn_ready, c)
        pool.tensor_tensor(net.rstd[:], net.ve[:], net.m_half[:, 0:NB], ALU.pow).then_inc(self.rstd_ready, 1)

    def dve_scale(self, dve, c):
        net = self.net
        dve.wait_ge(self.rstd_ready, c + 1)
        wait(dve, self.x_saved, 16 * c)
        if not self.last and self.shared is None:
            wait(dve, self.xn_turned, c)
        for j in range(NB):
            sl = slice(j * P, (j + 1) * P)
            last = dve.tensor_scalar(net.x_new[:, sl], net.res[:, sl], net.mv[:, j, 0:1], net.rstd[:, j:j + 1],
                                     ALU.subtract, ALU.mult)
        last.then_inc(self.xn_ready, 1)

    def pe_turn_x(self, pe, c, bank, n=None):
        pe.wait_ge(self.xn_ready, c + 1)
        if n is None:
            wait(pe, self.lo_ready, c)
            self.turn(pe, self.net.x_new, bank).then_inc(self.xn_turned, 1)
        else:
            full, free = self.shared
            pe.wait_ge(free, n)
            self.turn(pe, self.net.x_new, bank).then_inc(full, 1)

    def act_hi(self, act, c, bank, n=None):
        if n is None:
            act.wait_ge(self.xn_turned, c + 1)
        else:
            act.wait_ge(self.shared[0], n + 1)
        act.activation(self.net.x_hi[:, at(c)], bank[:], ACT.Copy).then_inc(self.hi_ready, 1)

    def dve_lo(self, dve, c, bank, n=None):
        net = self.net
        dve.wait_ge(self.hi_ready, c + 1)
        dve.tensor_tensor(net.x_lo[:, at(c)], bank[:], net.x_hi[:, at(c)].bitcast(F32),
                          ALU.subtract).then_inc(self.lo_ready if n is None else self.shared[1], 1)

    def sp_save(self, sp, c):
        net = self.net
        sp.wait_ge(self.xn_ready, c + 1)
        if self.last:
            dst = net.dram["out"][bass.ds(c, 1)].rearrange("a (j p) d -> p (a j) d", p=P)
            sp.dma_start(dst, tile3(net.x_new[:])).then_inc(self.x_saved, 16)
        else:
            sp.dma_start(net.x_tok[:, bass.ds(c, 1), :], net.x_new[:].rearrange("p (a n) -> p a n", a=1)
                         ).then_inc(self.x_saved, 16)

    def sp_end(self, sp):
        sp.wait_ge(self.x_saved, 16 * NC)


class Weights:

    def __init__(self, nc, ctx, net, name, width):
        self.width, self.raw, self.loaded = width, net.raw[name], net.raw_loaded[name]
        self.hi = ctx.enter_context(nc.sbuf_tensor(f"{name}_w_hi", [P, width], F32R))
        self.lo = ctx.enter_context(nc.sbuf_tensor(f"{name}_w_lo", [P, width], F32R))
        self.hi_ready = ctx.sem(f"{name}_w_hi_ready")
        self.lo_ready = ctx.sem(f"{name}_w_lo_ready")

    def act_split(self, act):
        act.wait_ge(self.loaded, 16)
        act.activation(self.hi[:], self.raw[:, 0:self.width], ACT.Copy).then_inc(self.hi_ready, 1)

    def dve_split(self, dve):
        dve.wait_ge(self.hi_ready, 1)
        dve.tensor_tensor(self.lo[:], self.raw[:, 0:self.width], self.hi[:].bitcast(F32),
                          ALU.subtract).then_inc(self.lo_ready, 1)


def product3(pe, out, w_hi, w_lo, x_hi, x_lo, start=True, stop=True):
    pe.matmul(out, w_hi, x_hi, start=start, stop=False)
    pe.matmul(out, w_hi, x_lo, start=False, stop=False)
    return pe.matmul(out, w_lo, x_hi, start=False, stop=stop)


def lagged(eng, body, tail):
    body(0, None)
    with eng.Fori(1, NC) as c:
        body(c, c - 1)
    tail(NC - 1)


def chunks(eng, before, body, after, first=1):
    before()
    for c in range(first):
        body(c, c - 1 if c else None, True)
    with eng.Fori(first, NC - 1) as c:
        body(c, c - 1, True)
    body(NC - 1, NC - 2, False)
    after()


def each(eng, body):
    body(0)
    with eng.Fori(1, NC) as c:
        body(c)


def enter(nc, net):
    BANKS = 4
    with Layer(nc) as ctx:
        sem = lambda n: ctx.sem(f"in_{n}")
        bank = [ctx.enter_context(nc.psum_tensor(f"in_bank{i}", [P, CH], F32)) for i in range(BANKS)]
        x_loaded = [sem(f"x_loaded{c}") for c in range(NC)]
        const_loaded, made = sem("const_loaded"), sem("made")
        turned, hi_ready, lo_ready = sem("turned"), sem("hi_ready"), sem("lo_ready")
        with nc.Block() as block:
            @block.sync
            def _(sp):
                sp.dma_start(net.ident[:], net.dram["ident"]).then_inc(const_loaded, 16)
                for c in range(NC):
                    sp.dma_start(tile3(net.x_tok[:, c, :]),
                                 net.dram["x"][c].rearrange("(j p) d -> p j d", p=P)).then_inc(x_loaded[c], 16)
                    if c == 0:
                        sp.dma_start(net.ident16[:], net.dram["ident16"]).then_inc(const_loaded, 16)
                        sp.dma_start(net.const[:], net.dram["const"]).then_inc(const_loaded, 16)
                    if c == NC // 2:
                        layer, part = WEIGHTS[0]
                        sp.dma_start(net.raw[layer][:], net.dram[layer][part]).then_inc(net.raw_loaded[layer], 16)

            @block.gpsimd
            def _(pool):
                pool.memset(net.m_half[:], -0.5).then_inc(made, 1)

            @block.tensor
            def _(pe):
                pe.wait_ge(const_loaded, 48)
                for c in range(NC):
                    pe.wait_ge(x_loaded[c], 16)
                    wait(pe, lo_ready, c - BANKS + 1)
                    for j in range(NB):
                        mm = pe.transpose(bank[c % BANKS][:, j * P:(j + 1) * P], net.x_tok[:, c, j * P:(j + 1) * P],
                                          net.ident[:])
                    mm.then_inc(turned, 1)

            @block.scalar
            def _(act):
                act.wait_ge(const_loaded, 48)
                act.activation(net.spare[:, 0:1], net.ident[:, 0:1], ACT.Copy)
                with act.Fori(0, NC // BANKS) as turn:
                    for i in range(BANKS):
                        c = turn * BANKS + i
                        act.wait_ge(turned, c + 1)
                        act.activation(net.x_hi[:, at(c)], bank[i][:], ACT.Copy).then_inc(hi_ready, 1)

            @block.vector
            def _(dve):
                with dve.Fori(0, NC // BANKS) as turn:
                    for i in range(BANKS):
                        c = turn * BANKS + i
                        dve.wait_ge(hi_ready, c + 1)
                        dve.tensor_tensor(net.x_lo[:, at(c)], bank[i][:], net.x_hi[:, at(c)].bitcast(F32),
                                          ALU.subtract).then_inc(lo_ready, 1)


def softmax_attention(nc, net, name, windowed):
    dram = net.dram[name]
    WQ, WK, WV, WO = 0, GROUPS * P, 2 * GROUPS * P, 2 * GROUPS * P + P
    WIDTH = WO + P
    BIAS = WIDTH
    if windowed:
        max_slots = [[(0, 0, 2, 0, 0, 1, [(0, 0)]), (1, 0, 2, 256, 0, 2, [(1, 256), (0, 384)])],
                     [(2, 1, 2, 0, 1, 2, [(1, 0), (0, 128)]), (3, 2, 2, 256, 2, 2, [(1, 256), (0, 384)])]]
        exp_slots = [[(0, 0, 2, 0, 0, 2, [(0, 0), (1, 128)]), (1, 1, 2, 256, 1, 2, [(0, 256), (1, 384)])],
                     [(3, 2, 2, 0, 3, 1, [(0, 128)]), (2, 2, 2, 256, 2, 2, [(0, 256), (1, 384)])]]
    else:
        max_slots = [[(0, 0, 4, 0, 0, 4, [(0, 0)])],
                     [(1, 1, 3, 0, 1, 3, [(0, 0)])],
                     [(2, 2, 2, 0, 2, 2, [(0, 0)]), (3, 2, 2, 256, 3, 1, [(0, 384)])]]
        exp_slots = [[(3, 0, 4, 0, 0, 4, [(0, 384)])],
                     [(2, 0, 3, 0, 0, 3, [(0, 256)])],
                     [(1, 0, 2, 0, 0, 2, [(0, 128)]), (0, 0, 2, 256, 0, 1, [(0, 256)])]]
    SLOTS = len(exp_slots)
    N = SLOTS * GH
    NP = 8
    NSE = 3
    NV = N // GH
    AT_PV = 1
    AT_START, AT_K, AT_Q, AT_O, AT_V, AT_END = 0, 0, 2, 3, 5, N - 1

    def ahead(s):
        return min(N, s + 2 + (s >= N // 2))

    EVENTS = {
        "A": dict(before=["K0", "Q0", "V", "K1", "Q1"],
                  body=["K2", "Q2", "K3", "Q3", "WO", "K0", "Q0", "V", "K1", "Q1"],
                  lag=["WO"], new=["K0", "Q0", "V", "K1", "Q1"], after=["WO"]),
        "B": dict(before=["VT", "T0"],
                  body=["O3", "T1", "AT", "O0", "T2", "Y", "O1", "T3", "X", "O2", "VT", "T0"],
                  lag=["O3", "AT", "Y", "X"], new=["VT", "T0"], after=["O3", "AT", "Y", "X"]),
    }

    def nth(bank, e, c):
        ev = EVENTS[bank]
        first = [x for x in ev["body"] if x not in ev["lag"]]
        if isinstance(c, int) and c == -1:
            return ev["before"].index(e)
        if isinstance(c, int) and c == 0:
            return len(ev["before"]) + first.index(e)
        done = len(ev["before"]) + len(first) + (c - 1) * len(ev["body"])
        if isinstance(c, int) and c == NC - 1:
            return done + [x for x in ev["body"] if x not in ev["new"]].index(e)
        if isinstance(c, int) and c == NC:
            return done - len(ev["new"]) + ev["after"].index(e)
        return done + ev["body"].index(e)

    with Layer(nc) as ctx:
        sb = lambda n, s, dt=F32: ctx.enter_context(nc.sbuf_tensor(f"{name}_{n}", s, dt))
        ps = lambda n, s: ctx.enter_context(nc.psum_tensor(f"{name}_{n}", s, F32))
        sem = lambda n: ctx.sem(f"{name}_{n}")
        w = Weights(nc, ctx, net, name, WIDTH)
        masks = sb("masks", [P, 4, P], BF16)
        q_bias = sb("q_bias", [P, GROUPS])
        v_t = sb("v_t", [P, CH])
        vals = sb("vals", [P, NB, HEADS, QUAD])
        v_last = sb("v_last", [P, NB, GH, DH])
        raw = [sb(f"raw{i}", [P, CH]) for i in range(2)]
        raw_hi = [sb(f"raw_hi{i}", [P, CH], F32R) for i in range(2)]
        q_st = [sb(f"q_st{i}", [P, CH], F32R) for i in range(2)]
        qm_st = [sb(f"qm_st{i}", [P, CH], F32R) for i in range(2)]
        k_st = [sb(f"k_st{i}", [P, CH], F32R) for i in range(2)]
        k_head = [sb(f"k_head{g}", [P, GH, CH], F32R) for g in range(GROUPS)]
        mx = sb("mx", [P, HEADS, NB])
        m_rest = sb("m_rest", [P, NB, GH])
        m_stage = sb("m_stage", [P, NB, P], BF16)
        probs = [sb(f"probs{i}", [P, CH]) for i in range(NP)]
        o_t = sb("o_t", [P, CH])
        rden = sb("rden", [P, NB * GH])
        attn = sb("attn", [P, CH])
        a_hi = sb("a_hi", [P, CH], F32R)
        a_lo = sb("a_lo", [P, CH], F32R)
        SM = [ps(f"SM{i}", [P, CH]) for i in range(2)]
        SE = [ps(f"SE{i}", [P, CH]) for i in range(NSE)]
        OT = ps("OT", [P, CH])
        BANK = {b: ps(f"bank_{b}", [P, CH]) for b in "AB"}
        A, B = BANK["A"], BANK["B"]

        masks_loaded, zeroed = sem("masks_loaded"), sem("zeroed")
        full = {b: sem(f"full_{b}") for b in "AB"}
        free = {b: sem(f"free_{b}") for b in "AB"}
        norm = Norm(nc, ctx, net, name, shared=(full["B"], free["B"]))
        split_ready = sem("split_ready")
        k_placed = [sem(f"k_placed{g}") for g in range(GROUPS)]
        smax_full, smax_read = sem("smax_full"), sem("smax_read")
        m_stepped, m_staged = sem("m_stepped"), sem("m_staged")
        sexp_full, exp_done, pv_done = sem("sexp_full"), sem("exp_done"), sem("pv_done")
        ot_read, rden_ready, attn_hi = sem("ot_read"), sem("rden_ready"), sem("attn_hi")
        bias_ready, v_ready = sem("bias_ready"), sem("v_ready")

        def mst(i):
            return m_stage[:, :, R_MAX + i:R_MAX + i + QUAD * (GH - 1) + 1:QUAD]

        def shifted(c, g, by):
            return c + (g + by) // GROUPS, (g + by) % GROUPS

        def start(i):
            return isinstance(i, int) and i == 0

        with nc.Block() as block:
            @block.sync
            def _(sp):
                def place(c, g):
                    i = c * GROUPS + g
                    if isinstance(c, int) and c == 0:
                        sp.wait_ge(zeroed, 4 + g)
                    sp.wait_ge(split_ready, 2 * i + 1)
                    for r in range(GH):
                        rows = slice(QUAD * r, QUAD * r + QUAD)
                        sp.dma_start(k_head[g][rows, r, :].bitcast(F32), k_st[g % 2][rows, :].bitcast(F32)).then_inc(k_placed[g], 16)

                def before():
                    place(0, 0)
                    place(0, 1)

                def body(c, lag, more):
                    for g in range(GROUPS):
                        if g < 2 or more:
                            place(*shifted(c, g, 2))
                        if g == 2 and lag is not None:
                            norm.sp_save(sp, lag)

                def after():
                    norm.sp_save(sp, NC - 1)

                sp.dma_start(masks[:], dram["masks"]).then_inc(masks_loaded, 16)
                chunks(sp, before, body, after)
                norm.sp_end(sp)

            @block.gpsimd
            def _(pool):
                pool.memset(m_stage[:], 0.0).then_inc(zeroed, 1)
                pool.memset(vals[:], 0.0).then_inc(zeroed, 1)
                pool.wait_ge(zeroed, 2)
                pool.memset(vals[:, :, :, DH:DH + 1], 1.0).then_inc(zeroed, 1)
                for g in range(GROUPS):
                    pool.memset(k_head[g][:].bitcast(F32), 0.0).then_inc(zeroed, 1)
                if name == WEIGHTS[0][0]:
                    for layer, part in WEIGHTS[1:]:
                        pool.dma_start(net.raw[layer][:], net.dram[layer][part]).then_inc(net.raw_loaded[layer], 16)
                each(pool, lambda c: norm.pool_root(pool, c))

            @block.tensor
            def _(pe):
                def claim(bank, e, c):
                    wait(pe, free[bank], nth(bank, e, c))

                def project(e, c, of, col):
                    claim("A", e, c)
                    product3(pe, A[:], w.hi[:, col:col + P], w.lo[:, col:col + P],
                             net.x_hi[:, at(of)], net.x_lo[:, at(of)]).then_inc(full["A"], 1)

                def turn(e, c, src):
                    claim("B", e, c)
                    for j in range(NB):
                        mm = pe.transpose(B[:, j * P:(j + 1) * P], src[:, j * P:(j + 1) * P], net.ident[:])
                    mm.then_inc(full["B"], 1)

                def max_slot(c, g, s):
                    r, slot = s // SLOTS, max_slots[s % SLOTS]
                    i = c * GROUPS + g
                    if s == 0:
                        pe.wait_ge(split_ready, 2 * i + 2)
                        pe.wait_ge(k_placed[g], 16 * GH * (c + 1))
                    if not start(i) or s >= 2:
                        pe.wait_ge(smax_read, i * N + s - 1)
                    for a, b0, nb, col, u0, nu, mk in slot:
                        pe.matmul(SM[s % 2][:, col:col + nb * P], q_st[g % 2][:, a * P:(a + 1) * P],
                                  k_head[g][:, r, b0 * P:(b0 + nb) * P], start=True, stop=False)
                        for k, (table, mcol) in enumerate(mk):
                            mm = pe.matmul(SM[s % 2][:, mcol:mcol + P], net.ident16[:], masks[:, table, :],
                                           start=False, stop=k == len(mk) - 1)
                    mm.then_inc(smax_full, 1)

                def exp_slot(c, g, s):
                    r, slot = s % GH, exp_slots[s // GH]
                    i = c * GROUPS + g
                    ago = NSE if s >= NSE or N % NSE == 0 else s + N - max(t for t in range(N) if t % NSE == s)
                    if s == 0:
                        if g == 0:
                            pe.wait_ge(free["B"], nth("B", "T0", c - 1) + 1)
                        else:
                            pe.wait_ge(free["B"], nth("B", f"T{g}", c) + 1)
                    if not start(i) or s >= NSE:
                        pe.wait_ge(exp_done, i * N + s - ago + 1)
                    for a, b0, nb, col, u0, nu, mk in slot:
                        pe.matmul(SE[s % NSE][:, col:col + nb * P], k_head[g][:, r, a * P:(a + 1) * P],
                                  qm_st[g % 2][:, b0 * P:(b0 + nb) * P], start=True, stop=False)
                        for k, (table, mcol) in enumerate(mk):
                            mm = pe.matmul(SE[s % NSE][:, mcol:mcol + P], net.ident16[:], masks[:, 2 + table, :],
                                           start=False, stop=k == len(mk) - 1)
                    mm.then_inc(sexp_full, 1)

                def pv_batch(c, g, b):
                    i = c * GROUPS + g
                    if b == 0:
                        wait(pe, ot_read, i)
                        if g == 0:
                            pe.wait_ge(free["B"], nth("B", "VT", c - 1) + 1)
                        if g == GROUPS - 1:
                            pe.wait_ge(v_ready, c + 1)
                    pe.wait_ge(exp_done, i * N + (b + 1) * GH)
                    slot = exp_slots[b]
                    for k, (a, b0, nb, col, u0, nu, mk) in enumerate(slot):
                        used = col + (u0 - b0) * P
                        for r in range(GH):
                            mm = pe.matmul(OT[QUAD * r:QUAD * r + QUAD, u0 * P:(u0 + nu) * P], vals[:, a, GH * g + r, :],
                                           probs[(g * N + b * GH + r) % NP][:, used:used + nu * P],
                                           start=b == 0 and k == 0, stop=b == NV - 1 and k == len(slot) - 1,
                                           skip_group_check=True, tile_position=(0, QUAD * r))
                    mm.then_inc(pv_done, 1)

                def turn_max(e, c, i):
                    claim("B", e, c)
                    pe.wait_ge(m_staged, i + 1)
                    for j in range(NB):
                        mm = pe.matmul(B[:, j * P:(j + 1) * P], m_stage[:, j, :], net.ident16[:], start=True, stop=True)
                    mm.then_inc(full["B"], 1)

                def turn_out(e, c, i):
                    pe.wait_ge(ot_read, i + 1)
                    turn(e, c, o_t)

                def turn_attn(c):
                    turn("AT", c, attn)

                def out_proj(c, c_at):
                    claim("A", "WO", c)
                    pe.wait_ge(free["B"], nth("B", "AT", c_at) + 1)
                    product3(pe, A[:], w.hi[:, WO:WO + P], w.lo[:, WO:WO + P], a_hi[:], a_lo[:]).then_inc(full["A"], 1)

                def turn_y(c, lag):
                    pe.wait_ge(free["A"], nth("A", "WO", c) + 1)
                    norm.pe_turn_y(pe, lag, B, nth("B", "Y", c))

                def before():
                    project("K0", -1, 0, WK)
                    project("Q0", -1, 0, WQ)
                    project("V", -1, 0, WV)
                    for s in range(N):
                        max_slot(0, 0, s)
                        if s == 1:
                            project("K1", -1, 0, WK + P)
                        if s == 3:
                            pe.wait_ge(free["A"], nth("A", "V", -1) + 1)
                            turn("VT", -1, v_t)
                            project("Q1", -1, 0, WQ + P)
                    turn_max("T0", -1, 0)

                def body(c, lag, more):
                    for g in range(GROUPS):
                        i = c * GROUPS + g
                        c1, g1 = shifted(c, g, 1)
                        c2, g2 = shifted(c, g, 2)
                        for s in range(N):
                            if g < 3 or more:
                                for m in range(ahead(s - 1) if s else 0, ahead(s)):
                                    max_slot(c1, g1, m)
                            exp_slot(c, g, s)
                            if s % GH == AT_PV:
                                if s > GH:
                                    pv_batch(c, g, s // GH - 1)
                                elif g:
                                    pv_batch(c, g - 1, NV - 1)
                                elif lag is not None:
                                    pv_batch(lag, GROUPS - 1, NV - 1)
                            if s == AT_START and g == 1 and lag is not None:
                                turn_attn(c)
                            if s == AT_START and g == 2 and lag is not None:
                                turn_y(c, lag)
                            if s == AT_START and g == 3 and lag is not None:
                                norm.pe_turn_x(pe, lag, B, nth("B", "X", c))
                            if s == AT_V and g == 3 and more:
                                pe.wait_ge(free["A"], nth("A", "V", c) + 1)
                                turn("VT", c, v_t)
                            if s == AT_Q and (g < 2 or more):
                                project(f"Q{g2}", c, c2, WQ + g2 * P)
                            if s == AT_O and (g or lag is not None):
                                turn_out(f"O{(g - 1) % GROUPS}", c, i - 1)
                            if s == AT_K and (g < 2 or more):
                                project(f"K{g2}", c, c2, WK + g2 * P)
                            if s == AT_O + 1 and g == 1 and lag is not None:
                                out_proj(c, c)
                            if s == AT_O + 1 and g == 2 and more:
                                project("V", c, c + 1, WV)
                            if s == AT_END and (g < 3 or more):
                                turn_max(f"T{g1}", c, i + 1)

                def after():
                    pv_batch(NC - 1, GROUPS - 1, NV - 1)
                    turn_out("O3", NC, NC * GROUPS - 1)
                    turn_attn(NC)
                    out_proj(NC, NC)
                    turn_y(NC, NC - 1)
                    norm.pe_turn_x(pe, NC - 1, B, nth("B", "X", NC))

                pe.wait_ge(w.lo_ready, 1)
                pe.wait_ge(masks_loaded, 16)
                pe.wait_ge(zeroed, 3)
                chunks(pe, before, body, after)

            @block.scalar
            def _(act):
                def take(bank, e, c):
                    act.wait_ge(full[bank], nth(bank, e, c) + 1)

                def values(c):
                    take("A", "V", c)
                    act.activation(v_t[:], A[:], ACT.Identity, bias=w.raw[:, BIAS + 8:BIAS + 9]).then_inc(free["A"], 1)

                def stage(e, c, i):
                    g, k = int(e[1]), int(e[0] == "K")
                    take("A", e, c)
                    if not start(i):
                        act.wait_ge(split_ready, 2 * i - k)
                    bias = w.raw[:, BIAS + 4 + g:BIAS + 5 + g] if k else q_bias[:, g:g + 1]
                    scale = 1.0 if k else w.raw[:, BIAS + 10:BIAS + 11]
                    act.activation(raw[k][:], A[:], ACT.Identity, bias=bias, scale=scale)
                    act.activation(raw_hi[k][:], A[:], ACT.Identity, bias=bias, scale=scale).then_inc(free["A"], 1)

                def exps(c, g, s):
                    slot, i = exp_slots[s // GH], c * GROUPS + g
                    lo = min(col + (u0 - b0) * P for _, b0, _, col, u0, _, _ in slot)
                    hi = max(col + (u0 - b0 + nu) * P for _, b0, _, col, u0, nu, _ in slot)
                    act.wait_ge(sexp_full, i * N + s + 1)
                    if not isinstance(i, int) or i * N + s >= NP:
                        act.wait_ge(pv_done, i * NV + (s - NP) // GH + 1)
                    act.activation(probs[(g * N + s) % NP][:, lo:hi], SE[s % NSE][:, lo:hi], ACT.Exp).then_inc(exp_done, 1)

                def outputs(i):
                    act.wait_ge(pv_done, (i + 1) * NV)
                    act.activation(o_t[:], OT[:], ACT.Copy).then_inc(ot_read, 1)

                def attn_upper(c):
                    take("B", "AT", c)
                    act.activation(a_hi[:], B[:], ACT.Copy).then_inc(attn_hi, 1)

                def y(c):
                    take("A", "WO", c)
                    act.activation(net.y_stage[:], A[:], ACT.Identity, bias=w.raw[:, BIAS + 9:BIAS + 10]
                                   ).then_inc(free["A"], 1)

                def before():
                    stage("K0", -1, 0)
                    stage("Q0", -1, 0)
                    values(-1)
                    stage("K1", -1, 1)
                    stage("Q1", -1, 1)

                def body(c, lag, more):
                    for g in range(GROUPS):
                        i = c * GROUPS + g
                        g2 = shifted(c, g, 2)[1]
                        for s in range(N):
                            if s == 2 and (g or lag is not None):
                                outputs(i - 1)
                            exps(c, g, s)
                            if s == AT_START and g == 1 and lag is not None:
                                attn_upper(c)
                            if s == AT_START and g == 3 and lag is not None:
                                norm.act_hi(act, lag, B, nth("B", "X", c))
                            if s == AT_Q and (g < 2 or more):
                                stage(f"Q{g2}", c, i + 2)
                            if s == AT_K and (g < 2 or more):
                                stage(f"K{g2}", c, i + 2)
                            if s == AT_O + 1 and g == 1 and lag is not None:
                                y(c)
                            if s == AT_O + 1 and g == 2 and more:
                                values(c)

                def after():
                    outputs(NC * GROUPS - 1)
                    attn_upper(NC)
                    y(NC)
                    norm.act_hi(act, NC - 1, B, nth("B", "X", NC))

                w.act_split(act)
                act.wait_ge(bias_ready, 1)
                act.activation(net.spare[:, 0:1], w.raw[:, 0:1], ACT.Exp)
                chunks(act, before, body, after)

            @block.vector
            def _(dve):
                def take(e, c):
                    dve.wait_ge(full["B"], nth("B", e, c) + 1)

                def values(c):
                    take("VT", c)
                    v4 = B[:].rearrange("p (j h d) -> p j h d", j=NB, d=DH)
                    n = GH * (GROUPS - 1)
                    dve.tensor_copy(vals[:, :, 0:n, 0:DH], v4[:, :, 0:n, :])
                    dve.tensor_copy(v_last[:], v4[:, :, n:, :]).then_inc(free["B"], 1)

                def values_last(before_c, i):
                    dve.wait_ge(free["B"], nth("B", "VT", before_c) + 1)
                    wait(dve, pv_done, i * NV)
                    dve.tensor_copy(vals[:, :, GH * (GROUPS - 1):, 0:DH], v_last[:]).then_inc(v_ready, 1)

                def split(e, c, placed=None):
                    g, k = int(e[1]), int(e[0] == "K")
                    dve.wait_ge(free["A"], nth("A", e, c) + 1)
                    if placed is not None:
                        dve.wait_ge(k_placed[placed[1]], 16 * GH * (placed[0] + 1))
                    dst = (k_st if k else q_st)[g % 2]
                    dve.scalar_tensor_tensor(out=dst[:], in0=raw_hi[k][:].bitcast(F32), scalar=net.const[:, k:k + 1],
                                             in1=raw[k][:], op0=ALU.mult, op1=ALU.add).then_inc(split_ready, 1)

                def maximum(c, g, s):
                    r, slot = s // SLOTS, max_slots[s % SLOTS]
                    i = c * GROUPS + g
                    dve.wait_ge(smax_full, i * N + s + 1)
                    if s == 0:
                        wait(dve, m_staged, i)
                    for a, b0, nb, col, u0, nu, mk in slot:
                        used = col + (u0 - b0) * P
                        last = dve.tensor_reduce(mx[:, GH * g + r, a:a + 1], SM[s % 2][:, used:used + nu * P],
                                                 AX.X, ALU.max)
                    last.then_inc(smax_read, 1)

                def stage_max(g, i):
                    mg = mx[:, GH * g:GH * g + GH, :].rearrange("p h j -> p j h")
                    dve.wait_ge(smax_read, (i + 1) * N)
                    dve.tensor_scalar(mst(0), mg, -1.0, None, ALU.mult).then_inc(m_stepped, 1)
                    dve.wait_ge(m_stepped, 3 * i + 1)
                    dve.scalar_tensor_tensor(out=m_rest[:], in0=mg, scalar=-1.0, in1=mst(0),
                                             op0=ALU.mult, op1=ALU.subtract).then_inc(m_stepped, 1)
                    dve.wait_ge(m_stepped, 3 * i + 2)
                    dve.tensor_copy(mst(1), m_rest[:]).then_inc(m_stepped, 1)
                    dve.wait_ge(m_stepped, 3 * i + 3)
                    dve.tensor_tensor(mst(2), m_rest[:], mst(1), ALU.subtract).then_inc(m_staged, 1)

                def add_max(e, c):
                    g = int(e[1])
                    take(e, c)
                    dve.tensor_tensor(qm_st[g % 2][:], q_st[g % 2][:].bitcast(F32), B[:], ALU.add).then_inc(free["B"], 1)

                def outputs(e, c, i):
                    g = int(e[1])
                    take(e, c)
                    o4 = B[:].rearrange("p (j r w) -> p j r w", j=NB, w=QUAD)
                    r3 = rden[:].rearrange("p (j r) -> p j r", r=GH)
                    dve.reciprocal(r3, o4[:, :, :, DH]).then_inc(rden_ready, 1)
                    dve.wait_ge(rden_ready, i + 1)
                    a4 = attn[:].rearrange("p (j g r d) -> p j g r d", j=NB, g=GROUPS, d=DH)[:, :, g]
                    dve.tensor_tensor(a4, o4[:, :, :, 0:DH], r3.unsqueeze(3).broadcast_to([P, NB, GH, DH]),
                                      ALU.mult).then_inc(free["B"], 1)

                def attn_lower(c, lag):
                    dve.wait_ge(attn_hi, lag + 1)
                    dve.tensor_tensor(a_lo[:], B[:], a_hi[:].bitcast(F32), ALU.subtract).then_inc(free["B"], 1)

                def before():
                    split("K0", -1)
                    split("Q0", -1)
                    for s in range(N):
                        maximum(0, 0, s)
                        if s == 2:
                            split("K1", -1)
                        if s == 4:
                            values(-1)
                            split("Q1", -1)
                    stage_max(0, 0)
                    add_max("T0", -1)

                def body(c, lag, more):
                    for g in range(GROUPS):
                        i = c * GROUPS + g
                        c1, g1 = shifted(c, g, 1)
                        g2 = shifted(c, g, 2)[1]
                        for s in range(N):
                            if g < 3 or more:
                                for m in range(ahead(s - 1) if s else 0, ahead(s)):
                                    maximum(c1, g1, m)
                                if ahead(s) == N and ahead(s - 1) < N:
                                    stage_max(g1, i + 1)
                            if s == AT_K + 1 and (g < 2 or more):
                                split(f"K{g2}", c, (c, g))
                            if s == AT_START + 1 and g == 1 and lag is not None:
                                attn_lower(c, lag)
                            if s == AT_START + 1 and g == 2 and lag is not None:
                                norm.dve_norm(dve, lag, B, nth("B", "Y", c))
                            if s == AT_V and g == 2 and lag is not None:
                                norm.dve_scale(dve, lag)
                            if s == AT_START + 1 and g == 3 and lag is not None:
                                norm.dve_lo(dve, lag, B, nth("B", "X", c))
                            if s == AT_V + 1 and g == 3 and more:
                                values(c)
                            if s == AT_Q + 1 and (g < 2 or more):
                                split(f"Q{g2}", c)
                            if s == 2 and g == 0:
                                values_last(c - 1 if lag is not None else -1, i)
                            if s == AT_O + 1 and (g or lag is not None):
                                outputs(f"O{(g - 1) % GROUPS}", c, i - 1)
                            if s == AT_END and (g < 3 or more):
                                add_max(f"T{g1}", c)
                def after():
                    outputs("O3", NC, NC * GROUPS - 1)
                    attn_lower(NC, NC - 1)
                    norm.dve_norm(dve, NC - 1, B, nth("B", "Y", NC))
                    norm.dve_scale(dve, NC - 1)
                    norm.dve_lo(dve, NC - 1, B, nth("B", "X", NC))

                w.dve_split(dve)
                dve.tensor_scalar(q_bias[:], w.raw[:, BIAS:BIAS + 4], w.raw[:, BIAS + 10:BIAS + 11], None,
                                  ALU.mult).then_inc(bias_ready, 1)
                dve.wait_ge(zeroed, 3)
                chunks(dve, before, body, after)


def gated_recurrence(nc, net):
    dram = net.dram["L1_attn"]
    WG, WH, WO = 0, P, 2 * P
    WIDTH = 3 * P
    BIAS = WIDTH
    with Layer(nc) as ctx:
        sb = lambda n, s, dt=F32: ctx.enter_context(nc.sbuf_tensor(f"rec_{n}", s, dt))
        ps = lambda n: ctx.enter_context(nc.psum_tensor(f"rec_{n}", [P, CH], F32))
        sem = lambda n: ctx.sem(f"rec_{n}")
        w = Weights(nc, ctx, net, "L1_attn", WIDTH)
        norm = Norm(nc, ctx, net, "rec")
        bias = sb("bias", [P, 3])
        t_gate, t_hid, hid = sb("t_gate", [P, CH]), sb("t_hid", [P, CH]), sb("hid", [P, CH])
        u, v, h = sb("u", [P, CH]), sb("v", [P, CH]), sb("h", [P, CH])
        h_hi, h_lo = sb("h_hi", [P, CH], F32R), sb("h_lo", [P, CH], F32R)
        decay = sb("decay", [P, CH])
        GATE, HIDB, OUT, TY, TX = ps("GATE"), ps("HIDB"), ps("OUT"), ps("TY"), ps("TX")
        made, bias_ready = sem("made"), sem("bias_ready")
        gate_full, hid_full, gate_read, hid_read = sem("gate_full"), sem("hid_full"), sem("gate_read"), sem("hid_read")
        u_ready, v_ready, h_ready = sem("u_ready"), sem("v_ready"), sem("h_ready")
        h_hi_ready, h_lo_ready, out_full = sem("h_hi_ready"), sem("h_lo_ready"), sem("out_full")
        with nc.Block() as block:
            @block.sync
            def _(sp):
                with sp.Fori(0, NC) as c:
                    norm.sp_save(sp, c)
                norm.sp_end(sp)

            @block.gpsimd
            def _(pool):
                pool.memset(decay[:], 0.9).then_inc(made, 1)
                each(pool, lambda c: norm.pool_root(pool, c))

            @block.tensor
            def _(pe):
                def gates(c):
                    xh, xl = net.x_hi[:, at(c)], net.x_lo[:, at(c)]
                    wait(pe, gate_read, c)
                    product3(pe, GATE[:], w.hi[:, WG:WG + P], w.lo[:, WG:WG + P], xh, xl).then_inc(gate_full, 1)
                    wait(pe, hid_read, c)
                    product3(pe, HIDB[:], w.hi[:, WH:WH + P], w.lo[:, WH:WH + P], xh, xl).then_inc(hid_full, 1)

                def body(c, lag, more):
                    if more:
                        gates(c + 1)
                    if lag is not None:
                        norm.pe_turn_y(pe, lag, TY)
                    pe.wait_ge(h_lo_ready, c + 1)
                    wait(pe, norm.y_staged, c)
                    product3(pe, OUT[:], w.hi[:, WO:WO + P], w.lo[:, WO:WO + P], h_hi[:], h_lo[:]).then_inc(out_full, 1)
                    if lag is not None:
                        norm.pe_turn_x(pe, lag, TX)

                def after():
                    norm.pe_turn_y(pe, NC - 1, TY)
                    norm.pe_turn_x(pe, NC - 1, TX)

                pe.wait_ge(w.lo_ready, 1)
                chunks(pe, lambda: gates(0), body, after, first=2)

            @block.scalar
            def _(act):
                def gates(c):
                    act.wait_ge(gate_full, c + 1)
                    wait(act, v_ready, c)
                    act.activation(t_gate[:], GATE[:], ACT.Tanh, bias=bias[:, 0:1], scale=0.5).then_inc(gate_read, 1)
                    act.wait_ge(hid_full, c + 1)
                    act.activation(t_hid[:], HIDB[:], ACT.Tanh, bias=bias[:, 1:2], scale=0.5)
                    act.activation(hid[:], HIDB[:], ACT.Identity, bias=bias[:, 2:3], scale=0.025).then_inc(hid_read, 1)

                def body(c, lag, more):
                    act.wait_ge(h_ready, c + 1)
                    wait(act, out_full, c)
                    act.activation(h_hi[:], h[:], ACT.Copy).then_inc(h_hi_ready, 1)
                    if more:
                        gates(c + 1)
                    act.wait_ge(out_full, c + 1)
                    wait(act, norm.y_turned, c)
                    act.activation(net.y_stage[:], OUT[:], ACT.Identity,
                                   bias=w.raw[:, BIAS + 2:BIAS + 3]).then_inc(norm.y_staged, 1)
                    if lag is not None:
                        norm.act_hi(act, lag, TX)

                w.act_split(act)
                act.wait_ge(bias_ready, 1)
                act.activation(net.spare[:, 0:1], bias[:, 0:1], ACT.Tanh)
                chunks(act, lambda: gates(0), body, lambda: norm.act_hi(act, NC - 1, TX), first=2)

            @block.vector
            def _(dve):
                def body(c, lag, more):
                    dve.wait_ge(gate_read, c + 1)
                    dve.wait_ge(hid_read, c + 1)
                    dve.scalar_tensor_tensor(out=u[:], in0=t_hid[:], scalar=1.0, in1=hid[:],
                                             op0=ALU.add, op1=ALU.mult).then_inc(u_ready, 1)
                    dve.wait_ge(u_ready, c + 1)
                    dve.scalar_tensor_tensor(out=v[:], in0=t_gate[:], scalar=1.0, in1=u[:],
                                             op0=ALU.add, op1=ALU.mult).then_inc(v_ready, 1)
                    dve.wait_ge(v_ready, c + 1)
                    wait(dve, h_hi_ready, c)
                    dve.tensor_tensor_scan(h[:], decay[:], v[:], 0.0, ALU.mult, ALU.add).then_inc(h_ready, 1)
                    if not (isinstance(c, int) and c < 2):
                        norm.dve_lo(dve, c - 2, TX)
                    if lag is not None:
                        norm.dve_norm(dve, lag, TY)
                    dve.wait_ge(h_hi_ready, c + 1)
                    wait(dve, out_full, c)
                    dve.tensor_tensor(h_lo[:], h[:], h_hi[:].bitcast(F32), ALU.subtract).then_inc(h_lo_ready, 1)
                    if lag is not None:
                        norm.dve_scale(dve, lag)

                def after():
                    norm.dve_lo(dve, NC - 2, TX)
                    norm.dve_norm(dve, NC - 1, TY)
                    norm.dve_scale(dve, NC - 1)
                    norm.dve_lo(dve, NC - 1, TX)

                w.dve_split(dve)
                dve.tensor_scalar(bias[:, 0:2], w.raw[:, BIAS:BIAS + 2], 0.5, None, ALU.mult)
                dve.tensor_scalar(bias[:, 2:3], w.raw[:, BIAS + 1:BIAS + 2], 0.025, None, ALU.mult).then_inc(bias_ready, 1)
                dve.wait_ge(made, 1)
                chunks(dve, lambda: None, body, after, first=2)


def ternary_ffn(nc, net):
    dram = net.dram["L1_ffn"]
    KT = HID // P
    W1, W2 = 0, HID
    H1, H2 = 2 * HID, 2 * HID + KT * HID
    W3 = 2 * HID + 2 * KT * HID
    WIDTH = W3 + KT * P
    S1, S2, SH1, SH2, S3 = 0, KT, 2 * KT, 3 * KT, 4 * KT
    UNITS = 3 * KT
    HALF = KT // 2
    FIRST, HIDDEN1, HIDDEN2 = range(3)
    with Layer(nc) as ctx:
        sb = lambda n, s, dt=F32: ctx.enter_context(nc.sbuf_tensor(f"ter_{n}", s, dt))
        ps = lambda n: ctx.enter_context(nc.psum_tensor(f"ter_{n}", [P, CH], F32))
        sem = lambda n: ctx.sem(f"ter_{n}")
        norm = Norm(nc, ctx, net, "ter")
        w_hi, w_lo = sb("w_hi", [P, WIDTH], F32R), sb("w_lo", [P, WIDTH], F32R)
        PIECES = [(0, H1), (H1, H2), (H2, W3), (W3, WIDTH)]
        w_raw = net.raw["L1_ffn"]
        scales = sb("scales", [P, 4 * KT + 1])
        half = sb("half", [P, KT])
        both = sb("both", [P, KT])
        t_silu = [sb(f"t_silu{i}", [P, CH]) for i in range(2)]
        silu = [sb(f"silu{i}", [P, CH]) for i in range(2)]
        hid = [sb(f"hid{i}", [P, CH]) for i in range(2)]
        h_hi = [sb(f"h_hi{i}", [P, KT, CH], F32R) for i in range(3)]
        h_lo = [sb(f"h_lo{i}", [P, KT, CH], F32R) for i in range(3)]
        W1B, W2B = ps("W1B"), ps("W2B")
        B = [ps(f"B{i}") for i in range(KT)]
        OUT, TX = ps("OUT"), ps("TX")
        scales_loaded, w_hi_ready, w_lo_ready, half_ready = (sem("scales_loaded"), sem("w_hi_ready"),
                                                             sem("w_lo_ready"), sem("half_ready"))
        a_full, b_full, tanh_ready = sem("a_full"), sem("b_full"), sem("tanh_ready")
        silu_ready, hid_made = sem("silu_ready"), sem("hid_made")
        g_full, g_made = sem("g_full"), sem("g_made")
        hi_made, lo_made, out_full = sem("hi_made"), sem("lo_made"), sem("out_full")

        def nth(layer, c, t):
            if layer == FIRST:
                if isinstance(c, int) and c == 0:
                    return t
                return KT + UNITS * (c - 1) + (t if t < HALF else KT + t)
            half = 0 if isinstance(c, int) and c == NC - 1 else HALF
            return KT + UNITS * c + t + (half if layer == HIDDEN1 else KT + 2 * half)

        with nc.Block() as block:
            @block.sync
            def _(sp):
                sp.dma_start(scales[:], dram["scales"]).then_inc(scales_loaded, 16)
                with sp.Fori(0, NC) as c:
                    norm.sp_save(sp, c)
                norm.sp_end(sp)

            @block.gpsimd
            def _(pool):
                each(pool, lambda c: norm.pool_root(pool, c))

            @block.tensor
            def _(pe):
                def first(c, t):
                    xh, xl = net.x_hi[:, at(c)], net.x_lo[:, at(c)]
                    wait(pe, silu_ready, KT * c + t)
                    col = W1 + t * P
                    product3(pe, W1B[:], w_hi[:, col:col + P], w_lo[:, col:col + P], xh, xl).then_inc(a_full, 1)
                    wait(pe, hid_made, KT * c + t)
                    col = W2 + t * P
                    product3(pe, W2B[:], w_hi[:, col:col + P], w_lo[:, col:col + P], xh, xl).then_inc(b_full, 1)

                def hidden(c, layer, lag, more):
                    base = (H1, H2)[layer - 1]
                    for k in range(KT):
                        pe.wait_ge(lo_made, nth(layer - 1, c, k) + 1)
                        for t in range(KT):
                            if k == 0:
                                if layer == HIDDEN2:
                                    pe.wait_ge(g_made, 2 * KT * c + t + 1)
                                elif not (isinstance(c, int) and c == 0):
                                    pe.wait_ge(g_made, 2 * KT * c - KT + t + 1)
                            col = base + k * HID + t * P
                            mm = product3(pe, B[t][:], w_hi[:, col:col + P], w_lo[:, col:col + P],
                                          h_hi[layer - 1][:, k, :], h_lo[layer - 1][:, k, :], start=k == 0, stop=k == KT - 1)
                            if k == KT - 1:
                                mm.then_inc(g_full, 1)
                        if k == 0 and layer == HIDDEN2 and lag is not None:
                            norm.pe_turn_y(pe, lag, OUT)
                        if k < HALF and more:
                            first(c + 1, HALF * (layer - 1) + k)
                        if k == HALF and layer == HIDDEN1 and lag is not None:
                            out(lag)

                def out(c):
                    wait(pe, norm.y_added, c)
                    for k in range(KT):
                        pe.wait_ge(lo_made, nth(HIDDEN2, c, k) + 1)
                        col = W3 + k * P
                        mm = product3(pe, OUT[:], w_hi[:, col:col + P], w_lo[:, col:col + P],
                                      h_hi[HIDDEN2][:, k, :], h_lo[HIDDEN2][:, k, :], start=k == 0, stop=k == KT - 1)
                    mm.then_inc(out_full, 1)

                def before():
                    pe.wait_ge(w_lo_ready, 1)
                    for k in range(KT):
                        first(0, k)

                def body(c, lag, more):
                    if lag is None:
                        pe.wait_ge(w_lo_ready, 2)
                    hidden(c, HIDDEN1, lag, more)
                    if lag is None:
                        pe.wait_ge(w_lo_ready, 3)
                    hidden(c, HIDDEN2, lag, more)
                    if lag is not None:
                        norm.pe_turn_x(pe, lag, TX)
                    else:
                        pe.wait_ge(w_lo_ready, 4)

                def after():
                    out(NC - 1)
                    norm.pe_turn_y(pe, NC - 1, OUT)
                    norm.pe_turn_x(pe, NC - 1, TX)

                chunks(pe, before, body, after)

            @block.scalar
            def _(act):
                def upper(layer, c, t):
                    if layer == FIRST:
                        act.wait_ge(hid_made, KT * c + t + 1)
                    else:
                        act.wait_ge(g_made, 2 * KT * c + KT * (layer - 1) + t + 1)
                    act.activation(h_hi[layer][:, t, :], hid[t % 2][:], ACT.Copy).then_inc(hi_made, 1)

                def first(c, t):
                    act.wait_ge(a_full, KT * c + t + 1)
                    if not (isinstance(c, int) and c == 0 and t < 2):
                        act.wait_ge(silu_ready, KT * c + t - 1)
                    act.activation(t_silu[t % 2][:], W1B[:], ACT.Tanh, scale=half[:, t:t + 1]).then_inc(tanh_ready, 1)
                    upper(FIRST, c, t)

                def hidden(c, layer):
                    for t in range(KT):
                        act.wait_ge(g_full, 2 * KT * c + KT * (layer - 1) + t + 1)
                        act.wait_ge(lo_made, nth(layer, c, t) - 1)
                        act.activation(hid[t % 2][:], B[t][:], ACT.Gelu,
                                       scale=scales[:, KT * (layer + 1) + t:KT * (layer + 1) + t + 1]).then_inc(g_made, 1)
                        upper(layer, c, t)

                def y(c):
                    act.wait_ge(out_full, c + 1)
                    wait(act, norm.y_turned, c)
                    act.activation(net.y_stage[:], OUT[:], ACT.Copy, scale=scales[:, S3:S3 + 1]).then_inc(norm.y_staged, 1)

                def before():
                    for t in range(KT):
                        first(0, t)

                def body(c, lag, more):
                    if more:
                        first(c + 1, 0)
                        first(c + 1, 1)
                    if lag is not None:
                        y(lag)
                    hidden(c, HIDDEN1)
                    if more:
                        first(c + 1, 2)
                        first(c + 1, 3)
                    hidden(c, HIDDEN2)
                    if lag is not None:
                        norm.act_hi(act, lag, TX)

                def after():
                    y(NC - 1)
                    norm.act_hi(act, NC - 1, TX)

                act.wait_ge(net.raw_loaded["L1_ffn"], 16)
                for a, b in PIECES:
                    act.activation(w_hi[:, a:b], w_raw[:, a:b], ACT.Copy).then_inc(w_hi_ready, 1)
                act.wait_ge(half_ready, 1)
                act.activation(net.spare[:, 0:1], half[:, 0:1], ACT.Gelu)
                chunks(act, before, body, after)

            @block.vector
            def _(dve):
                def lower(layer, c, t):
                    dve.wait_ge(hi_made, nth(layer, c, t) + 1)
                    dve.tensor_tensor(h_lo[layer][:, t, :], hid[t % 2][:], h_hi[layer][:, t, :].bitcast(F32),
                                      ALU.subtract).then_inc(lo_made, 1)

                def first(c, t):
                    dve.wait_ge(tanh_ready, KT * c + t + 1)
                    if not (isinstance(c, int) and c == 0 and t < 2):
                        dve.wait_ge(hid_made, KT * c + t - 1)
                    dve.scalar_tensor_tensor(out=silu[t % 2][:], in0=t_silu[t % 2][:], scalar=1.0,
                                             in1=W1B[:], op0=ALU.add, op1=ALU.mult).then_inc(silu_ready, 1)
                    dve.wait_ge(b_full, KT * c + t + 1)
                    dve.wait_ge(silu_ready, KT * c + t + 1)
                    wait(dve, lo_made, nth(FIRST, c, t) - 1)
                    dve.scalar_tensor_tensor(out=hid[t % 2][:], in0=W2B[:], scalar=both[:, t:t + 1],
                                             in1=silu[t % 2][:], op0=ALU.mult, op1=ALU.mult).then_inc(hid_made, 1)
                    lower(FIRST, c, t)

                def before():
                    for t in range(KT):
                        first(0, t)

                def body(c, lag, more):
                    if more:
                        first(c + 1, 0)
                        first(c + 1, 1)
                    for t in range(KT):
                        lower(HIDDEN1, c, t)
                    if lag is not None:
                        norm.dve_norm(dve, lag, OUT)
                    if more:
                        first(c + 1, 2)
                        first(c + 1, 3)
                    if lag is not None:
                        norm.dve_scale(dve, lag)
                    for t in range(KT):
                        lower(HIDDEN2, c, t)
                    if lag is not None:
                        norm.dve_lo(dve, lag, TX)

                def after():
                    norm.dve_norm(dve, NC - 1, OUT)
                    norm.dve_scale(dve, NC - 1)
                    norm.dve_lo(dve, NC - 1, TX)

                dve.wait_ge(scales_loaded, 16)
                dve.tensor_scalar(half[:], scales[:, S1:S1 + KT], 0.5, None, ALU.mult).then_inc(half_ready, 1)
                dve.wait_ge(half_ready, 1)
                dve.tensor_tensor(both[:], half[:], scales[:, S2:S2 + KT], ALU.mult).then_inc(half_ready, 1)
                dve.wait_ge(half_ready, 2)
                for i, (a, b) in enumerate(PIECES):
                    dve.wait_ge(w_hi_ready, i + 1)
                    dve.tensor_tensor(w_lo[:, a:b], w_raw[:, a:b], w_hi[:, a:b].bitcast(F32),
                                      ALU.subtract).then_inc(w_lo_ready, 1)
                chunks(dve, before, body, after)


def linear_attention(nc, net):
    dram = net.dram["L3_attn"]
    FEATS = 32
    FW = GH * FEATS
    VW = D + HEADS
    YAT = 0.1
    WQ, WK, WV, WO, WP = 0, P, 2 * P, 3 * P, 4 * P
    WIDTH = WP + GROUPS * FW
    BIAS = WIDTH
    AT_, WO_, Y_, X_ = range(4)
    with Layer(nc) as ctx:
        sb = lambda n, s, dt=F32: ctx.enter_context(nc.sbuf_tensor(f"lin_{n}", s, dt))
        ps = lambda n: ctx.enter_context(nc.psum_tensor(f"lin_{n}", [P, CH], F32))
        sem = lambda n: ctx.sem(f"lin_{n}")
        w = Weights(nc, ctx, net, "L3_attn", WIDTH)
        own = sb("own", [P, GROUPS, VW])
        qkv_t = [sb(f"qkv_t{i}", [P, CH]) for i in range(3)]
        sq = [sb(f"sq{i}", [P, CH]) for i in range(2)]
        ss, nrm, nrm_e, rinv = (sb("ss", [P, 2 * NB * HEADS]), sb("nrm", [P, 2 * NB * HEADS]),
                                sb("nrm_e", [P, 2 * NB * HEADS]), sb("rinv", [P, 2 * NB * HEADS]))
        root, root_g = sb("root", [P, 2 * NB * HEADS]), sb("root_g", [P, 2 * NB * HEADS])
        N_STEPS = 6
        normed = [sb(f"normed{i}", [P, CH]) for i in range(2)]
        n_hi = [sb(f"n_hi{i}", [P, CH], F32R) for i in range(2)]
        n_lo = [sb(f"n_lo{i}", [P, CH], F32R) for i in range(2)]
        vals = sb("vals", [P, NB, VW])
        k_feat = sb("k_feat", [P, NB, GROUPS * FW])
        q_feat = sb("q_feat", [P, GROUPS, CH])
        kv = sb("kv", [P, GROUPS, VW])
        den, rden = sb("den", [P, NB, HEADS]), sb("rden", [P, NB, HEADS])
        attn = sb("attn", [P, CH])
        a_hi, a_lo = sb("a_hi", [P, CH], F32R), sb("a_lo", [P, CH], F32R)
        A = [ps(f"A{i}") for i in range(3)]
        F = [ps(f"F{i}") for i in range(2)]
        KV = [ps(f"KV{i}") for i in range(2)]
        TB = ps("TB")
        norm_sems = sem("tb_full"), sem("tb_free")
        tb_full, tb_free = norm_sems
        norm = Norm(nc, ctx, net, "lin", shared=norm_sems)
        own_loaded, ones_made = sem("own_loaded"), sem("ones_made")
        proj_full, staged, turned = sem("proj_full"), sem("staged"), sem("turned")
        sq_ready, ss_ready, root_ready, n_stepped = sem("sq_ready"), sem("ss_ready"), sem("root_ready"), sem("n_stepped")
        normed_ready, vals_ready, back, n_hi_ready, n_lo_ready = (sem("normed_ready"), sem("vals_ready"), sem("back"),
                                                                  sem("n_hi_ready"), sem("n_lo_ready"))
        kf_full, kf_ready, qf_full, qf_ready = sem("kf_full"), sem("kf_ready"), sem("qf_full"), sem("qf_ready")
        kv_full, kv_ready, o_full, o_stepped, attn_ready, attn_hi = (sem("kv_full"), sem("kv_ready"), sem("o_full"),
                                                                     sem("o_stepped"), sem("attn_ready"), sem("attn_hi"))
        def two_before(c):
            return None if isinstance(c, int) and c < 2 else c - 2

        with nc.Block() as block:
            @block.sync
            def _(sp):
                sp.dma_start(own[:], dram["own"]).then_inc(own_loaded, 16)
                with sp.Fori(0, NC) as c:
                    norm.sp_save(sp, c)
                norm.sp_end(sp)

            @block.gpsimd
            def _(pool):
                pool.memset(vals[:, :, D:VW], 1.0).then_inc(ones_made, 1)

                each(pool, lambda c: norm.pool_root(pool, c))

            @block.tensor
            def _(pe):
                def turn(src, bank):
                    for j in range(NB):
                        mm = pe.transpose(bank[:, j * P:(j + 1) * P], src[:, j * P:(j + 1) * P], net.ident[:])
                    return mm

                def attn_t(lag):
                    pe.wait_ge(attn_ready, 2 * (lag + 1))
                    wait(pe, tb_free, 4 * lag)
                    turn(attn, TB).then_inc(tb_full, 1)

                def out_proj(lag):
                    pe.wait_ge(tb_free, 4 * lag + WO_)
                    product3(pe, TB[:], w.hi[:, WO:WO + P], w.lo[:, WO:WO + P], a_hi[:], a_lo[:]).then_inc(tb_full, 1)

                def project(c):
                    for i, col in enumerate((WQ, WK, WV)):
                        if i < 2:
                            wait(pe, n_lo_ready, 2 * c)
                        else:
                            wait(pe, vals_ready, c)
                        product3(pe, A[i][:], w.hi[:, col:col + P], w.lo[:, col:col + P],
                                 net.x_hi[:, at(c)], net.x_lo[:, at(c)]).then_inc(proj_full, 1)

                def to_tokens(c):
                    for i in range(3):
                        pe.wait_ge(staged, 3 * c + i + 1)
                        turn(qkv_t[i], A[i]).then_inc(turned, 1)

                def to_features(c):
                    for i in range(2):
                        pe.wait_ge(normed_ready, 2 * c + i + 1)
                        turn(normed[i], A[i]).then_inc(back, 1)

                def features_of_k(c):
                    pe.wait_ge(n_lo_ready, 2 * c + 2)
                    for j in range(NB):
                        if j < 2:
                            wait(pe, qf_ready, GROUPS * c)
                        else:
                            pe.wait_ge(kf_ready, NB * c + j - 1)
                        sl = slice(j * P, (j + 1) * P)
                        ph, pl = w.hi[:, WP:WIDTH], w.lo[:, WP:WIDTH]
                        pe.matmul(F[j % 2][:], n_hi[1][:, sl], ph, start=True, stop=False)
                        pe.matmul(F[j % 2][:], n_lo[1][:, sl], ph, start=False, stop=False)
                        pe.matmul(F[j % 2][:], n_hi[1][:, sl], pl, start=False, stop=True).then_inc(kf_full, 1)

                def features_of_q(c):
                    for g in range(GROUPS):
                        if g < 2:
                            pe.wait_ge(kf_ready, NB * c + NB - 1 + g)
                        else:
                            pe.wait_ge(qf_ready, GROUPS * c + g - 1)
                        col = WP + g * FW
                        product3(pe, F[g % 2][:], w.hi[:, col:col + FW], w.lo[:, col:col + FW],
                                 n_hi[0][:], n_lo[0][:]).then_inc(qf_full, 1)

                def keys_values(c):
                    pe.wait_ge(vals_ready, c + 1)
                    pe.wait_ge(kf_ready, NB * (c + 1))
                    wait(pe, attn_ready, 2 * c)
                    for g in range(GROUPS):
                        for j in range(NB):
                            mm = pe.matmul(KV[g // 2][:, (g % 2) * VW:(g % 2 + 1) * VW], k_feat[:, j, g * FW:(g + 1) * FW],
                                           vals[:, j, :], start=j == 0, stop=j == NB - 1)
                        if g % 2:
                            mm.then_inc(kv_full, 1)

                def outputs(c):
                    pe.wait_ge(kv_ready, 2 * c + 2)
                    pe.wait_ge(qf_ready, GROUPS * (c + 1))
                    for j in range(NB):
                        for g in range(GROUPS):
                            mm = pe.matmul(KV[j // 2][:, (j % 2) * VW:(j % 2 + 1) * VW], q_feat[:, g, j * P:(j + 1) * P],
                                           kv[:, g, :], start=g == 0, stop=g == GROUPS - 1)
                        if j % 2:
                            mm.then_inc(o_full, 1)

                def before():
                    project(0)
                    to_tokens(0)
                    to_features(0)

                def body(c, lag, more):
                    lag2 = two_before(c)
                    features_of_k(c)
                    if more:
                        project(c + 1)
                    if lag2 is not None:
                        norm.pe_turn_x(pe, lag2, TB, 4 * lag2 + X_)
                    if lag is not None:
                        attn_t(lag)
                    features_of_q(c)
                    if lag is not None:
                        out_proj(lag)
                    if more:
                        to_tokens(c + 1)
                    if lag is not None:
                        norm.pe_turn_y(pe, lag, TB, 4 * lag + Y_)
                    keys_values(c)
                    if more:
                        to_features(c + 1)
                    outputs(c)

                def after():
                    norm.pe_turn_x(pe, NC - 2, TB, 4 * (NC - 2) + X_)
                    attn_t(NC - 1)
                    out_proj(NC - 1)
                    norm.pe_turn_y(pe, NC - 1, TB, 4 * (NC - 1) + Y_)
                    norm.pe_turn_x(pe, NC - 1, TB, 4 * (NC - 1) + X_)

                pe.wait_ge(w.lo_ready, 1)
                pe.wait_ge(ones_made, 1)
                chunks(pe, before, body, after, first=2)

            @block.scalar
            def _(act):
                def attn_upper(lag):
                    act.wait_ge(tb_full, 4 * lag + AT_ + 1)
                    act.activation(a_hi[:], TB[:], ACT.Copy).then_inc(attn_hi, 1)

                def y(lag):
                    act.wait_ge(tb_full, 4 * lag + WO_ + 1)
                    act.activation(net.y_stage[:], TB[:], ACT.Identity, bias=w.raw[:, BIAS + 3:BIAS + 4]).then_inc(tb_free, 1)

                def stage(c):
                    for i in range(3):
                        act.wait_ge(proj_full, 3 * c + i + 1)
                        act.activation(qkv_t[i][:], A[i][:], ACT.Identity,
                                       bias=w.raw[:, BIAS + i:BIAS + i + 1]).then_inc(staged, 1)

                def roots(c):
                    for i in range(2):
                        act.wait_ge(turned, 3 * c + i + 1)
                        wait(act, ss_ready, c)
                        act.activation(sq[i][:], A[i][:], ACT.Square).then_inc(sq_ready, 1)
                    act.wait_ge(ss_ready, c + 1)
                    act.activation(root[:], ss[:], ACT.Sqrt).then_inc(root_ready, 1)
                    act.wait_ge(turned, 3 * c + 3)
                    wait(act, kv_full, 2 * c)
                    act.activation(vals[:, :, 0:D], tile3(A[2][:]), ACT.Copy).then_inc(vals_ready, 1)

                def normed_upper(c):
                    for i in range(2):
                        act.wait_ge(back, 2 * c + i + 1)
                        act.activation(n_hi[i][:], A[i][:], ACT.Copy).then_inc(n_hi_ready, 1)

                def before():
                    stage(0)
                    roots(0)
                    normed_upper(0)

                def body(c, lag, more):
                    lag2 = two_before(c)
                    if more:
                        stage(c + 1)
                    if lag2 is not None:
                        norm.act_hi(act, lag2, TB, 4 * lag2 + X_)
                    if lag is not None:
                        attn_upper(lag)
                        y(lag)
                    if more:
                        roots(c + 1)
                        normed_upper(c + 1)

                def after():
                    norm.act_hi(act, NC - 2, TB, 4 * (NC - 2) + X_)
                    attn_upper(NC - 1)
                    y(NC - 1)
                    norm.act_hi(act, NC - 1, TB, 4 * (NC - 1) + X_)

                w.act_split(act)
                act.activation(net.spare[:, 0:1], net.ident[:, 0:1], ACT.Sqrt)
                chunks(act, before, body, after, first=2)

            @block.vector
            def _(dve):
                def attn_lower(lag):
                    dve.wait_ge(attn_hi, lag + 1)
                    dve.tensor_tensor(a_lo[:], TB[:], a_hi[:].bitcast(F32), ALU.subtract).then_inc(tb_free, 1)

                def norms(c):
                    for i in range(2):
                        dve.wait_ge(sq_ready, 2 * c + i + 1)
                        last = dve.tensor_reduce(ss[:, i * 64:(i + 1) * 64], sq[i][:].rearrange("p (n d) -> p n d", d=DH),
                                                 AX.X, ALU.add)
                    last.then_inc(ss_ready, 1)
                    dve.wait_ge(root_ready, c + 1)
                    dve.tensor_scalar(root_g[:], root[:], 1e-30, None, ALU.max).then_inc(n_stepped, 1)
                    dve.wait_ge(n_stepped, N_STEPS * c + 1)
                    dve.reciprocal(rinv[:], root_g[:]).then_inc(n_stepped, 1)
                    dve.wait_ge(n_stepped, N_STEPS * c + 2)
                    dve.tensor_tensor(nrm[:], ss[:], rinv[:], ALU.mult).then_inc(n_stepped, 1)
                    dve.wait_ge(n_stepped, N_STEPS * c + 3)
                    dve.tensor_tensor(nrm_e[:], nrm[:], root_g[:], ALU.add).then_inc(n_stepped, 1)
                    dve.wait_ge(n_stepped, N_STEPS * c + 4)
                    dve.tensor_scalar(nrm[:], nrm_e[:], 0.5, 1e-8, ALU.mult, ALU.add).then_inc(n_stepped, 1)
                    dve.wait_ge(n_stepped, N_STEPS * c + 5)
                    dve.reciprocal(rinv[:], nrm[:]).then_inc(n_stepped, 1)
                    dve.wait_ge(n_stepped, N_STEPS * c + 6)
                    for i in range(2):
                        r3 = rinv[:, i * 64:(i + 1) * 64].unsqueeze(2).broadcast_to([P, 64, DH])
                        dve.tensor_tensor(normed[i][:].rearrange("p (n d) -> p n d", d=DH),
                                          A[i][:].rearrange("p (n d) -> p n d", d=DH), r3, ALU.mult).then_inc(normed_ready, 1)

                def normed_lower(c):
                    for i in range(2):
                        dve.wait_ge(n_hi_ready, 2 * c + i + 1)
                        dve.tensor_tensor(n_lo[i][:], A[i][:], n_hi[i][:].bitcast(F32), ALU.subtract).then_inc(n_lo_ready, 1)

                def features_of_k(c):
                    for j in range(NB):
                        dve.wait_ge(kf_full, NB * c + j + 1)
                        dve.tensor_scalar(k_feat[:, j, :], F[j % 2][:], YAT, YAT, ALU.add, ALU.max).then_inc(kf_ready, 1)

                def features_of_q(c):
                    for g in range(GROUPS):
                        dve.wait_ge(qf_full, GROUPS * c + g + 1)
                        dve.tensor_scalar(q_feat[:, g, :], F[g % 2][:], YAT, YAT, ALU.add, ALU.max).then_inc(qf_ready, 1)

                def own_heads(c):
                    for i in range(2):
                        dve.wait_ge(kv_full, 2 * c + i + 1)
                        dve.tensor_tensor(kv[:, 2 * i:2 * i + 2, :], tile3(KV[i][:, 0:2 * VW], 2), own[:, 2 * i:2 * i + 2, :],
                                          ALU.mult).then_inc(kv_ready, 1)

                def outputs(c):
                    for i in range(2):
                        o3 = tile3(KV[i][:, 0:2 * VW], 2)
                        dsl, rsl = den[:, 2 * i:2 * i + 2, :], rden[:, 2 * i:2 * i + 2, :]
                        dve.wait_ge(o_full, 2 * c + i + 1)
                        dve.tensor_scalar(dsl, o3[:, :, D:VW], 1e-6, None, ALU.max).then_inc(o_stepped, 1)
                        dve.wait_ge(o_stepped, 4 * c + 2 * i + 1)
                        dve.reciprocal(rsl, dsl).then_inc(o_stepped, 1)
                        dve.wait_ge(o_stepped, 4 * c + 2 * i + 2)
                        a4 = attn[:, i * 2 * P:(i + 1) * 2 * P].rearrange("p (j h d) -> p j h d", j=2, d=DH)
                        dve.tensor_tensor(a4, o3[:, :, 0:D].rearrange("p j (h d) -> p j h d", d=DH),
                                          rsl.unsqueeze(3).broadcast_to([P, 2, HEADS, DH]), ALU.mult).then_inc(attn_ready, 1)

                def before():
                    norms(0)
                    normed_lower(0)

                def body(c, lag, more):
                    lag2 = two_before(c)
                    features_of_k(c)
                    if lag2 is not None:
                        norm.dve_scale(dve, lag2)
                        norm.dve_lo(dve, lag2, TB, 4 * lag2 + X_)
                    if lag is not None:
                        attn_lower(lag)
                    features_of_q(c)
                    if more:
                        norms(c + 1)
                    own_heads(c)
                    if lag is not None:
                        norm.dve_norm(dve, lag, TB, 4 * lag + Y_)
                    if more:
                        normed_lower(c + 1)
                    outputs(c)

                def after():
                    norm.dve_scale(dve, NC - 2)
                    norm.dve_lo(dve, NC - 2, TB, 4 * (NC - 2) + X_)
                    attn_lower(NC - 1)
                    norm.dve_norm(dve, NC - 1, TB, 4 * (NC - 1) + Y_)
                    norm.dve_scale(dve, NC - 1)
                    norm.dve_lo(dve, NC - 1, TB, 4 * (NC - 1) + X_)

                w.dve_split(dve)
                dve.wait_ge(own_loaded, 16)
                chunks(dve, before, body, after, first=2)


def experts_ffn(nc, net, name, hid, gelu, by_probs, shared, last=False):
    dram = net.dram[name]
    KT = hid // P
    NE = E + shared
    ROUND = 4
    CB = 2 if KT == ROUND else ROUND
    UNITS = CB * KT
    TURNS = NC // CB
    BEHIND = 3 if KT == ROUND else 2
    Y_LAG, S_LAG, X_LAG, ROOT_LAG = (2, 2, 3, 0) if KT == ROUND else (3, 4, 4, 1)
    EW = 2 * KT * P
    B1, B2 = EW, EW + KT
    G_BIAS = P
    CAP = int(1.25 * NC * CH / E)
    NT = NC * NB
    HALVES = NT * E // P
    with Layer(nc) as ctx:
        sb = lambda n, s, dt=F32: ctx.enter_context(nc.sbuf_tensor(f"{name}_{n}", s, dt))
        ps = lambda n: ctx.enter_context(nc.psum_tensor(f"{name}_{n}", [P, CH], F32))
        sem = lambda n: ctx.sem(f"{name}_{n}")
        norm = Norm(nc, ctx, net, name, last=last)
        gate = Weights(nc, ctx, net, name, P)
        weight_rows = nc.dram_tensor(f"{name}_weight_rows", [NE, NC, NB, P], F32, kind="Internal").ap()
        acc = sb("acc", [P, NC * CH])
        e_raw = [sb(f"e_raw{i}", [P, B2 + 1]) for i in range(2)]
        e_bias = [sb(f"e_bias{i}", [P, KT + 1]) for i in range(2)]
        e_hi = [sb(f"e_hi{i}", [P, EW], F32R) for i in range(2)]
        e_lo = [sb(f"e_lo{i}", [P, EW], F32R) for i in range(2)]
        wt = [sb(f"wt{i}", [P, NC * CH]) for i in range(2)]
        h = [sb(f"h{i}", [P, CH]) for i in range(ROUND)]
        h_hi = [sb(f"h_hi{i}", [P, CH], F32R) for i in range(ROUND)]
        h_lo = [sb(f"h_lo{i}", [P, CH], F32R) for i in range(ROUND)]
        yw = [sb(f"yw{i}", [P, CH]) for i in range(2)]
        used = [0]

        def early(*shape):
            n = int(np.prod(shape))
            used[0] += n
            names = " ".join("abc"[:len(shape)])
            sizes = dict(zip("abc", shape))
            return wt[1][:, used[0] - n:used[0]].rearrange(f"p ({names}) -> p {names}", **sizes)

        lg_t = [early(CH) for i in range(2)]
        iota8 = sb("iota8", [P, E])
        lg = early(NT, E)
        top, idx = early(NT, 8), sb("idx", [P, NT, 8], U32)
        idxf, d2, e2 = sb("idxf", [P, NT, 2]), sb("d2", [P, NT]), sb("e2", [P, NT])
        d8, ex8 = early(NT, E), early(NT, E)
        s1, r1 = sb("s1", [P, NT]), sb("r1", [P, NT])
        w2 = sb("w2", [P, NT, 2])
        oh = [early(NT, E) for i in range(2)]
        pick = [early(NT, E) for i in range(2)]
        count8, keep = sb("count8", [P, E]), sb("keep", [P, E])
        ones = sb("ones", [P, P])
        comb, comb_kept = sb("comb", [P, E, NT]), sb("comb_kept", [P, E, NT])
        comb_t = sb("comb_t", [P, HALVES, P])
        one_row = sb("one_row", [NT, P])

        H = [ps(f"H{i}") for i in range(ROUND)]
        TY, TX = ps("TY"), ps("TX")
        Y = [ps("Y0"), ps("Y1")]

        made, iota_loaded = sem("made"), sem("iota_loaded")
        lg_full, lg_staged, lg_turned = sem("lg_full"), sem("lg_staged"), sem("lg_turned")
        lg_read, g_stepped, g_exp, comb_turned, comb_saved = (sem("lg_read"), sem("g_stepped"), sem("g_exp"),
                                                              sem("comb_turned"), sem("comb_saved"))
        idx_ready, k_full, rows_out = sem("idx_ready"), sem("k_full"), sem("rows_out")
        e_loaded, wt_loaded = [sem(f"e_loaded{i}") for i in range(2)], [sem(f"wt_loaded{i}") for i in range(2)]
        e_hi_ready, e_ready = sem("e_hi_ready"), sem("e_ready")
        h_full, h_hi_ready, h_lo_ready = sem("h_full"), sem("h_hi_ready"), sem("h_lo_ready")
        y_full, yw_ready, acc_ready = sem("y_full"), sem("yw_ready"), sem("acc_ready")

        STEPS, BEFORE_EXP, COUNTED = (NC + 13, NC + 1, NC + 11) if by_probs else (NC + 7, NC + 1, None)
        PAIRS = (NE - 1) // 2

        def turns(eng, turn, new=None):
            def expert(q, i, before):
                if new is not None:
                    new(q, i)
                turn((q, i), 0, before)
                first = 2 if final(q, i) else 1
                for b in range(1, first):
                    turn((q, i), b, (q, i, b - 1))
                if first < TURNS:
                    with eng.Fori(first, TURNS) as b:
                        turn((q, i), b, (q, i, b - 1))

            expert(0, 0, None)
            expert(0, 1, (0, 0, TURNS - 1))
            with eng.Fori(1, PAIRS) as q:
                expert(q, 0, (q - 1, 1, TURNS - 1))
                expert(q, 1, (q, 0, TURNS - 1))
            for e in range(2 * PAIRS, NE):
                expert(e // 2, e % 2, ((e - 1) // 2, (e - 1) % 2, TURNS - 1))

        def number(q, i, b=0, k=0):
            return (2 * q + i) * NC + b * CB + k

        def final(q, i):
            return isinstance(q, int) and 2 * q + i == NE - 1

        def some(c):
            return not isinstance(c, int) or 0 <= c < NC

        with nc.Block() as block:
            @block.sync
            def _(sp):
                sp.dma_start(iota8[:], dram["iota8"]).then_inc(iota_loaded, 16)
                def load(e, i):
                    sp.dma_start(e_raw[i][:], dram["w"][bass.ds(e, 1)].rearrange("a p n -> p (a n)")
                                 ).then_inc(e_loaded[i], 16)

                def load_row(e, i):
                    row = weight_rows[bass.ds(e, 1)].rearrange("a c j p -> a (c j p)")
                    sp.dma_start(wt[i][:], row.broadcast_to([P, NC * CH])).then_inc(wt_loaded[i], 16)

                def next_expert(e, i):
                    sp.wait_ge(e_ready, e - 1)
                    load(e, i)
                    sp.wait_ge(yw_ready, (e - 1) * NC)
                    load_row(e, i)

                load(0, 0)
                load(1, 1)
                sp.wait_ge(comb_saved, 1)
                rows = weight_rows[0:E].rearrange("e c j p -> (e c j) p")
                for half in range(HALVES):
                    sp.dma_start(rows[half * P:(half + 1) * P], comb_t[:, half, :]).then_inc(rows_out, 16)
                if shared:
                    sp.wait_ge(made, 2)
                    sp.dma_start(weight_rows[E].rearrange("c j p -> (c j) p"), one_row[:]).then_inc(rows_out, 16)
                sp.wait_ge(rows_out, 16 * (HALVES + shared))
                load_row(0, 0)
                load_row(1, 1)
                with sp.Fori(1, E // 2) as q:
                    for i in range(2):
                        next_expert(2 * q + i, i)
                if shared:
                    next_expert(E, 0)
                with sp.Fori(0, NC) as c:
                    norm.sp_save(sp, c)
                norm.sp_end(sp)

            @block.gpsimd
            def _(pool):
                pool.memset(ones[:], 1.0).then_inc(made, 1)
                pool.memset(one_row[:], 1.0).then_inc(made, 1)
                pool.memset(acc[:, 0:NC * CH // 2], 0.0).then_inc(made, 1)
                pool.memset(acc[:, NC * CH // 2:], 0.0).then_inc(made, 1)
                pool.wait_ge(made, 4)

                def split(e, i, turn):
                    pool.wait_ge(e_loaded[i], 16 * turn + 16)
                    wait(pool, yw_ready, (e - 1) * NC)
                    settle(pool, net)
                    pool.tensor_copy(e_hi[i][:], e_raw[i][:, 0:EW])
                    pool.tensor_copy(e_bias[i][:], e_raw[i][:, EW:B2 + 1]).then_inc(e_hi_ready, 1)
                    pool.wait_ge(e_hi_ready, e + 1)
                    pool.tensor_tensor(e_lo[i][:], e_raw[i][:, 0:EW], e_hi[i][:].bitcast(F32),
                                       ALU.subtract).then_inc(e_ready, 1)

                def gather(q, i, b, k):
                    c, n = b * CB + k, number(q, i, b, k)
                    pool.wait_ge(yw_ready, n + 1)
                    pool.tensor_tensor(acc[:, at(c)], acc[:, at(c)], yw[k % 2][:], ALU.add).then_inc(acc_ready, 1)

                def new(q, i):
                    if isinstance(q, int) and 2 * q + i == 0 or final(q, i):
                        return
                    if i == 0:
                        split(2 * q + 1, 1, q)
                    elif not isinstance(q, int) or 2 * q + 2 < NE:
                        split(2 * q + 2, 0, q + 1)

                def turn(expert, b, before):
                    for k in range(CB):
                        gather(*expert, b, k)
                        c = b * CB + k - ROOT_LAG
                        if final(*expert) and some(c):
                            norm.pool_root(pool, c)

                split(0, 0, 0)
                split(1, 1, 0)
                turns(pool, turn, new)
                for c in range(NC - ROOT_LAG, NC):
                    norm.pool_root(pool, c)

            @block.tensor
            def _(pe):
                def logits(c):
                    if c >= 2:
                        pe.wait_ge(lg_staged, c - 1)
                    product3(pe, H[c % 2][:], gate.hi[:], gate.lo[:], net.x_hi[:, at(c)], net.x_lo[:, at(c)]
                             ).then_inc(lg_full, 1)

                def turn_logits(c):
                    pe.wait_ge(lg_staged, c + 1)
                    if c >= 2:
                        pe.wait_ge(lg_read, c - 1)
                    for j in range(NB):
                        mm = pe.transpose(H[2 + c % 2][:, j * P:(j + 1) * P], lg_t[c % 2][:, j * P:(j + 1) * P], net.ident[:])
                    mm.then_inc(lg_turned, 1)

                def up(q, i, b, u):
                    c, sl = b * CB + u // KT, slice(u % KT * P, (u % KT + 1) * P)
                    product3(pe, H[u % ROUND][:], e_hi[i][:, sl], e_lo[i][:, sl],
                             net.x_hi[:, at(c)], net.x_lo[:, at(c)]).then_inc(h_full, 1)

                def down(q, i, b, u):
                    k, t, r = u // KT, u % KT, u % ROUND
                    n = number(q, i, b, k)
                    if t == 0:
                        wait(pe, yw_ready, n - 1)
                    pe.wait_ge(h_lo_ready, n * KT + t + 1)
                    sl = slice((KT + t) * P, (KT + t + 1) * P)
                    mm = product3(pe, Y[k % 2][:], e_hi[i][:, sl], e_lo[i][:, sl], h_hi[r][:], h_lo[r][:],
                                  start=t == 0, stop=t == KT - 1)
                    if t == KT - 1:
                        mm.then_inc(y_full, 1)

                def turn_both(c):
                    x = some(c - X_LAG) and not last
                    if x and X_LAG > S_LAG:
                        norm.pe_turn_x(pe, c - X_LAG, TX)
                    if some(c - Y_LAG):
                        norm.pe_turn_y(pe, c - Y_LAG, TY)
                    if x and X_LAG == S_LAG:
                        norm.pe_turn_x(pe, c - X_LAG, TX)

                def new(q, i):
                    pe.wait_ge(e_ready, 2 * q + i + 1)
                    settle(pe, net)

                def turn(expert, b, before):
                    for u in range(UNITS):
                        up(*expert, b, u)
                        if u >= BEHIND:
                            down(*expert, b, u - BEHIND)
                        elif before is not None:
                            down(*before, UNITS + u - BEHIND)
                        if final(*expert):
                            c, t = b * CB + u // KT, u % KT
                            if t == 0:
                                turn_both(c)

                pe.wait_ge(gate.lo_ready, 1)
                pe.wait_ge(made, 4)
                logits(0)
                for c in range(NC):
                    if c + 1 < NC:
                        logits(c + 1)
                    turn_logits(c)
                if by_probs:
                    pe.wait_ge(g_stepped, COUNTED)
                    pe.matmul(Y[1][:, 0:E], ones[:], count8[:], start=True, stop=True).then_inc(k_full, 1)
                pe.wait_ge(g_stepped, STEPS)
                w = (comb_kept if by_probs else comb)[:].rearrange("p e t -> p (e t)")
                for half in range(HALVES):
                    mm = pe.transpose(Y[0][:, half * P:(half + 1) * P], w[:, half * P:(half + 1) * P], net.ident[:])
                mm.then_inc(comb_turned, 1)
                pe.wait_ge(comb_saved, 1)
                turns(pe, turn, new)
                for u in range(UNITS - BEHIND, UNITS):
                    down((NE - 1) // 2, (NE - 1) % 2, TURNS - 1, u)
                for c in range(NC, NC + X_LAG):
                    turn_both(c)

            @block.scalar
            def _(act):
                func = ACT.Gelu if gelu else ACT.Relu

                def y(c):
                    act.wait_ge(acc_ready, (NE - 1) * NC + c + 1)
                    wait(act, norm.y_turned, c)
                    act.activation(net.y_stage[:], acc[:, at(c)], ACT.Copy).then_inc(norm.y_staged, 1)

                def new(q, i):
                    act.wait_ge(e_ready, 2 * q + i + 1)

                def turn(expert, b, before):
                    q, i = expert
                    for u in range(UNITS):
                        r, t, c = u % ROUND, u % KT, b * CB + u // KT
                        if final(*expert) and t == 0 and some(c - Y_LAG):
                            y(c - Y_LAG)
                        act.wait_ge(h_full, number(q, i, b) * KT + u + 1)
                        act.activation(h[r][:], H[r][:], func, bias=e_bias[i][:, t:t + 1])
                        act.activation(h_hi[r][:], H[r][:], func, bias=e_bias[i][:, t:t + 1]).then_inc(h_hi_ready, 1)
                        if final(*expert) and t == 0 and some(c - X_LAG) and not last:
                            norm.act_hi(act, c - X_LAG, TX)

                gate.act_split(act)
                act.activation(net.spare[:], gate.raw[:, 0:NB], ACT.Exp)
                for c in range(NC):
                    act.wait_ge(lg_full, c + 1)
                    if c >= 2:
                        act.wait_ge(lg_turned, c - 1)
                    act.activation(lg_t[c % 2], H[c % 2][:], ACT.Identity, bias=gate.raw[:, G_BIAS:G_BIAS + 1]
                                   ).then_inc(lg_staged, 1)
                act.wait_ge(g_stepped, BEFORE_EXP)
                if by_probs:
                    act.activation(ex8, d8, ACT.Exp).then_inc(g_exp, 1)
                else:
                    act.activation(e2[:], d2[:], ACT.Exp).then_inc(g_exp, 1)
                act.wait_ge(comb_turned, 1)
                act.activation(comb_t[:], Y[0][:, 0:HALVES * P].rearrange("p (a b) -> p a b", b=P), ACT.Copy
                               ).then_inc(comb_saved, 1)
                if gelu:
                    act.activation(net.spare[:, 0:1], gate.raw[:, 0:1], ACT.Gelu)
                turns(act, turn, new)
                for c in range(NC, NC + X_LAG):
                    if some(c - Y_LAG):
                        y(c - Y_LAG)
                    if not last:
                        norm.act_hi(act, c - X_LAG, TX)

            @block.vector
            def _(dve):
                def bc(ap):
                    return ap.unsqueeze(2).broadcast_to([P, NT, E])

                def gates():
                    k = [0]

                    def link(ins):
                        k[0] += 1
                        ins.then_inc(g_stepped, 1)
                        dve.wait_ge(g_stepped, k[0])

                    def best(a, b):
                        for j in range(a, b):
                            ins = dve.max(top[:, j, :], lg[:, j, :])
                        return ins

                    def which(a, b):
                        for j in range(a, b):
                            ins = dve.max_index(idx[:, j, :], top[:, j, :], lg[:, j, :])
                        return ins

                    for c in range(NC):
                        dve.wait_ge(lg_turned, c + 1)
                        dve.tensor_copy(lg[:, c * NB:(c + 1) * NB, :], tile3(H[2 + c % 2][:])[:, :, 0:E]).then_inc(lg_read, 1)
                        dve.wait_ge(lg_read, c + 1)
                        link(best(c * NB, (c + 1) * NB))
                        if not by_probs:
                            which(c * NB, (c + 1) * NB).then_inc(idx_ready, 1)
                    if by_probs:
                        link(dve.tensor_tensor(d8, lg, bc(top[:, :, 0]), ALU.subtract))
                        dve.wait_ge(g_exp, 1)
                        link(dve.tensor_reduce(s1[:], ex8, AX.X, ALU.add))
                        link(dve.reciprocal(r1[:], s1[:]))
                        link(dve.tensor_tensor(lg, ex8, bc(r1[:]), ALU.mult))
                        link(best(0, NT))
                        which(0, NT).then_inc(idx_ready, NC)
                    dve.wait_ge(idx_ready, NC)
                    dve.tensor_copy(idxf[:], idx[:, :, 0:2])
                    link(dve.tensor_tensor(d2[:], top[:, :, 1], top[:, :, 0], ALU.subtract))
                    for i in range(2):
                        ins = dve.tensor_tensor(oh[i], iota8[:].unsqueeze(1).broadcast_to([P, NT, E]),
                                                bc(idxf[:, :, i]), ALU.is_equal)
                    link(ins)
                    if by_probs:
                        w_first, w_second = top[:, :, 0], top[:, :, 1]
                    else:
                        dve.wait_ge(g_exp, 1)
                        link(dve.tensor_scalar(s1[:], e2[:], 1.0, None, ALU.add))
                        link(dve.reciprocal(w2[:, :, 0], s1[:]))
                        link(dve.tensor_tensor(w2[:, :, 1], e2[:], w2[:, :, 0], ALU.mult))
                        w_first, w_second = w2[:, :, 0], w2[:, :, 1]
                    dve.tensor_tensor(pick[0], oh[0], bc(w_first), ALU.mult)
                    link(dve.tensor_tensor(pick[1], oh[1], bc(w_second), ALU.mult))
                    link(dve.tensor_tensor(comb[:].rearrange("p e t -> p t e"), pick[0], pick[1], ALU.add))
                    if by_probs:
                        link(dve.tensor_tensor(d8, oh[0], oh[1], ALU.add))
                        link(dve.tensor_reduce(count8[:], d8.rearrange("p t e -> p e t"), AX.X, ALU.add))
                        dve.wait_ge(k_full, 1)
                        link(dve.tensor_scalar(keep[:], Y[1][:, 0:E], float(CAP), None, ALU.is_le))
                        link(dve.tensor_tensor(comb_kept[:], comb[:], keep[:].unsqueeze(2).broadcast_to([P, E, NT]),
                                               ALU.mult))
                    assert k[0] == STEPS and (not by_probs or COUNTED == k[0] - 2)

                def weigh_output(q, i, b, k):
                    n, c = number(q, i, b, k), b * CB + k
                    wait(dve, acc_ready, n - 1)
                    if k == 0 and isinstance(b, int) and b == 0:
                        dve.wait_ge(wt_loaded[i], 16 * q + 16)
                        settle(dve, net)
                    dve.wait_ge(y_full, n + 1)
                    dve.scalar_tensor_tensor(out=yw[k % 2][:], in0=Y[k % 2][:], scalar=e_bias[i][:, KT:KT + 1],
                                             in1=wt[i][:, at(c)], op0=ALU.add, op1=ALU.mult).then_inc(yw_ready, 1)

                def turn(expert, b, before):
                    q, i = expert
                    for u in range(UNITS):
                        r, t, c = u % ROUND, u % KT, b * CB + u // KT
                        if (u - BEHIND) % KT == KT - 1:
                            if u >= BEHIND:
                                weigh_output(q, i, b, (u - BEHIND) // KT)
                            elif before is not None:
                                weigh_output(*before, (UNITS + u - BEHIND) // KT)
                        dve.wait_ge(h_hi_ready, number(q, i, b) * KT + u + 1)
                        dve.tensor_tensor(h_lo[r][:], h[r][:], h_hi[r][:].bitcast(F32),
                                          ALU.subtract).then_inc(h_lo_ready, 1)
                        if final(*expert):
                            if KT == 1 and some(c - S_LAG):
                                norm.dve_scale(dve, c - S_LAG)
                            if t == 0 and some(c - Y_LAG):
                                norm.dve_norm(dve, c - Y_LAG, TY)
                            if KT > 1 and t == 1 and some(c - S_LAG):
                                norm.dve_scale(dve, c - S_LAG)
                            if t == KT - 1 and some(c - X_LAG) and not last:
                                norm.dve_lo(dve, c - X_LAG, TX)

                gate.dve_split(dve)
                dve.wait_ge(iota_loaded, 16)
                gates()
                turns(dve, turn)
                for k in range(CB - 1 - (BEHIND - 1) // KT, CB):
                    weigh_output((NE - 1) // 2, (NE - 1) % 2, TURNS - 1, k)
                for c in range(NC, NC + X_LAG):
                    if KT == 1 and some(c - S_LAG):
                        norm.dve_scale(dve, c - S_LAG)
                    if some(c - Y_LAG):
                        norm.dve_norm(dve, c - Y_LAG, TY)
                    if KT > 1 and some(c - S_LAG):
                        norm.dve_scale(dve, c - S_LAG)
                    if not last:
                        norm.dve_lo(dve, c - X_LAG, TX)


def steps(nc, net):
    return [
        lambda: softmax_attention(nc, net, "L0_attn", True),
        lambda: experts_ffn(nc, net, "L0_ffn", P, False, True, 0),
        lambda: gated_recurrence(nc, net),
        lambda: ternary_ffn(nc, net),
        lambda: softmax_attention(nc, net, "L2_attn", False),
        lambda: experts_ffn(nc, net, "L2_ffn", HID, False, False, 0),
        lambda: linear_attention(nc, net),
        lambda: experts_ffn(nc, net, "L3_ffn", HID, True, False, 1, last=True),
    ]


def program(nc, dram):
    with Layer(nc) as ctx:
        net = Net(nc, ctx, dram)
        enter(nc, net)
        for layer in steps(nc, net):
            layer()


def layout(inputs):
    a = {k: np.asarray(v) for k, v in inputs.items()}
    f = np.float32
    out = {"x": np.ascontiguousarray(a["L0_attn_x"])}

    def column(v):
        return v.reshape(-1, P).T

    def stacked(wt):
        s = np.zeros((wt.shape[0], GROUPS, GH, QUAD), f)
        v = wt.reshape(wt.shape[0], GROUPS, GH, DH)
        for i in range(3):
            s[:, :, :, i * DH:(i + 1) * DH] = v
        return s.reshape(wt.shape[0], GROUPS * P)

    def softmax_weights(pre, bias, scale):
        w = np.zeros((P, 2 * GROUPS * P + 2 * P + 11), f)
        w[:, 0:GROUPS * P] = stacked(a[pre + "Wq"].T)
        w[:, GROUPS * P:2 * GROUPS * P] = stacked(a[pre + "Wk"].T)
        w[:, 2 * GROUPS * P:2 * GROUPS * P + P] = a[pre + "Wv"].T
        w[:, 2 * GROUPS * P + P:2 * GROUPS * P + 2 * P] = a[pre + "Wo"].T
        b = 2 * GROUPS * P + 2 * P
        if bias:
            w[:, b:b + 4] = stacked(a[pre + "bq"][None, :]).reshape(GROUPS, P).T
            w[:, b + 4:b + 8] = stacked(a[pre + "bk"][None, :]).reshape(GROUPS, P).T
            w[:, b + 8] = a[pre + "bv"]
            w[:, b + 9] = a[pre + "bo"]
            w[:, b + 10] = a[pre + "attn_scale"][0]
        else:
            w[:, b + 10] = f(1.0) / np.sqrt(f(DH))
        for r in range(GH):
            w[QUAD * r + R_MAX:QUAD * r + K_MAX, b + 4:b + 8] = 1.0
        return w

    out["L0_attn_w"] = softmax_weights("L0_attn_", False, None)
    out["L2_attn_w"] = softmax_weights("L2_attn_", True, None)
    out["L1_attn_w"] = np.concatenate([a["L1_attn_W_in"], a["L1_attn_W_out"], column(a["L1_attn_b_in"]),
                                       column(a["L1_attn_b_out"])], axis=1)

    def tiles(wt):
        return wt.reshape(-1, P, wt.shape[1]).transpose(1, 0, 2).reshape(P, -1)

    out["L1_ffn_w"] = np.concatenate([a["L1_ffn_w1_w"].T, a["L1_ffn_w2_w"].T, tiles(a["L1_ffn_h1_w"].T),
                                      tiles(a["L1_ffn_h2_w"].T), tiles(a["L1_ffn_w3_w"].T)], axis=1)
    out["L1_ffn_scales"] = np.concatenate([column(a["L1_ffn_" + k]) for k in ("w1_s", "w2_s", "h1_s", "h2_s", "w3_s")], axis=1)
    block = np.zeros((HEADS, DH, HEADS, QUAD), f)
    for h in range(HEADS):
        block[h, :, h, :] = a["L3_attn_projection"][h].T
    out["L3_attn_w"] = np.concatenate([a["L3_attn_Wq"], a["L3_attn_Wk"], a["L3_attn_Wv"], a["L3_attn_Wo"],
                                       block.reshape(P, HEADS * QUAD)] +
                                      [column(a["L3_attn_" + k]) for k in ("bq", "bk", "bv", "bo")], axis=1)

    def gate(wt, b):
        g = np.zeros((P, P + 1), f)
        g[:, 0:E] = wt
        if b is not None:
            g[0:E, P] = b
        return g

    def experts(w1, b1, w2, b2):
        return np.concatenate([w1, np.stack([tiles(m) for m in w2]), b1.reshape(len(w1), -1, P).transpose(0, 2, 1),
                               b2.reshape(len(w1), P, 1)], axis=2)

    out["L0_ffn_gate"] = gate(a["L0_ffn_gate_w"].T, None)
    out["L0_ffn_w"] = experts(*[a["L0_ffn_" + k] for k in ("W1", "b1", "W2", "b2")])
    out["L2_ffn_gate"] = gate(a["L2_ffn_W_router"], a["L2_ffn_b_router"])
    out["L2_ffn_w"] = experts(*[a["L2_ffn_" + k] for k in ("W1", "b1", "W2", "b2")])
    out["L3_ffn_gate"] = gate(a["L3_ffn_gate_w"], a["L3_ffn_gate_b"])
    out["L3_ffn_w"] = np.concatenate(
        [experts(*[a["L3_ffn_" + k] for k in ("w1", "b1", "w2", "b2")]),
         experts(a["L3_ffn_ws1"][None], a["L3_ffn_bs1"][None], a["L3_ffn_ws2"][None], a["L3_ffn_bs2"][None])], axis=0)

    bf16 = mybir.dt.np(BF16)
    q, k = np.arange(P)[:, None], np.arange(P)[None, :]
    window = [np.where(ok, 0.0, NEG) for ok in (k <= q, k > q)]
    half = P // 2
    chunked = [np.where(((k // half == q // half) & (k <= q)) | (k // half > q // half), 0.0, NEG)] * 2
    for name, m in (("L0_attn_masks", window), ("L2_attn_masks", chunked)):
        out[name] = np.stack([m[0], m[1], m[0].T, m[1].T], axis=1).astype(bf16)
    out["ident"] = np.eye(P, dtype=f)
    out["ident16"] = np.eye(P).astype(bf16)
    c = np.zeros((P, 4), f)
    row = np.arange(P) % QUAD
    c[:, 0] = np.where((row >= DH) & (row < 2 * DH), -1.0, 0.0)
    c[:, 1] = np.where((row >= 2 * DH) & (row < 3 * DH), -1.0, 0.0)
    out["const"] = c
    iota = np.broadcast_to(np.arange(E, dtype=f), (P, E)).copy()
    for name in ("L0_ffn_iota8", "L2_ffn_iota8", "L3_ffn_iota8"):
        out[name] = iota
    own = np.zeros((P, GROUPS, D + HEADS), f)
    for g in range(GROUPS):
        for p in range(P):
            h = GH * g + p // QUAD
            own[p, g, h * DH:(h + 1) * DH] = 1.0
            own[p, g, D + h] = 1.0
    out["L3_attn_own"] = own
    return {n: np.ascontiguousarray(v) for n, v in out.items()}


def build(nc, inputs):
    arrays, dram = {}, {}
    for name, v in layout(inputs).items():
        arrays[f"in_{name}"] = v
        ap = nc.dram_tensor(f"in_{name}", v.shape, mybir.dt.from_np(v.dtype), kind="ExternalInput").ap()
        if name[0] == "L":
            layer, part = name[:name.rindex("_")], name[name.rindex("_") + 1:]
            dram.setdefault(layer, {})[part] = ap
        else:
            dram[name] = ap
    dram["out"] = nc.dram_tensor("out_x", (BATCH, SEQ, D), F32, kind="ExternalOutput").ap()
    program(nc, dram)
    return arrays


def kernel(**inputs):
    import concourse.bacc as bacc
    from concourse.bass_utils import run_bass_kernel_spmd
    nc = bacc.Bacc("TRN2", target_bir_lowering=False, num_devices=1)
    arrays = build(nc, inputs)
    r = run_bass_kernel_spmd(nc, [arrays], core_ids=[0])
    return r.results[0]["out_x"]
```
